# Optimizing a Trainium2 kernel written in Bass

```python
import numpy as np
import jax
import jax.numpy as jnp

def _softmax(x, axis=-1):
    return jax.nn.softmax(x, axis=axis)

def _gelu(x):
    return jax.nn.gelu(x, approximate=True)

def _silu(x):
    return jax.nn.silu(x)

def _sigmoid(x):
    return jax.nn.sigmoid(x)

def _layernorm(x, axis=-1, eps=1e-05):
    m = jnp.mean(x, axis=axis, keepdims=True)
    v = jnp.var(x, axis=axis, keepdims=True)
    return (x - m) / jnp.sqrt(v + eps)

def _scatter_add(tgt, idx, src, axis=0):
    return tgt.at[idx].add(src)

def _segment_sum(src, seg, n):
    return jax.ops.segment_sum(src, seg, n)
kernel_name = 'mk_flamingo_gated_d1_seqx_r8_338a50'

def setup_inputs(seed: int=0):
    np.random.seed(seed)
    _w = jnp.asarray

    def _rec_inputs():
        import jax
        import jax.numpy as jnp
        _rk = jax.random.key(seed)
        x = 7.22e-05 + 1 * jax.random.normal(jax.random.fold_in(_rk, 1), (128, 64, 128), jnp.float32)
        _lenS = 64 - jax.random.randint(jax.random.fold_in(_rk, 7), (128,), 0, max(1, 64 // 4) + 1, jnp.int32)
        _lenS2 = 64 - jax.random.randint(jax.random.fold_in(_rk, 8), (128,), 0, max(1, 64 // 4) + 1, jnp.int32)
        _ctx_1024P = jax.random.normal(jax.random.fold_in(_rk, 11), (128, 16, 128), jnp.float32)
        _ctx_1024c = jax.random.dirichlet(jax.random.fold_in(_rk, 511), 0.3 * jnp.ones((16,), jnp.float32), (128, 64))
        _ctx_1024t = jnp.einsum('bsk,bkd->bsd', _ctx_1024c, _ctx_1024P)
        _ctx_1024t = _ctx_1024t * jax.lax.rsqrt(jnp.mean(jnp.square(_ctx_1024t)) + 1e-12) * 0.953939
        ctx_1024 = 4.13588e-05 + 0.999923 * (_ctx_1024t + 0.3 * jax.random.normal(jax.random.fold_in(_rk, 611), (128, 64, 128), jnp.float32))
        _validS = jnp.arange(64)[None, :] < _lenS[:, None]
        _validS2 = jnp.arange(64)[None, :] < _lenS2[:, None]
        _causal = jnp.tril(jnp.ones((64, 64), dtype=bool))
        mask_1x1xSxS2_ff0 = jnp.where(jnp.ones((1, 1, 64, 64), dtype=bool), 0.0, -1000000000.0).astype(jnp.float32)
        mask_BxS2_ik0 = jnp.where(jnp.broadcast_to(_validS2[:, :], (128, 64)), 0, 1).astype(jnp.int32)
        _g = jax.random.normal(jax.random.fold_in(_rk, 9001), (2, 1), jnp.float32)
        _g = jnp.sign(_g) * jnp.maximum(jnp.abs(_g), 1.0) + (_g == 0) * 1.0
        g_xattn = _g[0]
        g_ffn = _g[1]
        return (x, ctx_1024, mask_1x1xSxS2_ff0, mask_BxS2_ik0, g_xattn, g_ffn)
    x, ctx_1024, mask_1x1xSxS2_ff0, mask_BxS2_ik0, g_xattn, g_ffn = _rec_inputs()

    def _L0_xattn_setup():
        import jax, jax.numpy as jnp
        import numpy as np
        H = 16
        D_MODEL = 128
        D_K = D_MODEL // H
        B, S = (4, 256)

        def _split_heads(x):
            b, s, _ = x.shape
            return x.reshape(b, s, H, D_K).transpose(0, 2, 1, 3)
        key = jax.random.key(seed)
        ks = jax.random.split(key, 12)
        scale = 1.0 / np.sqrt(D_MODEL)
        inp = {'query': jax.random.normal(ks[0], (B, S, D_MODEL), jnp.float32), 'key_in': jax.random.normal(ks[1], (B, S, D_MODEL), jnp.float32), 'value': jax.random.normal(ks[2], (B, S, D_MODEL), jnp.float32), 'src_mask': jnp.zeros((1, 1, S, S), jnp.float32), 'pad_mask': jax.random.randint(ks[3], (B, S), 0, 2, jnp.int32), 'Wq': jax.random.normal(ks[4], (D_MODEL, D_MODEL), jnp.float32) * scale, 'bq': jnp.zeros((D_MODEL,), jnp.float32), 'Wk': jax.random.normal(ks[5], (D_MODEL, D_MODEL), jnp.float32) * scale, 'bk': jnp.zeros((D_MODEL,), jnp.float32), 'Wv': jax.random.normal(ks[6], (D_MODEL, D_MODEL), jnp.float32) * scale, 'bv': jnp.zeros((D_MODEL,), jnp.float32), 'Wo': jax.random.normal(ks[7], (D_MODEL, D_MODEL), jnp.float32) * scale, 'bo': jnp.zeros((D_MODEL,), jnp.float32)}
        return inp
    _L0_xattn_all = _L0_xattn_setup()
    _L0_xattn_in = {k: v for k, v in _L0_xattn_all.items() if k in ('Wq', 'bq', 'Wk', 'bk', 'Wv', 'bv', 'Wo', 'bo')}
    del _L0_xattn_all

    def _L0_ffn_setup():
        import jax, jax.numpy as jnp
        import numpy as np
        E = 8
        K = 2
        LN_EPS = 1e-05

        def _expert_ffn(x, w1, b1, gate, w2, b2):
            h = jax.nn.gelu((x @ w1 + b1) * gate, approximate=False)
            return h @ w2 + b2
        key = jax.random.key(seed)
        B, S, D, F = (4, 256, 128, 512)
        F2 = F // 2
        ks = jax.random.split(key, 8)
        s = 0.02
        return {'hidden_states': jax.random.normal(ks[0], (B, S, D), jnp.float32), 'router_w': jax.random.normal(ks[1], (D, E), jnp.float32) * s, 'router_b': jnp.zeros((E,), jnp.float32), 'w1': jax.random.normal(ks[2], (E, D, F), jnp.float32) * s, 'b1': jnp.zeros((E, F), jnp.float32), 'gate': jnp.ones((E, F), jnp.float32), 'w2': jax.random.normal(ks[3], (E, F, D), jnp.float32) * s, 'b2': jnp.zeros((E, D), jnp.float32), 'sw1': jax.random.normal(ks[4], (D, F2), jnp.float32) * s, 'sb1': jnp.zeros((F2,), jnp.float32), 'sgate': jnp.ones((F2,), jnp.float32), 'sw2': jax.random.normal(ks[5], (F2, D), jnp.float32) * s, 'sb2': jnp.zeros((D,), jnp.float32), 'shared_weight': jnp.float32(0.5), 'ln_g': jnp.ones((D,), jnp.float32), 'ln_b': jnp.zeros((D,), jnp.float32)}
    _L0_ffn_all = _L0_ffn_setup()
    _L0_ffn_in = {k: v for k, v in _L0_ffn_all.items() if k in ('router_w', 'router_b', 'w1', 'b1', 'gate', 'w2', 'b2', 'sw1', 'sb1', 'sgate', 'sw2', 'sb2', 'shared_weight', 'ln_g', 'ln_b')}
    del _L0_ffn_all
    return {'x': x, 'ctx_1024': ctx_1024, 'mask_1x1xSxS2_ff0': mask_1x1xSxS2_ff0, 'mask_BxS2_ik0': mask_BxS2_ik0, 'g_xattn': g_xattn, 'g_ffn': g_ffn, 'L0_xattn_Wq': _L0_xattn_in['Wq'], 'L0_xattn_bq': _L0_xattn_in['bq'], 'L0_xattn_Wk': _L0_xattn_in['Wk'], 'L0_xattn_bk': _L0_xattn_in['bk'], 'L0_xattn_Wv': _L0_xattn_in['Wv'], 'L0_xattn_bv': _L0_xattn_in['bv'], 'L0_xattn_Wo': _L0_xattn_in['Wo'], 'L0_xattn_bo': _L0_xattn_in['bo'], 'L0_ffn_router_w': _L0_ffn_in['router_w'], 'L0_ffn_router_b': _L0_ffn_in['router_b'], 'L0_ffn_w1': _L0_ffn_in['w1'], 'L0_ffn_b1': _L0_ffn_in['b1'], 'L0_ffn_gate': _L0_ffn_in['gate'], 'L0_ffn_w2': _L0_ffn_in['w2'], 'L0_ffn_b2': _L0_ffn_in['b2'], 'L0_ffn_sw1': _L0_ffn_in['sw1'], 'L0_ffn_sb1': _L0_ffn_in['sb1'], 'L0_ffn_sgate': _L0_ffn_in['sgate'], 'L0_ffn_sw2': _L0_ffn_in['sw2'], 'L0_ffn_sb2': _L0_ffn_in['sb2'], 'L0_ffn_shared_weight': _L0_ffn_in['shared_weight'], 'L0_ffn_ln_g': _L0_ffn_in['ln_g'], 'L0_ffn_ln_b': _L0_ffn_in['ln_b']}

def reference(x, ctx_1024, mask_1x1xSxS2_ff0, mask_BxS2_ik0, g_xattn, g_ffn, L0_xattn_Wq, L0_xattn_bq, L0_xattn_Wk, L0_xattn_bk, L0_xattn_Wv, L0_xattn_bv, L0_xattn_Wo, L0_xattn_bo, L0_ffn_router_w, L0_ffn_router_b, L0_ffn_w1, L0_ffn_b1, L0_ffn_gate, L0_ffn_w2, L0_ffn_b2, L0_ffn_sw1, L0_ffn_sb1, L0_ffn_sgate, L0_ffn_sw2, L0_ffn_sb2, L0_ffn_shared_weight, L0_ffn_ln_g, L0_ffn_ln_b):
    import jax
    import jax.numpy as jnp

    def _L0_xattn_ref(query, key_in, value, src_mask, pad_mask, Wq, bq, Wk, bk, Wv, bv, Wo, bo):
        import jax, jax.numpy as jnp
        import numpy as np
        H = 16
        D_MODEL = 128
        D_K = D_MODEL // H
        B, S = (4, 256)

        def _split_heads(x):
            b, s, _ = x.shape
            return x.reshape(b, s, H, D_K).transpose(0, 2, 1, 3)
        q = _split_heads(query @ Wq.T + bq)
        k = _split_heads(key_in @ Wk.T + bk)
        v = _split_heads(value @ Wv.T + bv)
        scores = jnp.einsum('bhqd,bhkd->bhqk', q, k) / jnp.sqrt(jnp.float32(D_K))
        pm = pad_mask[:, None, None, :]
        scores = jnp.where(pm == 0, jnp.float32(-1000000000.0), scores)
        scores = scores + src_mask
        p_attn = jax.nn.softmax(scores, axis=-1)
        x = jnp.einsum('bhqk,bhkd->bhqd', p_attn, v)
        x = x.transpose(0, 2, 1, 3).reshape(query.shape[0], -1, H * D_K)
        return x @ Wo.T + bo

    def _L0_ffn_ref(hidden_states, router_w, router_b, w1, b1, gate, w2, b2, sw1, sb1, sgate, sw2, sb2, shared_weight, ln_g, ln_b):
        import jax, jax.numpy as jnp
        import numpy as np
        E = 8
        K = 2
        LN_EPS = 1e-05

        def _expert_ffn(x, w1, b1, gate, w2, b2):
            h = jax.nn.gelu((x @ w1 + b1) * gate, approximate=False)
            return h @ w2 + b2
        x = hidden_states
        logits = jnp.einsum('bsd,de->bse', x, router_w) + router_b
        probs = jax.nn.softmax(logits, axis=-1)
        topk_p, topk_i = jax.lax.top_k(probs, K)
        topk_p = topk_p / jnp.sum(topk_p, axis=-1, keepdims=True)
        combine = jnp.sum(jax.nn.one_hot(topk_i, E, dtype=x.dtype) * topk_p[..., None], axis=-2)
        moe = jnp.zeros_like(x)
        for e in range(E):
            moe = moe + combine[..., e:e + 1] * _expert_ffn(x, w1[e], b1[e], gate[e], w2[e], b2[e])
        shared = _expert_ffn(x, sw1, sb1, sgate, sw2, sb2) * jax.nn.sigmoid(shared_weight)
        y = moe + shared
        mu = jnp.mean(y, axis=-1, keepdims=True)
        var = jnp.var(y, axis=-1, keepdims=True)
        return (y - mu) * jax.lax.rsqrt(var + LN_EPS) * ln_g + ln_b
    x = x + jnp.tanh(g_xattn[0]) * _L0_xattn_ref(_layernorm(x, axis=-1), ctx_1024, ctx_1024, mask_1x1xSxS2_ff0, mask_BxS2_ik0, L0_xattn_Wq, L0_xattn_bq, L0_xattn_Wk, L0_xattn_bk, L0_xattn_Wv, L0_xattn_bv, L0_xattn_Wo, L0_xattn_bo)
    x = x + jnp.tanh(g_ffn[0]) * _L0_ffn_ref(_layernorm(x, axis=-1), L0_ffn_router_w, L0_ffn_router_b, L0_ffn_w1, L0_ffn_b1, L0_ffn_gate, L0_ffn_w2, L0_ffn_b2, L0_ffn_sw1, L0_ffn_sb1, L0_ffn_sgate, L0_ffn_sw2, L0_ffn_sb2, L0_ffn_shared_weight, L0_ffn_ln_g, L0_ffn_ln_b)
    return x

_drawn_inputs = setup_inputs


def setup_inputs(seed=0):
    import zlib

    import numpy as np

    out = dict(_drawn_inputs(seed))
    spreads = {'L0_xattn_bq': (0.0, 0.1),
     'L0_xattn_bk': (0.0, 0.1),
     'L0_xattn_bv': (0.0, 0.1),
     'L0_xattn_bo': (0.0, 0.1),
     'L0_ffn_router_b': (0.0, 0.1),
     'L0_ffn_b1': (0.0, 0.1),
     'L0_ffn_gate': (1.0, 0.2),
     'L0_ffn_b2': (0.0, 0.1),
     'L0_ffn_sb1': (0.0, 0.1),
     'L0_ffn_sgate': (1.0, 0.2),
     'L0_ffn_sb2': (0.0, 0.1),
     'L0_ffn_ln_g': (1.0, 0.2),
     'L0_ffn_ln_b': (0.0, 0.1)}
    factors = {}
    for name, (base, spread) in spreads.items():
        noise = np.random.default_rng([zlib.crc32(name.encode()), seed]).standard_normal(out[name].shape)
        drawn = base * np.exp(spread * noise) if base else spread * noise
        out[name] = jnp.asarray(drawn.astype(out[name].dtype))
    for name, factor in factors.items():
        out[name] = (out[name] * factor).astype(out[name].dtype)
    return out
```

```python
from contextlib import ExitStack

import numpy as np
import concourse.bass as bass
from concourse import mybir
from concourse.alu_op_type import AluOpType as ALU

ACT = mybir.ActivationFunctionType
F32 = mybir.dt.float32
BF16 = mybir.dt.bfloat16
I32 = mybir.dt.int32
X = mybir.AxisListType.X

P = 128
D = 128
H = 16
DK = D // H
HG = 32 // DK
NG = H // HG
S = 64
E = 8
F = 512
FS = 256
QT = 4
QW = QT * D
VS = 48
ROW = D + 2
SL = 256
NEG = -1.0e9
EPS = 1e-5
RSQRT_MAGIC = float(0x5F3759DF)
LN_STEPS = 14
RA_STEPS = 12
RB_STEPS = 5

C_ID = 0
C_TRI = C_ID + P
C_JM = C_TRI + P
C_REV = C_JM + HG
C_BASE = C_REV + QT * E
C_PART = C_BASE + E
C_EXP = C_PART + 1
C_STEP = C_EXP + E


def steps_listed(NT):
    return 2 * NT * P // SL + E + 2


def constants(NT):
    c = np.zeros((P, C_STEP + steps_listed(NT)), np.float32)
    p = np.arange(P)
    c[:, C_ID:C_ID + P] = np.eye(P)
    c[:, C_TRI:C_TRI + P] = p[:, None] < p[None, :]
    c[:, C_JM:C_JM + HG] = (p[:, None] % 32) // DK == np.arange(HG)[None, :]
    c[:, C_REV:C_REV + QT * E] = np.tile(E - np.arange(E), QT)
    c[:, C_BASE:C_BASE + E] = np.arange(E) * (NT * P + SL)
    c[:, C_PART] = p
    c[:, C_EXP:C_EXP + E] = np.arange(E)
    c[:, C_STEP:] = np.arange(steps_listed(NT))
    return c


def bass_kernel(nc, a, out):
    NT = a["x"].shape[0] // 2
    TOK = NT * P
    REGION = TOK + SL
    assert NT % (2 * QT) == 0


    lists = nc.dram_tensor("expert_lists", [E * REGION + 3 * SL, ROW], F32).ap()
    results = nc.dram_tensor("expert_results", [2 * TOK + (E + 1) * SL, D], F32).ap()

    with ExitStack() as whole:
        m = shared_memory(nc, whole, NT)
        attention(nc, a, NT, lists, m)
        experts(nc, a, NT, REGION, lists, results, m)
        combine(nc, a, NT, results, out, m)


def wait_alone(eng, s, value, passed):
    eng.wait_ge(s, value)
    eng.sem_inc(passed, 1)


def tools(nc, ctx):
    def sb(name, shape, dt=F32):
        return ctx.enter_context(nc.sbuf_tensor(name, shape, dt))

    def sem(name):
        return ctx.enter_context(nc.semaphore(name))
    return sb, sem


class Shared:
    pass


def shared_memory(nc, ctx, NT):
    sb, sem = tools(nc, ctx)
    m = Shared()
    m.x_all = sb("x_all", [P, NT * D])
    m.xn2T = sb("xn2T", [P, NT * D])
    m.weight = sb("weight", [P, NT, 2])
    m.cst = sb("cst", [P, C_STEP + steps_listed(NT)])
    m.gates = sb("gates", [P, 4])
    m.count = sb("count", [P, E])
    m.xn2 = sb("xn2", [P, 2, QT, ROW])
    m.slots = sb("slots", [P, 2, QT, 2], I32)
    m.scattered = [sem(f"scattered{i}") for i in range(2)]
    m.sw1 = sb("sw1", [P, FS])
    m.sw2 = sb("sw2", [P, FS // P, D])
    m.scols = sb("scols", [P, 3, FS // P])
    m.sb2_row = sb("sb2_row", [P, D])
    m.shared_in = sem("shared_in")
    m.banks = [ctx.enter_context(nc.psum_tensor(f"bank{i}", [P, 512], F32)) for i in range(8)]
    return m


def scatter_rows(po, lists, m, par, which):
    for i in which:
        t, k = i // 2, i % 2
        po.indirect_dma_start(lists[:, :], bass.IndirectOffsetOnAxis(ap=m.slots[:, par, t, k:k + 1], axis=0),
                              m.xn2[:, par, t, :], None).then_inc(m.scattered[par], 16)


def attention(nc, a, NT, lists, m):
    NQ = NT // QT
    x_all, xn2T, weight, cst, gates, count = m.x_all, m.xn2T, m.weight, m.cst, m.gates, m.count
    xn2, slots, scattered, banks = m.xn2, m.slots, m.scattered, m.banks
    x_rows = a["x"].rearrange("b s d -> (b s) d")
    c_rows = a["ctx_1024"].rearrange("b s d -> (b s) d")
    pad_mask = a["mask_BxS2_ik0"]
    with ExitStack() as ctx:
        sb, sem = tools(nc, ctx)

        ident = cst[:, C_ID:C_ID + P]
        rev = cst[:, C_REV:C_REV + QT * E].rearrange("p (t e) -> p t e", t=QT)
        tri_bf = sb("tri_bf", [P, P], BF16)
        ones_bf = sb("ones_bf", [P, P], BF16)
        wq = sb("wq", [P, D])
        wk = sb("wk", [P, D])
        wv = sb("wv", [P, D])
        wo = sb("wo", [P, D])
        cols = sb("cols", [P, 8])
        bo_row = sb("bo_row", [P, D])
        bo_tmp = sb("bo_tmp", [P, D])
        bv_mat = sb("bv_mat", [P, P])
        rw = sb("rw", [P, 32])
        rb = sb("rb", [P, 1])
        srcm = sb("srcm", [P, S])
        ctx_in = sb("ctx_in", [P, 2, QW])
        pad_q = sb("pad_q", [P, 2, QT, S], I32)
        pad_k = sb("pad_k", [P, 2, QW], I32)
        keep = sb("keep", [P, QW])
        mask = sb("mask", [P, 2, QT, S])
        xn = sb("xn", [P, QW])
        xT = sb("xT", [P, QW])
        cT = sb("cT", [P, QW])
        kT = sb("kT", [P, QW])
        qg = sb("qg", [P, 2, NG, QW])
        kbd = sb("kbd", [P, 2, QT * 2, HG, S])
        vb = sb("vb", [P, 2, QT, 2, 8 * VS])
        prob = sb("prob", [P, QT, H * S])
        PT = sb("PT", [P, 2, 8 * P])
        mx = sb("mx", [P, QT, H])
        sm = sb("sm", [P, QT, H])
        rsx = sb("rsx", [P, QT, D])
        rsT = sb("rsT", [P, 2, P])
        aT = sb("aT", [P, 2, P])
        st1 = sb("st1", [P, QT, 6])
        st2 = sb("st2", [P, QT, 6])
        mv = sb("mv", [P, 2 * QT, 2])
        ln_v = sb("ln_v", [P, 2 * QT])
        ln_i = sb("ln_i", [P, 2 * QT], I32)
        ln_a = sb("ln_a", [P, 2 * QT])
        ln_b = sb("ln_b", [P, 2 * QT])
        ln_r = sb("ln_r", [P, 2 * QT])
        ln_s = sb("ln_s", [P, 2 * QT])
        x2T = sb("x2T", [P, 2, QW])
        LT = sb("LT", [P, P])
        lg = sb("lg", [P, QT, E])
        ra = sb("ra", [P, 4, QT, E])
        r_m = sb("r_m", [P, 6, QT])
        oh = sb("oh", [P, 2, QT, E])
        oh_bf = sb("oh_bf", [P, QT, E], BF16)
        posn = sb("posn", [P, QT, E])
        rt = sb("rt", [P, 2, QT, E])
        slotf = sb("slotf", [P, QT, 2])
        tokf = sb("tokf", [P, NT])

        sc_ps, pt_ps = banks[0:2], banks[2:4]
        fa_ps, fb_ps, att_ps, out_ps = banks[4:8]

        const_in = sem("const_in")
        setup_pool = sem("setup_pool")
        setup_act = sem("setup_act")
        setup_pe = sem("setup_pe")
        setup_dve = sem("setup_dve")
        quad_in = [sem(f"quad_in{i}") for i in range(2)]
        stats1 = sem("stats1")
        stats2 = sem("stats2")
        ln_step = sem("ln_step")
        xn_ready = sem("xn_ready")
        xT_done, xT_ready = sem("xT_done"), sem("xT_ready")
        cT_done, cT_ready = sem("cT_done"), sem("cT_ready")
        q_done, q_ready = sem("q_done"), sem("q_ready")
        k_done, kT_ready, k_ready = sem("k_done"), sem("kT_ready"), sem("k_ready")
        v_done, v_ready = sem("v_done"), sem("v_ready")
        keep_tmp = sem("keep_tmp")
        keep_ready, mask_tmp, mask_ready, xb_ready = sem("keep_ready"), sem("mask_tmp"), sem("mask_ready"), sem("xb_ready")
        scores_done, masked, maxed, subbed, exped = (sem(n) for n in ("scores_done", "masked", "maxed", "subbed", "exped"))
        summed, recips, rs_ready = sem("summed"), sem("recips"), sem("rs_ready")
        turned, PT_ready, att_done, rsT_ready, aT_ready = (sem(n) for n in ("turned", "PT_ready", "att_done", "rsT_ready", "aT_ready"))
        wo_done, x2_ready = sem("wo_done"), sem("x2_ready")
        xn2_ready, x2T_done, x2T_ready = sem("xn2_ready"), sem("x2T_done"), sem("x2T_ready")
        lg_done, LT_ready, lgT_done, lg_copied = (sem(n) for n in ("lg_done", "LT_ready", "lgT_done", "lg_copied"))
        ra_step, p2_ready, pref_done, pref_copied, rb_step = (sem(n) for n in ("ra_step", "p2_ready", "pref_done", "pref_copied", "rb_step"))
        x2T_kept = [sem(f"x2T_kept{i}") for i in range(2)]
        passed = sem("a_passed")

        def need(eng, s, item, per=1, k=None, total=NT, apart=False):
            k = per if k is None else k
            if isinstance(item, int):
                if item < 0:
                    return
                if item >= total:
                    item, k = total - 1, per
            if apart and not isinstance(item, int):
                wait_alone(eng, s, item * per + k, passed)
            else:
                eng.wait_ge(s, item * per + k)

        def exists(item, total):
            return not isinstance(item, int) or 0 <= item < total

        def loop(eng, step, first, last):
            lo, hi = 2, NQ // 2 - 1
            for j in range(first, min(lo, last)):
                step(j)
            if hi > lo:
                with eng.Fori(lo, hi) as j:
                    step(j)
            for j in range(max(hi, lo), last):
                step(j)

        J0, J1 = -1, NQ // 2 + 2

        def cols_of(t, n=1):
            return bass.ds(t * D, n * D)

        block = ctx.enter_context(nc.Block())

        @block.sync
        def _(sp):
            sp.dma_start(cst[:, :], a["consts"]).then_inc(const_in, 16)
            for t, n in ((wq, "WqT"), (wk, "WkT"), (wv, "WvT"), (wo, "WoT")):
                sp.dma_start(t[:, :], a[n]).then_inc(const_in, 16)
            for i, n in enumerate(("bq", "bk", "bv")):
                sp.dma_start(cols[:, i:i + 1], a[n].unsqueeze(1)).then_inc(const_in, 16)
            sp.dma_start(bo_tmp[:, :], a["bo"].unsqueeze(0).broadcast_to([P, D])).then_inc(const_in, 16)
            for b in range(2):
                sp.dma_start(srcm[b * S:(b + 1) * S, :], a["src_mask"]).then_inc(const_in, 16)
            sp.dma_start(gates[:, 0:1], a["g_xattn"].unsqueeze(0).broadcast_to([P, 1])).then_inc(const_in, 16)
            sp.dma_start(gates[:, 1:2], a["g_ffn"].unsqueeze(0).broadcast_to([P, 1])).then_inc(const_in, 16)
            sp.dma_start(gates[:, 2:3], a["shared_weight"].unsqueeze(0).broadcast_to([P, 1])).then_inc(const_in, 16)
            sp.wait_ge(setup_pool, 2)
            sp.dma_start(rw[:, 0:E], a["router_w"]).then_inc(const_in, 16)
            for t in range(QT):
                sp.dma_start(rb[32 * t:32 * t + E, :], a["router_b"].unsqueeze(1)).then_inc(const_in, 16)

            def load(q, par):
                need(sp, cT_done, q - 2, total=NQ)
                need(sp, mask_ready, q - 2, total=NQ)
                need(sp, keep_ready, q - 2, total=NQ)
                rows = bass.ds(q * QW, QW)
                done = quad_in[par]
                sp.dma_start(x_all[:, cols_of(q * QT, QT)].rearrange("p (t d) -> p t d", t=QT),
                             x_rows[rows, :].rearrange("(t p) d -> p t d", p=P)).then_inc(done, 16)
                sp.dma_start(ctx_in[:, par, :].rearrange("p (t d) -> p t d", t=QT),
                             c_rows[rows, :].rearrange("(t p) d -> p t d", p=P)).then_inc(done, 16)
                pads = pad_mask[bass.ds(q * 2 * QT, 2 * QT), :]
                for b in range(2):
                    src = pads.rearrange("(t b) k -> b t k", b=2)[b:b + 1].broadcast_to([S, QT, S])
                    sp.dma_start(pad_q[b * S:(b + 1) * S, par], src).then_inc(done, 16)
                sp.dma_start(pad_k[:, par].rearrange("p (b k) -> p b k", k=S),
                             pads.unsqueeze(0).broadcast_to([P, 2 * QT, S])).then_inc(done, 16)

            load(0, 0)
            load(1, 1)
            if NQ // 2 > 1:
                with sp.Fori(1, NQ // 2) as j:
                    load(j * 2, 0)
                    load(j * 2 + 1, 1)
            sp.dma_start(m.sw1[:, :], a["sw1"]).then_inc(m.shared_in, 16)
            for i, n in enumerate(("sgate", "sb1")):
                sp.dma_start(m.scols[:, i, :], a[n]).then_inc(m.shared_in, 16)
            sp.dma_start(m.sw2[:, :, :], a["sw2"].rearrange("(c f) d -> f c d", f=P)).then_inc(m.shared_in, 16)
            sp.dma_start(m.sb2_row[:, :], a["sb2"].unsqueeze(0).broadcast_to([P, D])).then_inc(m.shared_in, 16)

        LOADS = 5
        CONSTS = 16 * (1 + 4 + 3 + 1 + 2 + 3 + 1 + QT)

        def quad_loaded(eng, j, par, dq, apart=False):
            p2, j2 = (par + dq) % 2, j + (par + dq) // 2
            need(eng, quad_in[p2], j2, per=16 * LOADS, total=NQ // 2, apart=apart)
            return p2

        @block.tensor
        def _(pe):
            pe.wait_ge(const_in, CONSTS)
            pe.wait_ge(setup_dve, 4)
            pe.matmul(att_ps[:, 0:D], bv_mat[:, :], wo[:, :], start=True, stop=True).then_inc(setup_pe, 1)
            pe.wait_ge(setup_dve, 5)
            pe.wait_ge(setup_pool, 5)

            def scores(n, u, par, q):
                for h in range(2):
                    if u == 0 and h == 0:
                        need(pe, q_ready, q, per=NG, total=NQ)
                        need(pe, k_ready, q, per=HG, total=NQ)
                    need(pe, masked, n - 1, per=2, k=h + 1)
                    for g in (2 * h, 2 * h + 1):
                        for b in range(2):
                            i = pe.matmul(sc_ps[h][b * S:(b + 1) * S, (g % 2) * 256:(g % 2) * 256 + 256],
                                          qg[:, par, g, u * P + b * S:u * P + (b + 1) * S],
                                          kbd[:, par, 2 * u + b].rearrange("p j k -> p (j k)"), start=True, stop=True)
                    i.then_inc(scores_done, 1)

            def turn(n, u):
                need(pe, exped, n)
                for h in range(2):
                    need(pe, PT_ready, n - 1, per=2, k=h + 1)
                    for i in range(4):
                        p = 4 * h + i
                        t = pe.transpose(pt_ps[h][:, i * P:(i + 1) * P], prob[:, u, p * P:(p + 1) * P], ident)
                    t.then_inc(turned, 1)

            def project_out(n, u):
                need(pe, aT_ready, n)
                need(pe, x2_ready, n - 1)
                pe.matmul(out_ps[:, 0:D], aT[:, u % 2, :], wo[:, :], start=True, stop=True).then_inc(wo_done, 1)

            def step(j):
                for v in range(2 * QT):
                    par, u = v // QT, v % QT
                    q = j * 2 + par
                    n = j * 2 * QT + v
                    if exists(n, NT):
                        scores(n, u, par, q)
                    if u == 1:
                        need(pe, lg_copied, q - 2, total=NQ)
                    if u == 3:
                        need(pe, pref_copied, q - 2, per=2, total=NQ)
                    if u == 0:
                        need(pe, LT_ready, q - 2, total=NQ)
                    if exists(n - 3, NT):
                        project_out(n - 3, (u - 3) % QT)
                    if u == 0 and exists(q + 1, NQ):
                        need(pe, xn_ready, q + 1, per=QT, total=NQ)
                        need(pe, v_ready, q, per=4, total=NQ)
                        for t in range(QT):
                            i = pe.transpose(fa_ps[:, t * P:(t + 1) * P], xn[:, t * P:(t + 1) * P], ident)
                        i.then_inc(xT_done, 1)
                    if u == 1 and exists(q + 1, NQ):
                        need(pe, xT_ready, q + 1, total=NQ)
                        pe.matmul(fa_ps[:, :], wq[:, :], xT[:, :], start=True, stop=True).then_inc(q_done, 1)
                    if u == 2 and exists(q + 1, NQ):
                        need(pe, q_ready, q + 1, per=NG, total=NQ)
                        for t in range(QT):
                            i = pe.matmul(fa_ps[:, t * P:(t + 1) * P], cT[:, t * P:(t + 1) * P], wv[:, :],
                                          start=True, stop=True)
                        i.then_inc(v_done, 1)
                    if u == 3 and exists(q - 1, NQ):
                        need(pe, xn2_ready, q - 1, per=QT, total=NQ)
                        need(pe, kT_ready, q + 1, total=NQ)
                        for t in range(QT):
                            i = pe.transpose(fb_ps[:, t * P:(t + 1) * P], xn2[:, 1 - par, t, 0:D], ident)
                        i.then_inc(x2T_done, 1)
                    if exists(n - 2, NT):
                        turn(n - 2, (u - 2) % QT)
                    if u == 0 and exists(q + 1, NQ):
                        p2 = quad_loaded(pe, j, par, 1)
                        need(pe, x2T_ready, q - 2, total=NQ)
                        for t in range(QT):
                            i = pe.transpose(fb_ps[:, t * P:(t + 1) * P], ctx_in[:, p2, t * P:(t + 1) * P], ident)
                        i.then_inc(cT_done, 1)
                    if u == 0 and exists(q - 2, NQ):
                        need(pe, LT_ready, q - 2, total=NQ)
                        need(pe, x2_ready, n - 3)
                        pe.transpose(out_ps[:, 2 * P:3 * P], LT[:, :], ident).then_inc(lgT_done, 1)
                    if u == 1 and exists(q + 1, NQ):
                        need(pe, cT_ready, q + 1, total=NQ)
                        pe.matmul(fb_ps[:, :], wk[:, :], cT[:, :], start=True, stop=True).then_inc(k_done, 1)
                    if u == 2 and exists(q - 2, NQ):
                        need(pe, ra_step, q - 2, per=RA_STEPS, total=NQ)
                        need(pe, x2_ready, n - 3)
                        pre = out_ps[:, 3 * P:3 * P + QT * E]
                        tot = out_ps[:, 3 * P + QT * E:3 * P + (QT + 1) * E]
                        pe.matmul(pre, tri_bf[:, :], oh_bf[:, :, :].rearrange("p t e -> p (t e)"),
                                  start=True, stop=False, skip_group_check=True)
                        for t in range(QT):
                            for t2 in range(t + 1, QT + 1):
                                i = pe.matmul(out_ps[:, 3 * P + t2 * E:3 * P + (t2 + 1) * E], ones_bf[:, :],
                                              oh_bf[:, t, :], start=False, stop=(t == QT - 1),
                                              skip_group_check=True)
                        i.then_inc(pref_done, 1)
                    if u == 3 and exists(q - 1, NQ):
                        need(pe, x2T_ready, q - 1, total=NQ)
                        need(pe, x2_ready, n - 3)
                        for t in range(QT):
                            i = pe.matmul(out_ps[32 * t:32 * t + 32, P:2 * P], rw[:, :],
                                          x2T[:, 1 - par, t * P:(t + 1) * P], start=True, stop=True)
                        i.then_inc(lg_done, 1)
                    if exists(n - 2, NT):
                        if u == 2:
                            need(pe, v_ready, q, per=4, total=NQ)
                        values(n - 2, (u - 2) % QT, par if u >= 2 else 1 - par)

            def values(n, u, par):
                need(pe, PT_ready, n, per=2)
                need(pe, aT_ready, n - 1)
                for b in range(2):
                    for c in range(2):
                        for g in range(NG):
                            p = 2 * g + c
                            pe.matmul(att_ps[32 * g:32 * g + 32, b * S:(b + 1) * S],
                                      vb[:, par, u, b, 16 + VS * p - 16 * c:16 + VS * p - 16 * c + 32],
                                      PT[:, u % 2, p * P + b * S:p * P + (b + 1) * S],
                                      start=(c == 0), stop=(c == 1))
                need(pe, rs_ready, n)
                pe.transpose(att_ps[:, P:2 * P], rsx[:, u, :], ident).then_inc(att_done, 1)

            loop(pe, step, J0, J1)

        @block.vector
        def _(ve):
            ve.wait_ge(const_in, CONSTS)
            ve.tensor_copy(tri_bf[:, :], cst[:, C_TRI:C_TRI + P]).then_inc(setup_dve, 1)
            ve.tensor_copy(count[:, :], cst[:, C_BASE:C_BASE + E]).then_inc(setup_dve, 1)
            ve.tensor_scalar(cols[:, 3:4], cols[:, 0:1], float(DK) ** -0.5, None, ALU.mult).then_inc(setup_dve, 1)
            ve.tensor_copy(bv_mat[:, :], cols[:, 2:3].broadcast_to([P, P])).then_inc(setup_dve, 1)
            ve.wait_ge(setup_pe, 1)
            ve.wait_ge(setup_act, 1)
            ve.tensor_tensor(bo_tmp[:, :], att_ps[:, 0:D], bo_tmp[:, :], ALU.add).then_inc(setup_dve, 1)
            ve.wait_ge(setup_dve, 5)
            ve.tensor_scalar(bo_row[:, :], bo_tmp[:, :], gates[:, 0:1], None, ALU.mult).then_inc(setup_dve, 1)
            ve.memset(mv[:, :, :], 1.0).then_inc(setup_dve, 1)
            ve.memset(st1[:, :, :], 1.0).then_inc(setup_dve, 1)
            ve.memset(st2[:, :, :], 1.0).then_inc(setup_dve, 1)
            for t in range(NT):
                ve.tensor_scalar(tokf[:, t:t + 1], cst[:, C_PART:C_PART + 1], float(t * P), None,
                                 ALU.add).then_inc(setup_dve, 1)
            ve.wait_ge(setup_act, 2)
            ve.wait_ge(setup_dve, 9 + NT)
            ve.tensor_scalar(gates[:, 2:3], gates[:, 2:3], 1.0, None, ALU.add).then_inc(setup_dve, 1)
            ve.wait_ge(setup_dve, 10 + NT)
            ve.reciprocal(gates[:, 2:3], gates[:, 2:3]).then_inc(setup_dve, 1)

            def chain(s, base, per):
                k = [0]

                def then(ins):
                    k[0] += 1
                    ins.then_inc(s, 1)
                    ve.wait_ge(s, base * per + k[0])
                    assert k[0] <= per
                return then

            def mask_max(n, u, par, q):
                for h in range(2):
                    if h == 0:
                        need(ve, turned, n - QT, per=2)
                        need(ve, mask_ready, q, total=NQ)
                    need(ve, scores_done, n, per=2, k=h + 1)
                    ve.tensor_tensor(prob[:, u, h * 512:(h + 1) * 512].rearrange("p (h k) -> p h k", k=S),
                                     sc_ps[h][:, :].rearrange("p (h k) -> p h k", k=S),
                                     mask[:, par, u, :].unsqueeze(1).broadcast_to([P, H // 2, S]),
                                     ALU.add).then_inc(masked, 1)
                need(ve, masked, n, per=2)
                ve.tensor_reduce(mx[:, u, :], prob[:, u, :].rearrange("p (h k) -> p h k", k=S),
                                 X, ALU.max).then_inc(maxed, 1)

            def add_out(n, u, q):
                need(ve, wo_done, n)
                need(ve, xb_ready, q, total=NQ)
                xs = x_all[:, cols_of(n)]
                ve.scalar_tensor_tensor(out=xs, in0=out_ps[:, 0:D], scalar=gates[:, 0:1], in1=xs,
                                        op0=ALU.mult, op1=ALU.add).then_inc(x2_ready, 1)
                need(ve, x2_ready, n, apart=True)
                ve.bn_stats(st2[:, u, :], xs).then_inc(stats2, 1)

            def sums(n, u):
                need(ve, exped, n)
                ve.tensor_reduce(sm[:, u, :], prob[:, u, :].rearrange("p (h k) -> p h k", k=S),
                                 X, ALU.add).then_inc(summed, 1)
                need(ve, summed, n)
                ve.reciprocal(sm[:, u, :], sm[:, u, :]).then_inc(recips, 1)
                need(ve, recips, n)
                need(ve, att_done, n - QT)
                ve.tensor_copy(rsx[:, u, :].rearrange("p (h d) -> p h d", d=DK),
                               sm[:, u, :].unsqueeze(2).broadcast_to([P, H, DK])).then_inc(rs_ready, 1)

            def normalise(n, u):
                need(ve, rsT_ready, n)
                need(ve, wo_done, n - 2)
                ve.tensor_tensor(aT[:, u % 2, :], att_ps[:, 0:P], rsT[:, u % 2, :], ALU.mult).then_inc(aT_ready, 1)

            def norms(j, par, q):
                if exists(q + 2, NQ):
                    quad_loaded(ve, j, par, 2, apart=True)
                    for t in range(QT):
                        ve.bn_stats(st1[:, t, :], x_all[:, cols_of((q + 2) * QT + t)]).then_inc(stats1, 1)
                need(ve, stats1, q + 2, per=QT, total=NQ)
                need(ve, stats2, q - 1, per=QT, total=NQ)
                need(ve, xn_ready, q + 1, per=QT, total=NQ, apart=True)
                then = chain(ln_step, q + 2, LN_STEPS)
                for t in range(QT):
                    ve.bn_aggr(mv[:, t, :], st1[:, t, :])
                    i = ve.bn_aggr(mv[:, QT + t, :], st2[:, t, :])
                then(i)
                then(ve.tensor_scalar(ln_v[:, :], mv[:, :, 1], EPS, None, ALU.add))
                then(ve.tensor_scalar(ln_i[:, :], ln_v[:, :].bitcast(I32), 1, None, ALU.logical_shift_right))
                then(ve.tensor_scalar(ln_r[:, :].bitcast(I32), ln_i[:, :], -1.0, RSQRT_MAGIC, ALU.mult, ALU.add))
                for k in range(3):
                    then(ve.tensor_tensor(ln_a[:, :], ln_r[:, :], ln_r[:, :], ALU.mult))
                    then(ve.scalar_tensor_tensor(out=ln_b[:, :], in0=ln_a[:, :], scalar=-0.5, in1=ln_v[:, :],
                                                 op0=ALU.mult, op1=ALU.mult))
                    then(ve.scalar_tensor_tensor(out=ln_r[:, :], in0=ln_b[:, :], scalar=1.5, in1=ln_r[:, :],
                                                 op0=ALU.add, op1=ALU.mult))
                then(ve.scalar_tensor_tensor(out=ln_s[:, :], in0=mv[:, :, 0], scalar=-1.0, in1=ln_r[:, :],
                                             op0=ALU.mult, op1=ALU.mult))
                if exists(q - 1, NQ):
                    rp = 1 - par
                    p2, j2 = (par - 3) % 2, j + (par - 3) // 2
                    need(ve, scattered[p2], j2, per=16 * 2 * QT, total=NQ // 2)
                    for t in range(QT):
                        ve.tensor_scalar(xn2[:, rp, t, 0:D], x_all[:, cols_of((q - 1) * QT + t)],
                                         ln_r[:, QT + t:QT + t + 1], ln_s[:, QT + t:QT + t + 1],
                                         ALU.mult, ALU.add).then_inc(xn2_ready, 1)

            def route_a(q):
                need(ve, lgT_done, q, total=NQ)
                ve.tensor_copy(lg[:, :, :], out_ps[:, 2 * P:3 * P].rearrange("p (t e) -> p t e", t=QT)[:, :, 0:E])\
                    .then_inc(lg_copied, 1)
                need(ve, lg_copied, q, total=NQ)
                then = chain(ra_step, q, RA_STEPS)
                d1, c1, d2, c2 = (ra[:, i] for i in range(4))
                m1, f1, m2, f2 = (r_m[:, i] for i in range(4))

                def wide(t):
                    return t.unsqueeze(2).broadcast_to([P, QT, E])
                then(ve.tensor_reduce(m1, lg[:, :, :], X, ALU.max))
                then(ve.tensor_tensor(d1, lg[:, :, :], wide(m1), ALU.subtract))
                then(ve.scalar_tensor_tensor(out=c1, in0=d1, scalar=0.0, in1=rev, op0=ALU.is_equal, op1=ALU.mult))
                then(ve.tensor_reduce(f1, c1, X, ALU.max))
                then(ve.tensor_tensor(oh[:, 0], rev, wide(f1), ALU.is_equal))
                then(ve.scalar_tensor_tensor(out=d2, in0=oh[:, 0], scalar=-3.0e38, in1=d1, op0=ALU.mult, op1=ALU.add))
                then(ve.tensor_reduce(m2, d2, X, ALU.max))
                then(ve.tensor_tensor(c2, d2, wide(m2), ALU.is_equal))
                then(ve.tensor_tensor(c2, c2, rev, ALU.mult))
                then(ve.tensor_reduce(f2, c2, X, ALU.max))
                then(ve.tensor_tensor(oh[:, 1], rev, wide(f2), ALU.is_equal))
                then(ve.tensor_tensor(oh_bf[:, :, :], oh[:, 0], oh[:, 1], ALU.add))

            def route_b(q, par):
                need(ve, p2_ready, q, total=NQ)
                need(ve, pref_done, q, total=NQ)
                pre = out_ps[:, 3 * P:3 * P + QT * E].rearrange("p (t e) -> p t e", t=QT)
                ve.tensor_tensor(posn[:, :, :], pre, count[:, :].unsqueeze(1).broadcast_to([P, QT, E]), ALU.add)\
                    .then_inc(pref_copied, 1)
                need(ve, pref_copied, q, per=2, k=1, total=NQ)
                ve.tensor_tensor(count[:, :], out_ps[:, 3 * P + QT * E:3 * P + (QT + 1) * E], count[:, :],
                                 ALU.add).then_inc(pref_copied, 1)
                need(ve, pref_copied, q, per=2, total=NQ)
                then = chain(rb_step, q, RB_STEPS)
                p2, s2 = r_m[:, 4], r_m[:, 5]
                tiles = bass.ds(q * QT, QT)
                then(ve.tensor_scalar(s2, p2, 1.0, None, ALU.add))
                then(ve.reciprocal(s2, s2))
                ve.tensor_copy(weight[:, tiles, 0], s2)
                ve.tensor_tensor(weight[:, tiles, 1], p2, s2, ALU.mult)
                ve.tensor_scalar(xn2[:, par, :, D], r_m[:, 1], -1.0, float(E), ALU.mult, ALU.add)
                ve.tensor_copy(xn2[:, par, :, D + 1], tokf[:, tiles])
                ve.tensor_tensor(rt[:, 0], oh[:, 0], posn[:, :, :], ALU.mult)
                then(ve.tensor_tensor(rt[:, 1], oh[:, 1], posn[:, :, :], ALU.mult))
                ve.tensor_reduce(slotf[:, :, 0], rt[:, 0], X, ALU.add)
                then(ve.tensor_reduce(slotf[:, :, 1], rt[:, 1], X, ALU.add))
                then(ve.tensor_copy(slots[:, par], slotf[:, :, :]))

            def step(j):
                for v in range(2 * QT):
                    par, u = v // QT, v % QT
                    q = j * 2 + par
                    n = j * 2 * QT + v
                    if exists(n, NT):
                        mask_max(n, u, par, q)
                    if u == 1 and exists(q - 2, NQ):
                        route_a(q - 2)
                    if u == 3 and exists(q - 2, NQ):
                        route_b(q - 2, par)
                    if exists(n - 3, NT):
                        add_out(n - 3, (u - 3) % QT, q if u == 3 else q - 1)
                    if u == 2 and -2 <= (q if isinstance(q, int) else 0) and (not isinstance(q, int) or q <= NQ):
                        norms(j, par, q)
                    if exists(n - 1, NT):
                        sums(n - 1, (u - 1) % QT)
                    if u == 1 and exists(q + 1, NQ):
                        need(ve, k_done, q + 1, total=NQ)
                        need(ve, keep_ready, q + 1, total=NQ)
                        need(ve, k_ready, q, per=HG, total=NQ)
                        ve.scalar_tensor_tensor(out=kT[:, :], in0=fb_ps[:, :], scalar=cols[:, 1:2], in1=keep[:, :],
                                                op0=ALU.add, op1=ALU.mult).then_inc(kT_ready, 1)
                    if exists(n - 2, NT):
                        normalise(n - 2, (u - 2) % QT)

            loop(ve, step, J0, J1)

        @block.scalar
        def _(ac):
            ac.wait_ge(const_in, CONSTS)
            ac.activation(gates[:, 0:2], gates[:, 0:2], ACT.Tanh).then_inc(setup_act, 1)
            ac.activation(gates[:, 2:3], gates[:, 2:3], ACT.Exp, scale=-1.0).then_inc(setup_act, 1)
            ac.wait_ge(setup_dve, 9)
            ac.wait_ge(setup_pool, 5)

            def step(j):
                for v in range(2 * QT):
                    par, u = v // QT, v % QT
                    q = j * 2 + par
                    n = j * 2 * QT + v
                    if exists(n - 1, NT):
                        need(ac, subbed, n - 1)
                        ps = prob[:, (u - 1) % QT, :]
                        ac.activation(ps, ps, ACT.Exp).then_inc(exped, 1)
                    if u == 0 and exists(q + 1, NQ):
                        need(ac, xT_done, q + 1, total=NQ)
                        ac.activation(xT[:, :], fa_ps[:, :], ACT.Copy).then_inc(xT_ready, 1)
                    if u == 1 and exists(q + 1, NQ):
                        need(ac, q_done, q + 1, total=NQ)
                        for g in range(NG):
                            r = slice(32 * g, 32 * g + 32)
                            ac.activation(qg[r, 1 - par, g, :], fa_ps[r, :], ACT.Identity, bias=cols[r, 3:4],
                                          scale=float(DK) ** -0.5).then_inc(q_ready, 1)
                    if u == 3 and exists(q - 1, NQ):
                        need(ac, x2T_done, q - 1, total=NQ)
                        p2, j2 = (par - 3) % 2, j + (par - 3) // 2
                        need(ac, x2T_kept[p2], j2, per=16, total=NQ // 2)
                        ac.activation(x2T[:, p2, :], fb_ps[:, :], ACT.Copy).then_inc(x2T_ready, 1)
                        need(ac, x2T_ready, q - 1, total=NQ)
                        ac.dma_start(xn2T[:, cols_of((q - 1) * QT, QT)], x2T[:, p2, :]).then_inc(x2T_kept[p2], 16)
                    if exists(n - 2, NT):
                        w = n - 2
                        for h in range(2):
                            need(ac, turned, w, per=2, k=h + 1)
                            ac.activation(PT[:, u % 2, h * 512:(h + 1) * 512], pt_ps[h][:, :], ACT.Copy)\
                                .then_inc(PT_ready, 1)
                    if u == 0 and exists(q + 1, NQ):
                        need(ac, cT_done, q + 1, total=NQ)
                        ac.activation(cT[:, :], fb_ps[:, :], ACT.Copy).then_inc(cT_ready, 1)
                    if u == 2 and exists(q + 1, NQ):
                        need(ac, v_done, q + 1, total=NQ)
                        for b in range(2):
                            for c in range(2):
                                src = fa_ps[b * S:(b + 1) * S, :].rearrange("k (t p c d) -> k t p c d", t=QT, c=2, d=DK)
                                dst = vb[c * S:(c + 1) * S, 1 - par, :, b, :].rearrange("k t (p m) -> k t p m", m=VS)
                                src, dst = src[:, :, :, c, :], dst[:, :, :, 16 + DK * c:16 + DK * c + DK]
                                ac.activation(dst, src, ACT.Copy).then_inc(v_ready, 1)
                        need(ac, kT_ready, q + 1, total=NQ)
                        for i in range(HG):
                            dst = kbd[:, 1 - par, :, i, :]
                            ac.activation(dst, kT[:, :].rearrange("p (b k) -> p b k", k=S), ACT.Copy,
                                          scale=cst[:, C_JM + i:C_JM + i + 1]).then_inc(k_ready, 1)
                    if u == 2 and exists(q - 2, NQ):
                        need(ac, ra_step, q - 2, per=RA_STEPS, total=NQ)
                        ac.activation(r_m[:, 4], r_m[:, 2], ACT.Exp).then_inc(p2_ready, 1)
                    if u == 3 and exists(q + 2, NQ):
                        need(ac, ln_step, q + 2, per=LN_STEPS, total=NQ + 3)
                        need(ac, xT_done, q + 1, total=NQ)
                        for t in range(QT):
                            ac.activation(xn[:, t * P:(t + 1) * P], x_all[:, cols_of((q + 2) * QT + t)], ACT.Identity,
                                          bias=ln_s[:, t:t + 1], scale=ln_r[:, t:t + 1]).then_inc(xn_ready, 1)
                    if u == 3 and exists(q - 1, NQ):
                        need(ac, lg_done, q - 1, total=NQ)
                        ac.activation(LT[:, :], out_ps[:, P:2 * P], ACT.Identity, bias=rb[:, 0:1]).then_inc(LT_ready, 1)
                    if exists(n - 2, NT):
                        need(ac, att_done, n - 2)
                        ac.activation(rsT[:, u % 2, :], att_ps[:, P:2 * P], ACT.Copy).then_inc(rsT_ready, 1)

            loop(ac, step, J0, J1)
            for i in range(2):
                ac.wait_ge(x2T_kept[i], 16 * (NQ // 2))

        @block.gpsimd
        def _(po):
            po.memset(rw[:, :], 0.0).then_inc(setup_pool, 1)
            po.memset(rb[:, :], 0.0).then_inc(setup_pool, 1)
            po.memset(qg[:, :, :, :], 0.0).then_inc(setup_pool, 1)
            po.memset(vb[:, :, :, :, :], 0.0).then_inc(setup_pool, 1)
            po.memset(ones_bf[:, :], 1.0).then_inc(setup_pool, 1)
            po.wait_ge(const_in, CONSTS)
            po.wait_ge(setup_dve, 9 + NT)

            def scatter(q, par, which):
                need(po, rb_step, q, per=RB_STEPS, total=NQ, apart=True)
                scatter_rows(po, lists, m, par, which)

            def step(j):
                for v in range(2 * QT):
                    par, u = v // QT, v % QT
                    q = j * 2 + par
                    n = j * 2 * QT + v
                    if exists(n, NT):
                        need(po, maxed, n)
                        ps = prob[:, u, :].rearrange("p (h k) -> p h k", k=S)
                        po.tensor_tensor(ps, ps, mx[:, u, :].unsqueeze(2).broadcast_to([P, H, S]),
                                         ALU.subtract).then_inc(subbed, 1)
                    if u == 0 and exists(q + 1, NQ):
                        p2 = quad_loaded(po, j, par, 1)
                        need(po, kT_ready, q, total=NQ, apart=True)
                        po.tensor_scalar(keep[:, :], pad_k[:, p2, :], 0, -1.0, ALU.is_equal, ALU.mult).then_inc(keep_tmp, 1)
                        need(po, keep_tmp, q + 1, total=NQ, apart=True)
                        po.tensor_scalar(keep[:, :], keep[:, :], 1.0, None, ALU.add).then_inc(keep_ready, 1)
                        po.tensor_scalar(mask[:, p2], pad_q[:, p2], 0, NEG, ALU.is_equal, ALU.mult).then_inc(mask_tmp, 1)
                        need(po, mask_tmp, q + 1, total=NQ)
                        po.tensor_tensor(mask[:, p2], mask[:, p2], srcm[:, :].unsqueeze(1).broadcast_to([P, QT, S]),
                                         ALU.add).then_inc(mask_ready, 1)
                        need(po, xn_ready, q + 1, per=QT, total=NQ, apart=True)
                        xs = x_all[:, cols_of((q + 1) * QT, QT)].rearrange("p (t d) -> p t d", t=QT)
                        po.tensor_tensor(xs, xs, bo_row[:, :].unsqueeze(1).broadcast_to([P, QT, D]),
                                         ALU.add).then_inc(xb_ready, 1)
                    if u == 3 and exists(q - 2, NQ - 2):
                        scatter(q - 2, par, range(0, 2))
                    if u == 0 and exists(q - 3, NQ - 2):
                        scatter(q - 3, 1 - par, range(2, 5))
                    if u == 1 and exists(q - 3, NQ - 2):
                        scatter(q - 3, 1 - par, range(5, 8))

            loop(po, step, J0, J1)


def experts(nc, a, NT, REGION, lists, results, m):
    TOK = NT * P
    NQ = NT // QT
    FC = F // P
    SC = FS // P
    HB = FC * SL // 512
    T = steps_listed(NT)
    xn2T, cst, gates, count, banks = m.xn2T, m.cst, m.gates, m.count, m.banks
    sw1, sw2, scols, sb2_row, shared_in = m.sw1, m.sw2, m.scols, m.sb2_row, m.shared_in
    with ExitStack() as ctx:
        sb, sem = tools(nc, ctx)
        hs = sb("hs", [P, 2, SC, QW])
        w1 = sb("w1", [P, E, F])
        w2 = sb("w2", [P, E, FC, D])
        gate_c = sb("gate_c", [P, FC, E])
        b1g_c = sb("b1g_c", [P, FC, E])
        b2_row = sb("b2_row", [P, E, D])
        pad_rows = sb("pad_rows", [P, E + 1, 2, ROW])
        tf = sb("tf", [P, 4, E])
        trips = sb("trips", [P, E], I32)
        ends = sb("ends", [P, E], I32)
        begun = sb("begun", [P, T, E])
        step_f = sb("step_f", [P, 2, T])
        expert_of = sb("expert_of", [P, T], I32)
        row_of = sb("row_of", [P, T], I32)
        pairs = sb("pairs", [P, 1], I32)
        rows = sb("rows", [P, 2, 2, ROW])
        meta = sb("meta", [P, 2, 2, 2])
        destf = sb("destf", [P, 2])
        dest = sb("dest", [P, 2, 2, 1], I32)
        rT = sb("rT", [P, 2, SL])
        w1_now = sb("w1_now", [P, 2, F])
        hT = sb("hT", [P, 2, FC, SL])
        y = sb("y", [P, 2, 2, D])

        sh_ps, sy_ps = [banks[0:2], banks[2:4]], banks[4:6]
        h_ps, y_ps, t_ps = [banks[0:2], banks[2:4]], banks[4:6], banks[6:8]

        biases_in, weights_in = sem("biases_in"), sem("weights_in")
        shared_scaled, biases_ready = sem("shared_scaled"), sem("biases_ready")
        sh_done, sh_gelued, sy_done, kept = (sem(n) for n in ("sh_done", "sh_gelued", "sy_done", "kept"))
        plan_step, pads_ready, pads_in, table_ready = (sem(n) for n in ("plan_step", "pads_ready", "pads_in", "table_ready"))
        rows_in = [sem(f"rows_in{i}") for i in range(2)]
        meta_read, turned, rT_ready = (sem(n) for n in ("meta_read", "rows_turned", "rT_ready"))
        h_done, gelued, y_done, y_ready = (sem(n) for n in ("h_done", "gelued", "y_done", "y_ready"))
        dest_step, w1_ready = sem("dest_step"), sem("w1_ready")
        sent = [sem(f"sent{i}") for i in range(2)]
        passed = sem("e_passed")

        def wait_apart(eng, s, value):
            wait_alone(eng, s, value, passed)

        def iterations(eng, body):
            n = eng.value_load(pairs[0:1, 0:1], min_val=TOK // SL, max_val=(T - 2) // 2)
            body(0, 0, 0)
            body(1, 1, 0)
            with eng.Fori(1, n) as i:
                body(i * 2, 0, i)
                body(i * 2 + 1, 1, i)

        def expert(eng, t):
            return eng.value_load(expert_of[0:1, bass.ds(t, 1)], min_val=0, max_val=E - 1)

        block = ctx.enter_context(nc.Block())

        @block.sync
        def _(sp):
            sp.dma_start(gate_c[:, :, :], a["gate"]).then_inc(biases_in, 16)
            sp.dma_start(b1g_c[:, :, :], a["b1"]).then_inc(biases_in, 16)
            sp.dma_start(b2_row[:, :, :], a["b2"].unsqueeze(0).broadcast_to([P, E, D])).then_inc(biases_in, 16)
            sp.wait_ge(table_ready, 1)
            sp.wait_ge(pads_ready, 2)
            for e in range(E):
                at = sp.value_load(ends[0:1, e:e + 1], min_val=e * REGION, max_val=e * REGION + TOK)
                sp.dma_start(lists[bass.ds(at, SL), :].rearrange("(t p) d -> p t d", p=P), pad_rows[:, e])\
                  .then_inc(pads_in, 16)
            for i in range(3):
                sp.dma_start(lists[E * REGION + i * SL:E * REGION + (i + 1) * SL, :]
                             .rearrange("(t p) d -> p t d", p=P), pad_rows[:, E]).then_inc(pads_in, 16)
            sp.wait_ge(pads_in, 16 * (E + 3))
            for i in range(2):
                sp.wait_ge(m.scattered[i], 16 * 2 * QT * (NQ // 2))

            def load(t, par, wait=True):
                at = sp.value_load(row_of[0:1, bass.ds(t, 1)], min_val=0, max_val=E * REGION + 2 * SL)
                if wait:
                    sp.wait_ge(turned, t - 1)
                    sp.wait_ge(meta_read, t - 1)
                sp.dma_start(rows[:, par], lists[bass.ds(at, SL), :].rearrange("(t p) d -> p t d", p=P))\
                  .then_inc(rows_in[par], 16)
            load(0, 0, False)
            load(1, 1, False)
            iterations(sp, lambda t, par, i: load(t + 2, par))
            n = sp.value_load(pairs[0:1, 0:1], min_val=TOK // SL, max_val=(T - 2) // 2)
            for i in range(2):
                wait_apart(sp, rows_in[i], n * 16 + 16)
                wait_apart(sp, sent[i], n * 32)

        @block.tensor
        def _(pe):
            ident = cst[:, C_ID:C_ID + P]

            def hidden(q, par):
                for c in range(SC):
                    if not isinstance(q, int) or q >= 2:
                        pe.wait_ge(sh_gelued, (q - 2) * SC + c + 1)
                    pe.matmul(sh_ps[par][c][:, :], sw1[:, c * P:(c + 1) * P], xn2T[:, bass.ds(q * QW, QW)],
                              start=True, stop=True).then_inc(sh_done, 1)

            def second(q, par):
                pe.wait_ge(sh_gelued, q * SC + SC)
                if not isinstance(q, int) or q >= 2:
                    pe.wait_ge(kept, q - 1)
                for t in range(QT):
                    for c in range(SC):
                        last = pe.matmul(sy_ps[par][:, t * D:(t + 1) * D], hs[:, par, c, t * P:(t + 1) * P],
                                      sw2[:, c, :], start=(c == 0), stop=(c == SC - 1))
                last.then_inc(sy_done, 1)

            pe.wait_ge(shared_in, 80)
            pe.wait_ge(shared_scaled, 3)
            hidden(0, 0)
            hidden(1, 1)
            second(0, 0)
            with pe.Fori(1, NQ // 2) as j:
                hidden(j * 2, 0)
                second(j * 2 - 1, 1)
                hidden(j * 2 + 1, 1)
                second(j * 2, 0)
            second(NQ - 1, 1)

            def turn(t, par, i):
                pe.wait_ge(rows_in[par], i * 16 + 16)
                if not isinstance(t, int) or t >= 2:
                    pe.wait_ge(rT_ready, t - 1)
                for h in range(2):
                    last = pe.transpose(t_ps[par][:, h * P:(h + 1) * P], rows[:, par, h, 0:D], ident)
                last.then_inc(turned, 1)

            def first_layer(t, par):
                pe.wait_ge(rT_ready, t + 1)
                pe.wait_ge(w1_ready, t + 1)
                if not isinstance(t, int) or t >= 2:
                    pe.wait_ge(gelued, (t - 1) * FC)
                for c in range(FC):
                    last = pe.matmul(h_ps[par][c // 2][:, (c % 2) * SL:(c % 2 + 1) * SL],
                                  w1_now[:, par, c * P:(c + 1) * P], rT[:, par, :], start=True, stop=True)
                    if c % 2:
                        last.then_inc(h_done, 1)

            def second_layer(t, par, e):
                if not isinstance(t, int) or t >= 2:
                    pe.wait_ge(y_ready, t - 1)
                for h in range(2):
                    for c in range(FC):
                        if h == 0:
                            pe.wait_ge(gelued, t * FC + c + 1)
                        last = pe.matmul(y_ps[par][:, h * D:(h + 1) * D], hT[:, par, c, h * P:(h + 1) * P],
                                      w2[:, bass.ds(e, 1), c, :].rearrange("p a d -> p (a d)"),
                                      start=(c == 0), stop=(c == FC - 1))
                last.then_inc(y_done, 1)

            pe.wait_ge(table_ready, 1)
            turn(0, 0, 0)
            pe.wait_ge(weights_in, 64)
            pe.wait_ge(sh_gelued, NQ * SC)
            pe.wait_ge(kept, NQ)
            first_layer(0, 0)
            turn(1, 1, 0)

            def body(t, par, i):
                first_layer(t + 1, 1 - par)
                turn(t + 2, par, i + 1)
                second_layer(t, par, expert(pe, t))
            iterations(pe, body)

        @block.scalar
        def _(ac):
            for k in range(2):
                es = slice(k * E // 2, (k + 1) * E // 2)
                ac.dma_start(w1[:, es, :], a["w1"][es].rearrange("e d f -> d e f")).then_inc(weights_in, 16)
                ac.dma_start(w2[:, es], a["w2"][es].rearrange("e (c f) d -> f e c d", f=P)).then_inc(weights_in, 16)
            ac.wait_ge(shared_scaled, 1)

            def shared_gelu(q, par):
                for c in range(SC):
                    if c == 0 and (not isinstance(q, int) or q >= 2):
                        ac.wait_ge(sy_done, q - 1)
                    ac.wait_ge(sh_done, q * SC + c + 1)
                    ac.activation(hs[:, par, c, :], sh_ps[par][c][:, :], ACT.Gelu, bias=scols[:, 2, c:c + 1],
                                  scale=scols[:, 0, c:c + 1]).then_inc(sh_gelued, 1)
            shared_gelu(0, 0)
            shared_gelu(1, 1)
            with ac.Fori(1, NQ // 2) as j:
                shared_gelu(j * 2, 0)
                shared_gelu(j * 2 + 1, 1)

            ac.wait_ge(biases_ready, 1)
            ac.wait_ge(table_ready, 1)

            def body(t, par, i):
                e = expert(ac, t)
                if not isinstance(t, int) or t >= 2:
                    ac.wait_ge(y_done, t - 1)
                for c in range(FC):
                    if c % 2 == 0:
                        ac.wait_ge(h_done, t * HB + c // 2 + 1)
                    ac.activation(hT[:, par, c, :], h_ps[par][c // 2][:, (c % 2) * SL:(c % 2 + 1) * SL], ACT.Gelu,
                                  bias=b1g_c[:, c, bass.ds(e, 1)], scale=gate_c[:, c, bass.ds(e, 1)])\
                      .then_inc(gelued, 1)
            iterations(ac, body)

        @block.vector
        def _(ve):
            ve.wait_ge(shared_in, 80)
            ve.tensor_tensor(scols[:, 2, :], scols[:, 0, :], scols[:, 1, :], ALU.mult).then_inc(shared_scaled, 1)
            ve.tensor_scalar(sw2[:, :, :], sw2[:, :, :], gates[:, 2:3], None, ALU.mult).then_inc(shared_scaled, 1)
            ve.tensor_scalar(sb2_row[:, :], sb2_row[:, :], gates[:, 2:3], None, ALU.mult).then_inc(shared_scaled, 1)

            steps = [0]

            def then(ins):
                steps[0] += 1
                ins.then_inc(plan_step, 1)
                ve.wait_ge(plan_step, steps[0])
            n, cum, gap = tf[:, 0], tf[:, 1], tf[:, 2]
            then(ve.tensor_tensor(n, count[:, :], cst[:, C_BASE:C_BASE + E], ALU.subtract))
            then(ve.tensor_scalar(n, n, float(SL - 1), None, ALU.add))
            then(ve.tensor_copy(trips[:, :], n))
            then(ve.tensor_scalar(trips[:, :], trips[:, :], SL.bit_length() - 1, None, ALU.logical_shift_right))
            then(ve.tensor_copy(cum, trips[:, :]))
            then(ve.tensor_scalar(gap, cum, -float(SL), float(REGION), ALU.mult, ALU.add))
            for e in range(1, E):
                then(ve.tensor_tensor(cum[:, e:e + 1], cum[:, e - 1:e], cum[:, e:e + 1], ALU.add))
            then(ve.tensor_tensor(begun[:, :, :], cst[:, C_STEP:C_STEP + T].unsqueeze(2).broadcast_to([P, T, E]),
                                  cum.unsqueeze(1).broadcast_to([P, T, E]), ALU.is_ge))
            then(ve.tensor_reduce(step_f[:, 0], begun[:, :, :], X, ALU.add))
            then(ve.tensor_scalar(expert_of[:, :], step_f[:, 0], float(E - 1), None, ALU.min))
            then(ve.tensor_tensor(begun[:, :, :], begun[:, :, :], gap.unsqueeze(1).broadcast_to([P, T, E]), ALU.mult))
            then(ve.tensor_reduce(step_f[:, 1], begun[:, :, :], X, ALU.add))
            then(ve.scalar_tensor_tensor(out=row_of[:, :], in0=cst[:, C_STEP:C_STEP + T], scalar=float(SL),
                                         in1=step_f[:, 1], op0=ALU.mult, op1=ALU.add))
            then(ve.tensor_scalar(tf[:, 3, 0:1], cum[:, E - 1:E], 1.0, None, ALU.add))
            then(ve.tensor_copy(pairs[:, :], tf[:, 3, 0:1]))
            then(ve.tensor_scalar(pairs[:, :], pairs[:, :], 1, None, ALU.logical_shift_right))
            ve.tensor_copy(ends[:, :], count[:, :]).then_inc(table_ready, 1)
            ve.wait_ge(biases_in, 48)
            ve.tensor_tensor(b1g_c[:, :, :], b1g_c[:, :, :], gate_c[:, :, :], ALU.mult).then_inc(biases_ready, 1)

            def keep(q, par):
                ve.wait_ge(sy_done, q + 1)
                out = xn2T[:, bass.ds(q * QW, QW)].rearrange("p (t d) -> p t d", d=D)
                ve.tensor_tensor(out, sy_ps[par][:, :].rearrange("p (t d) -> p t d", d=D),
                                 sb2_row[:, :].unsqueeze(1).broadcast_to([P, QT, D]), ALU.add).then_inc(kept, 1)
            with ve.Fori(0, NQ // 2) as j:
                keep(j * 2, 0)
                keep(j * 2 + 1, 1)

            def take_meta(t, par, i):
                ve.wait_ge(rows_in[par], i * 16 + 16)
                if not isinstance(t, int) or t >= 2:
                    ve.wait_ge(dest_step, (t - 1) * 3)
                ve.tensor_copy(meta[:, par], rows[:, par, :, D:ROW]).then_inc(meta_read, 1)

            def take_rows(t, par):
                ve.wait_ge(turned, t + 1)
                if not isinstance(t, int) or t >= 2:
                    ve.wait_ge(h_done, (t - 1) * HB)
                ve.tensor_copy(rT[:, par, :], t_ps[par][:, 0:SL]).then_inc(rT_ready, 1)

            def take_weights(t, par):
                e = expert(ve, t)
                if not isinstance(t, int) or t >= 2:
                    wait_apart(ve, h_done, (t - 1) * HB)
                ve.tensor_copy(w1_now[:, par, :], w1[:, bass.ds(e, 1), :].rearrange("p a f -> p (a f)"))\
                  .then_inc(w1_ready, 1)

            def destinations(t, par, i, e):
                ve.wait_ge(meta_read, t + 1)
                if not isinstance(t, int) or t >= 2:
                    ve.wait_ge(dest_step, t * 3)
                ve.tensor_scalar(destf[:, :], meta[:, par, :, 0], cst[:, bass.ds(C_EXP + e, 1)], float(TOK),
                                 ALU.not_equal, ALU.mult).then_inc(dest_step, 1)
                ve.wait_ge(dest_step, t * 3 + 1)
                ve.tensor_tensor(destf[:, :], destf[:, :], meta[:, par, :, 1], ALU.add).then_inc(dest_step, 1)
                ve.wait_ge(dest_step, t * 3 + 2)
                if not isinstance(i, int) or i >= 1:
                    ve.wait_ge(sent[par], i * 32)
                ve.tensor_copy(dest[:, par, :, 0], destf[:, :]).then_inc(dest_step, 1)

            ve.wait_ge(table_ready, 1)
            ve.wait_ge(weights_in, 64)
            for t in range(2):
                take_weights(t, t)
            for t in range(2):
                take_meta(t, t, 0)
                take_rows(t, t)

            def body(t, par, i):
                take_weights(t + 2, par)
                e = expert(ve, t)
                take_rows(t + 2, par)
                destinations(t, par, i, e)
                take_meta(t + 2, par, i + 1)
                ve.wait_ge(y_done, t + 1)
                ve.tensor_tensor(y[:, par], y_ps[par][:, 0:2 * D].rearrange("p (h d) -> p h d", d=D),
                                 b2_row[:, bass.ds(e, 1), :].broadcast_to([P, 2, D]), ALU.add).then_inc(y_ready, 1)
            iterations(ve, body)

        @block.gpsimd
        def _(po):
            for par in range(2):
                scatter_rows(po, lists, m, par, range(2 * QT))
            po.memset(pad_rows[:, :, :, :], 0.0).then_inc(pads_ready, 1)
            po.wait_ge(pads_ready, 1)
            po.memset(pad_rows[:, :, :, D:D + 1], -1.0)
            for e in range(E + 1):
                for h in range(2):
                    last = po.tensor_scalar(pad_rows[:, e, h, D + 1:ROW], cst[:, C_PART:C_PART + 1],
                                            float(TOK + e * SL + h * P), None, ALU.add)
            last.then_inc(pads_ready, 1)
            po.wait_ge(table_ready, 1)

            def body(t, par, i):
                po.wait_ge(dest_step, t * 3 + 3)
                wait_apart(po, y_ready, t + 1)
                for h in range(2):
                    po.indirect_dma_start(results[:, :], bass.IndirectOffsetOnAxis(ap=dest[:, par, h, :], axis=0),
                                          y[:, par, h, :], None).then_inc(sent[par], 16)
            iterations(po, body)


def combine(nc, a, NT, results, out, m):
    NQ = NT // QT
    TOK = NT * P
    x_all, xn2T, weight, gates = m.x_all, m.xn2T, m.weight, m.gates
    out_rows = out.rearrange("b s d -> (b s) d")
    with ExitStack() as ctx:
        sb, sem = tools(nc, ctx)
        ln_row = sb("ln_row", [P, 2, D])
        yin = sb("yin", [P, 2, 2, QT, D])
        acc = sb("acc", [P, 2, QT, D])
        st = sb("st", [P, QT, 6])
        mv = sb("mv3", [P, 2, QT, 2])
        tmp = sb("tmp", [P, 5, QT])
        tmi = sb("tmi", [P, QT], I32)
        rr = sb("rr", [P, 2, 2, QT])
        res = sb("res", [P, 2, QT, D])

        w_in, setup, wready = sem("sw_in"), sem("s_setup"), sem("s_wready")
        y_in = [sem(f"y_in{i}") for i in range(2)]
        h_done, h_ready, y_done, acc_step, stat_step, n_step, normed, scaled, xb, fin = (
            sem("c_" + n) for n in ("h_done", "h_ready", "y_done", "acc_step", "stat_step", "n_step", "normed",
                                    "scaled", "xb", "fin"))
        stored = [sem(f"stored{i}") for i in range(2)]
        passed = sem("c_passed")
        N_STEPS = 14

        def wait_apart(eng, s, value):
            wait_alone(eng, s, value, passed)

        block = ctx.enter_context(nc.Block())

        @block.sync
        def _(sp):
            for i, n in enumerate(("ln_g", "ln_b")):
                sp.dma_start(ln_row[:, i, :], a[n].unsqueeze(0).broadcast_to([P, D])).then_inc(w_in, 16)

            def load(q, par, wait):
                if wait:
                    sp.wait_ge(acc_step, (q - 1) * 2 * QT)
                for k in range(2):
                    sp.dma_start(yin[:, par, k], results[bass.ds(q * QW + k * TOK, QW), :]
                                 .rearrange("(t p) d -> p t d", p=P)).then_inc(y_in[par], 16)
            load(0, 0, False)
            load(1, 1, False)
            if NQ > 2:
                with sp.Fori(1, NQ // 2) as j:
                    for par in range(2):
                        load(j * 2 + par, par, True)

        @block.scalar
        def _(ac):
            def scale(q, par):
                ac.wait_ge(n_step, q * N_STEPS + N_STEPS)
                for t in range(QT):
                    ac.activation(acc[:, par, t, :], acc[:, par, t, :], ACT.Identity, bias=rr[:, par, 1, t:t + 1],
                                  scale=rr[:, par, 0, t:t + 1]).then_inc(scaled, 1)
            with ac.Fori(0, NQ // 2) as j:
                for par in range(2):
                    scale(j * 2 + par, par)

        @block.vector
        def _(ve):
            ve.wait_ge(w_in, 32)
            ve.tensor_scalar(ln_row[:, :, :], ln_row[:, :, :], gates[:, 1:2], None, ALU.mult).then_inc(setup, 1)

            def quad(q, par, j):
                ve.wait_ge(y_in[par], j * 32 + 32)
                if not isinstance(j, int) or j > 0:
                    ve.wait_ge(fin, q - 1)
                for t in range(QT):
                    w = weight[:, bass.ds(q * QT + t, 1), :].rearrange("p a k -> p (a k)")
                    ve.scalar_tensor_tensor(out=acc[:, par, t, :], in0=yin[:, par, 0, t, :], scalar=w[:, 0:1],
                                            in1=xn2T[:, bass.ds(q * QW + t * D, D)], op0=ALU.mult, op1=ALU.add)\
                      .then_inc(acc_step, 1)
                for t in range(QT):
                    w = weight[:, bass.ds(q * QT + t, 1), :].rearrange("p a k -> p (a k)")
                    ve.wait_ge(acc_step, q * 2 * QT + t + 1)
                    ve.scalar_tensor_tensor(out=acc[:, par, t, :], in0=yin[:, par, 1, t, :], scalar=w[:, 1:2],
                                            in1=acc[:, par, t, :], op0=ALU.mult, op1=ALU.add).then_inc(acc_step, 1)
                for t in range(QT):
                    wait_apart(ve, acc_step, q * 2 * QT + QT + t + 1)
                    ve.bn_stats(st[:, t, :], acc[:, par, t, :]).then_inc(stat_step, 1)
                for t in range(QT):
                    wait_apart(ve, stat_step, q * QT + t + 1)
                    i = ve.bn_aggr(mv[:, par, t, :], st[:, t, :])
                k = [0]

                def then(ins):
                    k[0] += 1
                    ins.then_inc(n_step, 1)
                    ve.wait_ge(n_step, q * N_STEPS + k[0])
                v, aa, bb = tmp[:, 0], tmp[:, 1], tmp[:, 2]
                rs, sh = rr[:, par, 0], rr[:, par, 1]
                then(i)
                then(ve.tensor_scalar(v, mv[:, par, :, 1], EPS, None, ALU.add))
                then(ve.tensor_scalar(tmi[:, :], v.bitcast(I32), 1, None, ALU.logical_shift_right))
                then(ve.tensor_scalar(rs.bitcast(I32), tmi[:, :], -1.0, RSQRT_MAGIC, ALU.mult, ALU.add))
                for _ in range(3):
                    then(ve.tensor_tensor(aa, rs, rs, ALU.mult))
                    then(ve.scalar_tensor_tensor(out=bb, in0=aa, scalar=-0.5, in1=v, op0=ALU.mult, op1=ALU.mult))
                    then(ve.scalar_tensor_tensor(out=rs, in0=bb, scalar=1.5, in1=rs, op0=ALU.add, op1=ALU.mult))
                then(ve.scalar_tensor_tensor(out=sh, in0=mv[:, par, :, 0], scalar=-1.0, in1=rs, op0=ALU.mult,
                                             op1=ALU.mult))

            quad(0, 0, 0)
            quad(1, 1, 0)
            with ve.Fori(1, NQ // 2) as j:
                for par in range(2):
                    quad(j * 2 + par, par, j)

        @block.gpsimd
        def _(po):
            po.wait_ge(setup, 1)

            def finish(q, par, wait):
                xs = x_all[:, bass.ds(q * QW, QW)].rearrange("p (t d) -> p t d", t=QT)
                po.tensor_tensor(xs, xs, ln_row[:, 1, :].unsqueeze(1).broadcast_to([P, QT, D]), ALU.add).then_inc(xb, 1)
                po.wait_ge(scaled, q * QT + QT)
                if wait:
                    po.wait_ge(stored[par], (q - par) * 8)
                po.tensor_tensor(res[:, par], acc[:, par], ln_row[:, 0, :].unsqueeze(1).broadcast_to([P, QT, D]),
                                 ALU.mult).then_inc(fin, 1)
                po.wait_ge(fin, q + 1)
                wait_apart(po, xb, q * 2 + 1)
                po.tensor_tensor(res[:, par], res[:, par], xs, ALU.add).then_inc(xb, 1)
                po.wait_ge(xb, q * 2 + 2)
                po.dma_start(out_rows[bass.ds(q * QW, QW), :].rearrange("(t p) d -> p t d", p=P), res[:, par])\
                  .then_inc(stored[par], 16)
            finish(0, 0, False)
            finish(1, 1, False)
            with po.Fori(1, NQ // 2) as j:
                for par in range(2):
                    finish(j * 2 + par, par, True)
            for i in range(2):
                po.wait_ge(stored[i], 8 * NQ)


def build_inputs(inputs):
    g = {k: np.asarray(v) for k, v in inputs.items()}
    f32 = {}
    f32["x"], f32["ctx_1024"] = g["x"], g["ctx_1024"]
    f32["mask_BxS2_ik0"] = g["mask_BxS2_ik0"]
    f32["src_mask"] = g["mask_1x1xSxS2_ff0"][0, 0]
    for n in ("Wq", "Wk", "Wv", "Wo"):
        f32[n + "T"] = g["L0_xattn_" + n].T
    for n in ("bq", "bk", "bv", "bo"):
        f32[n] = g["L0_xattn_" + n]
    f32["g_xattn"], f32["g_ffn"] = g["g_xattn"], g["g_ffn"]
    f32["shared_weight"] = g["L0_ffn_shared_weight"].reshape(1)
    for n in ("router_w", "router_b"):
        f32[n] = g["L0_ffn_" + n]
    for n in ("w1", "b1", "gate", "w2", "b2", "sw1", "sb1", "sgate", "sw2", "sb2", "ln_g", "ln_b"):
        f32[n] = g["L0_ffn_" + n]
    for n in ("b1", "gate"):
        f32[n] = f32[n].reshape(E, F // P, P).transpose(2, 1, 0)
    for n in ("sb1", "sgate"):
        f32[n] = f32[n].reshape(FS // P, P).T
    f32["consts"] = constants(g["x"].shape[0] // 2)
    return {k: np.ascontiguousarray(v) for k, v in f32.items()}


def kernel(**inputs):
    import concourse.bacc as bacc
    from concourse.bass_utils import run_bass_kernel_spmd

    arrays = build_inputs(inputs)
    nc = bacc.Bacc("TRN2", target_bir_lowering=False, num_devices=1)
    a = {n: nc.dram_tensor(f"in_{n}", v.shape, mybir.dt.from_np(v.dtype), kind="ExternalInput").ap()
         for n, v in arrays.items()}
    out = nc.dram_tensor("out", inputs["x"].shape, F32, kind="ExternalOutput").ap()
    bass_kernel(nc, a, out)
    r = run_bass_kernel_spmd(nc, [{f"in_{n}": v for n, v in arrays.items()}], core_ids=[0])
    return r.results[0]["out"]
```

```python
from contextlib import ExitStack

import numpy as np
import concourse.bass as bass
from concourse import mybir
from concourse.alu_op_type import AluOpType as ALU

ACT = mybir.ActivationFunctionType
F32 = mybir.dt.float32
BF16 = mybir.dt.bfloat16
I32 = mybir.dt.int32
X = mybir.AxisListType.X

P = 128
D = 128
H = 16
DK = D // H
HG = 32 // DK
NG = H // HG
S = 64
E = 8
F = 512
FS = 256
QT = 4
QW = QT * D
VS = 48
ROW = D + 2
SL = 256
NEG = -1.0e9
EPS = 1e-5
RSQRT_MAGIC = float(0x5F3759DF)
LN_STEPS = 14
RA_STEPS = 12
RB_STEPS = 5

C_ID = 0
C_TRI = C_ID + P
C_JM = C_TRI + P
C_REV = C_JM + HG
C_BASE = C_REV + QT * E
C_PART = C_BASE + E
C_EXP = C_PART + 1
C_STEP = C_EXP + E


def steps_listed(NT):
    return 2 * NT * P // SL + E + 2


def constants(NT):
    c = np.zeros((P, C_STEP + steps_listed(NT)), np.float32)
    p = np.arange(P)
    c[:, C_ID:C_ID + P] = np.eye(P)
    c[:, C_TRI:C_TRI + P] = p[:, None] < p[None, :]
    c[:, C_JM:C_JM + HG] = (p[:, None] % 32) // DK == np.arange(HG)[None, :]
    c[:, C_REV:C_REV + QT * E] = np.tile(E - np.arange(E), QT)
    c[:, C_BASE:C_BASE + E] = np.arange(E) * (NT * P + SL)
    c[:, C_PART] = p
    c[:, C_EXP:C_EXP + E] = np.arange(E)
    c[:, C_STEP:] = np.arange(steps_listed(NT))
    return c


def bass_kernel(nc, a, out):
    NT = a["x"].shape[0] // 2
    TOK = NT * P
    REGION = TOK + SL
    assert NT % (2 * QT) == 0


    lists = nc.dram_tensor("expert_lists", [E * REGION + 3 * SL, ROW], F32).ap()
    results = nc.dram_tensor("expert_results", [2 * TOK + (E + 1) * SL, D], F32).ap()

    with ExitStack() as whole:
        m = shared_memory(nc, whole, NT)
        attention(nc, a, NT, lists, m)
        experts(nc, a, NT, REGION, lists, results, m)
        combine(nc, a, NT, results, out, m)


def wait_alone(eng, s, value, passed):
    eng.wait_ge(s, value)
    eng.sem_inc(passed, 1)


def tools(nc, ctx):
    def sb(name, shape, dt=F32):
        return ctx.enter_context(nc.sbuf_tensor(name, shape, dt))

    def sem(name):
        return ctx.enter_context(nc.semaphore(name))
    return sb, sem


class Shared:
    pass


def shared_memory(nc, ctx, NT):
    sb, sem = tools(nc, ctx)
    m = Shared()
    m.x_all = sb("x_all", [P, NT * D])
    m.xn2T = sb("xn2T", [P, NT * D])
    m.weight = sb("weight", [P, NT, 2])
    m.cst = sb("cst", [P, C_STEP + steps_listed(NT)])
    m.gates = sb("gates", [P, 4])
    m.count = sb("count", [P, E])
    m.xn2 = sb("xn2", [P, 2, QT, ROW])
    m.slots = sb("slots", [P, 2, QT, 2], I32)
    m.scattered = [sem(f"scattered{i}") for i in range(2)]
    m.sw1 = sb("sw1", [P, FS])
    m.sw2 = sb("sw2", [P, FS // P, D])
    m.scols = sb("scols", [P, 3, FS // P])
    m.sb2_row = sb("sb2_row", [P, D])
    m.shared_in = sem("shared_in")
    m.banks = [ctx.enter_context(nc.psum_tensor(f"bank{i}", [P, 512], F32)) for i in range(8)]
    return m


def scatter_rows(po, lists, m, par, which):
    for i in which:
        t, k = i // 2, i % 2
        po.indirect_dma_start(lists[:, :], bass.IndirectOffsetOnAxis(ap=m.slots[:, par, t, k:k + 1], axis=0),
                              m.xn2[:, par, t, :], None).then_inc(m.scattered[par], 16)


def attention(nc, a, NT, lists, m):
    NQ = NT // QT
    x_all, xn2T, weight, cst, gates, count = m.x_all, m.xn2T, m.weight, m.cst, m.gates, m.count
    xn2, slots, scattered, banks = m.xn2, m.slots, m.scattered, m.banks
    x_rows = a["x"].rearrange("b s d -> (b s) d")
    c_rows = a["ctx_1024"].rearrange("b s d -> (b s) d")
    pad_mask = a["mask_BxS2_ik0"]
    with ExitStack() as ctx:
        sb, sem = tools(nc, ctx)

        ident = cst[:, C_ID:C_ID + P]
        rev = cst[:, C_REV:C_REV + QT * E].rearrange("p (t e) -> p t e", t=QT)
        tri_bf = sb("tri_bf", [P, P], BF16)
        ones_bf = sb("ones_bf", [P, P], BF16)
        wq = sb("wq", [P, D])
        wk = sb("wk", [P, D])
        wv = sb("wv", [P, D])
        wo = sb("wo", [P, D])
        cols = sb("cols", [P, 8])
        bo_row = sb("bo_row", [P, D])
        bo_tmp = sb("bo_tmp", [P, D])
        bv_mat = sb("bv_mat", [P, P])
        rw = sb("rw", [P, 32])
        rb = sb("rb", [P, 1])
        srcm = sb("srcm", [P, S])
        ctx_in = sb("ctx_in", [P, 2, QW])
        pad_q = sb("pad_q", [P, 2, QT, S], I32)
        pad_k = sb("pad_k", [P, 2, QW], I32)
        keep = sb("keep", [P, QW])
        mask = sb("mask", [P, 2, QT, S])
        xn = sb("xn", [P, QW])
        xT = sb("xT", [P, QW])
        cT = sb("cT", [P, QW])
        kT = sb("kT", [P, QW])
        qg = sb("qg", [P, 2, NG, QW])
        kbd = sb("kbd", [P, 2, QT * 2, HG, S])
        vb = sb("vb", [P, 2, QT, 2, 8 * VS])
        prob = sb("prob", [P, QT, H * S])
        PT = sb("PT", [P, 2, 8 * P])
        mx = sb("mx", [P, QT, H])
        sm = sb("sm", [P, QT, H])
        rsx = sb("rsx", [P, QT, D])
        rsT = sb("rsT", [P, 2, P])
        aT = sb("aT", [P, 2, P])
        st1 = sb("st1", [P, QT, 6])
        st2 = sb("st2", [P, QT, 6])
        mv = sb("mv", [P, 2 * QT, 2])
        ln_v = sb("ln_v", [P, 2 * QT])
        ln_i = sb("ln_i", [P, 2 * QT], I32)
        ln_a = sb("ln_a", [P, 2 * QT])
        ln_b = sb("ln_b", [P, 2 * QT])
        ln_r = sb("ln_r", [P, 2 * QT])
        ln_s = sb("ln_s", [P, 2 * QT])
        x2T = sb("x2T", [P, 2, QW])
        LT = sb("LT", [P, P])
        lg = sb("lg", [P, QT, E])
        ra = sb("ra", [P, 4, QT, E])
        r_m = sb("r_m", [P, 6, QT])
        oh = sb("oh", [P, 2, QT, E])
        oh_bf = sb("oh_bf", [P, QT, E], BF16)
        posn = sb("posn", [P, QT, E])
        rt = sb("rt", [P, 2, QT, E])
        slotf = sb("slotf", [P, QT, 2])
        tokf = sb("tokf", [P, NT])

        sc_ps, pt_ps = banks[0:2], banks[2:4]
        fa_ps, fb_ps, att_ps, out_ps = banks[4:8]

        const_in = sem("const_in")
        setup_pool = sem("setup_pool")
        setup_act = sem("setup_act")
        setup_pe = sem("setup_pe")
        setup_dve = sem("setup_dve")
        quad_in = [sem(f"quad_in{i}") for i in range(2)]
        stats1 = sem("stats1")
        stats2 = sem("stats2")
        ln_step = sem("ln_step")
        xn_ready = sem("xn_ready")
        xT_done, xT_ready = sem("xT_done"), sem("xT_ready")
        cT_done, cT_ready = sem("cT_done"), sem("cT_ready")
        q_done, q_ready = sem("q_done"), sem("q_ready")
        k_done, kT_ready, k_ready = sem("k_done"), sem("kT_ready"), sem("k_ready")
        v_done, v_ready = sem("v_done"), sem("v_ready")
        keep_ready, mask_tmp, mask_ready, xb_ready = sem("keep_ready"), sem("mask_tmp"), sem("mask_ready"), sem("xb_ready")
        scores_done, masked, maxed, subbed, exped = (sem(n) for n in ("scores_done", "masked", "maxed", "subbed", "exped"))
        summed, recips, rs_ready = sem("summed"), sem("recips"), sem("rs_ready")
        turned, PT_ready, att_done, rsT_ready, aT_ready = (sem(n) for n in ("turned", "PT_ready", "att_done", "rsT_ready", "aT_ready"))
        wo_done, x2_ready = sem("wo_done"), sem("x2_ready")
        xn2_ready, x2T_done, x2T_ready = sem("xn2_ready"), sem("x2T_done"), sem("x2T_ready")
        lg_done, LT_ready, lgT_done, lg_copied = (sem(n) for n in ("lg_done", "LT_ready", "lgT_done", "lg_copied"))
        ra_step, p2_ready, pref_done, pref_copied, rb_step = (sem(n) for n in ("ra_step", "p2_ready", "pref_done", "pref_copied", "rb_step"))
        x2T_kept = [sem(f"x2T_kept{i}") for i in range(2)]
        passed = sem("a_passed")

        def need(eng, s, item, per=1, k=None, total=NT, apart=False):
            k = per if k is None else k
            if isinstance(item, int):
                if item < 0:
                    return
                if item >= total:
                    item, k = total - 1, per
            if apart and not isinstance(item, int):
                wait_alone(eng, s, item * per + k, passed)
            else:
                eng.wait_ge(s, item * per + k)

        def exists(item, total):
            return not isinstance(item, int) or 0 <= item < total

        def loop(eng, step, first, last):
            lo, hi = 2, NQ // 2 - 1
            for j in range(first, min(lo, last)):
                step(j)
            if hi > lo:
                with eng.Fori(lo, hi) as j:
                    step(j)
            for j in range(max(hi, lo), last):
                step(j)

        J0, J1 = -1, NQ // 2 + 2

        def cols_of(t, n=1):
            return bass.ds(t * D, n * D)

        block = ctx.enter_context(nc.Block())

        @block.sync
        def _(sp):
            sp.dma_start(cst[:, :], a["consts"]).then_inc(const_in, 16)
            for t, n in ((wq, "WqT"), (wk, "WkT"), (wv, "WvT"), (wo, "WoT")):
                sp.dma_start(t[:, :], a[n]).then_inc(const_in, 16)
            for i, n in enumerate(("bq", "bk", "bv")):
                sp.dma_start(cols[:, i:i + 1], a[n].unsqueeze(1)).then_inc(const_in, 16)
            sp.dma_start(bo_tmp[:, :], a["bo"].unsqueeze(0).broadcast_to([P, D])).then_inc(const_in, 16)
            for b in range(2):
                sp.dma_start(srcm[b * S:(b + 1) * S, :], a["src_mask"]).then_inc(const_in, 16)
            sp.dma_start(gates[:, 0:1], a["g_xattn"].unsqueeze(0).broadcast_to([P, 1])).then_inc(const_in, 16)
            sp.dma_start(gates[:, 1:2], a["g_ffn"].unsqueeze(0).broadcast_to([P, 1])).then_inc(const_in, 16)
            sp.dma_start(gates[:, 2:3], a["shared_weight"].unsqueeze(0).broadcast_to([P, 1])).then_inc(const_in, 16)
            sp.wait_ge(setup_pool, 2)
            sp.dma_start(rw[:, 0:E], a["router_w"]).then_inc(const_in, 16)
            for t in range(QT):
                sp.dma_start(rb[32 * t:32 * t + E, :], a["router_b"].unsqueeze(1)).then_inc(const_in, 16)

            def load(q, par):
                need(sp, cT_done, q - 2, total=NQ)
                need(sp, mask_ready, q - 2, total=NQ)
                need(sp, keep_ready, q - 2, total=NQ)
                rows = bass.ds(q * QW, QW)
                done = quad_in[par]
                sp.dma_start(x_all[:, cols_of(q * QT, QT)].rearrange("p (t d) -> p t d", t=QT),
                             x_rows[rows, :].rearrange("(t p) d -> p t d", p=P)).then_inc(done, 16)
                sp.dma_start(ctx_in[:, par, :].rearrange("p (t d) -> p t d", t=QT),
                             c_rows[rows, :].rearrange("(t p) d -> p t d", p=P)).then_inc(done, 16)
                pads = pad_mask[bass.ds(q * 2 * QT, 2 * QT), :]
                for b in range(2):
                    src = pads.rearrange("(t b) k -> b t k", b=2)[b:b + 1].broadcast_to([S, QT, S])
                    sp.dma_start(pad_q[b * S:(b + 1) * S, par], src).then_inc(done, 16)
                sp.dma_start(pad_k[:, par].rearrange("p (b k) -> p b k", k=S),
                             pads.unsqueeze(0).broadcast_to([P, 2 * QT, S])).then_inc(done, 16)

            load(0, 0)
            load(1, 1)
            if NQ // 2 > 1:
                with sp.Fori(1, NQ // 2) as j:
                    load(j * 2, 0)
                    load(j * 2 + 1, 1)
            sp.dma_start(m.sw1[:, :], a["sw1"]).then_inc(m.shared_in, 16)
            for i, n in enumerate(("sgate", "sb1")):
                sp.dma_start(m.scols[:, i, :], a[n]).then_inc(m.shared_in, 16)
            sp.dma_start(m.sw2[:, :, :], a["sw2"].rearrange("(c f) d -> f c d", f=P)).then_inc(m.shared_in, 16)
            sp.dma_start(m.sb2_row[:, :], a["sb2"].unsqueeze(0).broadcast_to([P, D])).then_inc(m.shared_in, 16)

        LOADS = 5
        CONSTS = 16 * (1 + 4 + 3 + 1 + 2 + 3 + 1 + QT)

        def quad_loaded(eng, j, par, dq, apart=False):
            p2, j2 = (par + dq) % 2, j + (par + dq) // 2
            need(eng, quad_in[p2], j2, per=16 * LOADS, total=NQ // 2, apart=apart)
            return p2

        @block.tensor
        def _(pe):
            pe.wait_ge(const_in, CONSTS)
            pe.wait_ge(setup_dve, 4)
            pe.matmul(att_ps[:, 0:D], bv_mat[:, :], wo[:, :], start=True, stop=True).then_inc(setup_pe, 1)
            pe.wait_ge(setup_dve, 5)
            pe.wait_ge(setup_pool, 5)

            def scores(n, u, par, q, h):
                if u == 0 and h == 0:
                    need(pe, q_ready, q, per=NG, total=NQ)
                    need(pe, k_ready, q, per=HG, total=NQ)
                need(pe, masked, n - 1, per=2, k=h + 1)
                for g in (2 * h, 2 * h + 1):
                    for b in range(2):
                        i = pe.matmul(sc_ps[h][b * S:(b + 1) * S, (g % 2) * 256:(g % 2) * 256 + 256],
                                      qg[:, par, g, u * P + b * S:u * P + (b + 1) * S],
                                      kbd[:, par, 2 * u + b].rearrange("p j k -> p (j k)"), start=True, stop=True)
                i.then_inc(scores_done, 1)

            def turn(n, u):
                need(pe, exped, n)
                for h in range(2):
                    need(pe, PT_ready, n - 1, per=2, k=h + 1)
                    for i in range(4):
                        p = 4 * h + i
                        t = pe.transpose(pt_ps[h][:, i * P:(i + 1) * P], prob[:, u, p * P:(p + 1) * P], ident)
                    t.then_inc(turned, 1)

            def project_out(n, u):
                need(pe, aT_ready, n)
                need(pe, x2_ready, n - 1)
                pe.matmul(out_ps[:, 0:D], aT[:, u % 2, :], wo[:, :], start=True, stop=True).then_inc(wo_done, 1)

            def step(j):
                for v in range(2 * QT):
                    par, u = v // QT, v % QT
                    q = j * 2 + par
                    n = j * 2 * QT + v
                    for h in range(2):
                        if exists(n, NT):
                            scores(n, u, par, q, h)
                        if h == 0 and u == 3 and exists(q - 2, NQ):
                            need(pe, LT_ready, q - 2, total=NQ)
                            pe.transpose(fb_ps[:, 0:P], LT[:, :], ident).then_inc(lgT_done, 1)
                    if u == 0 and exists(q + 1, NQ):
                        need(pe, xn_ready, q + 1, per=QT, total=NQ)
                        need(pe, v_ready, q, per=4, total=NQ)
                        for t in range(QT):
                            i = pe.transpose(fa_ps[:, t * P:(t + 1) * P], xn[:, t * P:(t + 1) * P], ident)
                        i.then_inc(xT_done, 1)
                    if u == 1 and exists(q + 1, NQ):
                        need(pe, xT_ready, q + 1, total=NQ)
                        pe.matmul(fa_ps[:, :], wq[:, :], xT[:, :], start=True, stop=True).then_inc(q_done, 1)
                    if u == 2 and exists(q - 2, NQ):
                        need(pe, xn2_ready, q - 2, per=QT, total=NQ)
                        need(pe, q_ready, q + 1, per=NG, total=NQ)
                        for t in range(QT):
                            i = pe.transpose(fa_ps[:, t * P:(t + 1) * P], xn2[:, par, t, 0:D], ident)
                        i.then_inc(x2T_done, 1)
                    if u == 3 and exists(q + 1, NQ):
                        need(pe, cT_ready, q + 1, total=NQ)
                        need(pe, q_ready, q + 1, per=NG, total=NQ)
                        need(pe, x2T_ready, q - 2, total=NQ)
                        for t in range(QT):
                            i = pe.matmul(fa_ps[:, t * P:(t + 1) * P], cT[:, t * P:(t + 1) * P], wv[:, :],
                                          start=True, stop=True)
                        i.then_inc(v_done, 1)
                    if exists(n - 2, NT):
                        turn(n - 2, (u - 2) % QT)
                    if u == 0 and exists(q - 3, NQ):
                        need(pe, ra_step, q - 3, per=RA_STEPS, total=NQ)
                        need(pe, x2_ready, n - 5)
                        pre = out_ps[:, P:P + QT * E]
                        pe.matmul(pre, tri_bf[:, :], oh_bf[:, :, :].rearrange("p t e -> p (t e)"),
                                  start=True, stop=False, skip_group_check=True)
                        for t in range(QT):
                            for t2 in range(t + 1, QT + 1):
                                i = pe.matmul(out_ps[:, P + t2 * E:P + (t2 + 1) * E], ones_bf[:, :],
                                              oh_bf[:, t, :], start=False, stop=(t == QT - 1),
                                              skip_group_check=True)
                        i.then_inc(pref_done, 1)
                    if exists(n - 4, NT):
                        if u == 1:
                            need(pe, pref_copied, q - 3, per=2, total=NQ)
                        project_out(n - 4, u)
                    if u == 0 and exists(q + 1, NQ):
                        p2 = quad_loaded(pe, j, par, 1)
                        need(pe, lg_copied, q - 3, total=NQ)
                        for t in range(QT):
                            i = pe.transpose(fb_ps[:, t * P:(t + 1) * P], ctx_in[:, p2, t * P:(t + 1) * P], ident)
                        i.then_inc(cT_done, 1)
                    if u == 1 and exists(q + 1, NQ):
                        need(pe, cT_ready, q + 1, total=NQ)
                        pe.matmul(fb_ps[:, :], wk[:, :], cT[:, :], start=True, stop=True).then_inc(k_done, 1)
                    if exists(n - 3, NT):
                        if u == 3:
                            need(pe, v_ready, q, per=4, total=NQ)
                        values(n - 3, (u - 3) % QT, par if u == 3 else 1 - par)
                    if u == 2 and exists(q - 2, NQ):
                        need(pe, x2T_ready, q - 2, total=NQ)
                        need(pe, kT_ready, q + 1, total=NQ)
                        for t in range(QT):
                            i = pe.matmul(fb_ps[32 * t:32 * t + 32, 0:P], rw[:, :],
                                          x2T[:, par, t * P:(t + 1) * P], start=True, stop=True)
                        i.then_inc(lg_done, 1)

            def values(n, u, par):
                need(pe, PT_ready, n, per=2)
                need(pe, aT_ready, n - 1)
                for b in range(2):
                    for c in range(2):
                        for g in range(NG):
                            p = 2 * g + c
                            pe.matmul(att_ps[32 * g:32 * g + 32, b * S:(b + 1) * S],
                                      vb[:, par, u, b, 16 + VS * p - 16 * c:16 + VS * p - 16 * c + 32],
                                      PT[:, u % 2, p * P + b * S:p * P + (b + 1) * S],
                                      start=(c == 0), stop=(c == 1))
                need(pe, rs_ready, n)
                pe.transpose(att_ps[:, P:2 * P], rsx[:, u, :], ident).then_inc(att_done, 1)

            loop(pe, step, J0, J1)

        @block.vector
        def _(ve):
            ve.wait_ge(const_in, CONSTS)
            ve.tensor_copy(tri_bf[:, :], cst[:, C_TRI:C_TRI + P]).then_inc(setup_dve, 1)
            ve.tensor_copy(count[:, :], cst[:, C_BASE:C_BASE + E]).then_inc(setup_dve, 1)
            ve.tensor_scalar(cols[:, 3:4], cols[:, 0:1], float(DK) ** -0.5, None, ALU.mult).then_inc(setup_dve, 1)
            ve.tensor_copy(bv_mat[:, :], cols[:, 2:3].broadcast_to([P, P])).then_inc(setup_dve, 1)
            ve.wait_ge(setup_pe, 1)
            ve.wait_ge(setup_act, 1)
            ve.tensor_tensor(bo_tmp[:, :], att_ps[:, 0:D], bo_tmp[:, :], ALU.add).then_inc(setup_dve, 1)
            ve.wait_ge(setup_dve, 5)
            ve.tensor_scalar(bo_row[:, :], bo_tmp[:, :], gates[:, 0:1], None, ALU.mult).then_inc(setup_dve, 1)
            ve.memset(mv[:, :, :], 1.0).then_inc(setup_dve, 1)
            ve.memset(st1[:, :, :], 1.0).then_inc(setup_dve, 1)
            ve.memset(st2[:, :, :], 1.0).then_inc(setup_dve, 1)
            for t in range(NT):
                ve.tensor_scalar(tokf[:, t:t + 1], cst[:, C_PART:C_PART + 1], float(t * P), None,
                                 ALU.add).then_inc(setup_dve, 1)
            ve.wait_ge(setup_act, 2)
            ve.wait_ge(setup_dve, 9 + NT)
            ve.tensor_scalar(gates[:, 2:3], gates[:, 2:3], 1.0, None, ALU.add).then_inc(setup_dve, 1)
            ve.wait_ge(setup_dve, 10 + NT)
            ve.reciprocal(gates[:, 2:3], gates[:, 2:3]).then_inc(setup_dve, 1)

            def chain(s, base, per):
                k = [0]

                def then(ins):
                    k[0] += 1
                    ins.then_inc(s, 1)
                    ve.wait_ge(s, base * per + k[0])
                    assert k[0] <= per
                return then

            def sums(n, u):
                need(ve, exped, n)
                ve.tensor_reduce(sm[:, u, :], prob[:, u, :].rearrange("p (h k) -> p h k", k=S),
                                 X, ALU.add).then_inc(summed, 1)

            def sums_inverse(n, u):
                need(ve, summed, n)
                ve.reciprocal(sm[:, u, :], sm[:, u, :]).then_inc(recips, 1)

            def sums_spread(n, u):
                need(ve, recips, n)
                need(ve, att_done, n - QT)
                ve.tensor_copy(rsx[:, u, :].rearrange("p (h d) -> p h d", d=DK),
                               sm[:, u, :].unsqueeze(2).broadcast_to([P, H, DK])).then_inc(rs_ready, 1)

            def normalise(n, u):
                need(ve, rsT_ready, n)
                need(ve, wo_done, n - 2)
                ve.tensor_tensor(aT[:, u % 2, :], att_ps[:, 0:P], rsT[:, u % 2, :], ALU.mult).then_inc(aT_ready, 1)

            def add_mask(n, u, par, q, h):
                if h == 0:
                    need(ve, turned, n - QT, per=2)
                    need(ve, mask_ready, q, total=NQ)
                need(ve, scores_done, n, per=2, k=h + 1)
                ve.tensor_tensor(prob[:, u, h * 512:(h + 1) * 512].rearrange("p (h k) -> p h k", k=S),
                                 sc_ps[h][:, :].rearrange("p (h k) -> p h k", k=S),
                                 mask[:, par, u, :].unsqueeze(1).broadcast_to([P, H // 2, S]),
                                 ALU.add).then_inc(masked, 1)

            def maxima(n, u):
                need(ve, masked, n, per=2)
                ve.tensor_reduce(mx[:, u, :], prob[:, u, :].rearrange("p (h k) -> p h k", k=S),
                                 X, ALU.max).then_inc(maxed, 1)

            def add_out(n, u, q):
                need(ve, wo_done, n)
                need(ve, xb_ready, q, total=NQ)
                xs = x_all[:, cols_of(n)]
                ve.scalar_tensor_tensor(out=xs, in0=out_ps[:, 0:D], scalar=gates[:, 0:1], in1=xs,
                                        op0=ALU.mult, op1=ALU.add).then_inc(x2_ready, 1)

            def out_stats(n, u):
                need(ve, x2_ready, n, apart=True)
                ve.bn_stats(st2[:, u, :], x_all[:, cols_of(n)]).then_inc(stats2, 1)

            def norms(i, j, par, q):
                if i > 1:
                    need(ve, ln_step, q + 2, per=LN_STEPS, k=i - 1, total=NQ + 4)
                if i == 0:
                    if exists(q + 2, NQ):
                        quad_loaded(ve, j, par, 2, apart=True)
                        for t in range(QT):
                            ve.bn_stats(st1[:, t, :], x_all[:, cols_of((q + 2) * QT + t)]).then_inc(stats1, 1)
                    return
                if i == 1:
                    need(ve, stats1, q + 2, per=QT, total=NQ)
                    need(ve, stats2, q - 2, per=QT, total=NQ)
                    need(ve, xn2_ready, q - 3, per=QT, total=NQ)
                    need(ve, xn_ready, q + 1, per=QT, total=NQ, apart=True)
                    for t in range(QT):
                        ve.bn_aggr(mv[:, t, :], st1[:, t, :])
                        ins = ve.bn_aggr(mv[:, QT + t, :], st2[:, t, :])
                elif i == 2:
                    ins = ve.tensor_scalar(ln_v[:, :], mv[:, :, 1], EPS, None, ALU.add)
                elif i == 3:
                    ins = ve.tensor_scalar(ln_i[:, :], ln_v[:, :].bitcast(I32), 1, None, ALU.logical_shift_right)
                elif i == 4:
                    ins = ve.tensor_scalar(ln_r[:, :].bitcast(I32), ln_i[:, :], -1.0, RSQRT_MAGIC, ALU.mult, ALU.add)
                elif i in (5, 8, 11):
                    ins = ve.tensor_tensor(ln_a[:, :], ln_r[:, :], ln_r[:, :], ALU.mult)
                elif i in (6, 9, 12):
                    ins = ve.scalar_tensor_tensor(out=ln_b[:, :], in0=ln_a[:, :], scalar=-0.5, in1=ln_v[:, :],
                                                  op0=ALU.mult, op1=ALU.mult)
                elif i in (7, 10, 13):
                    ins = ve.scalar_tensor_tensor(out=ln_r[:, :], in0=ln_b[:, :], scalar=1.5, in1=ln_r[:, :],
                                                  op0=ALU.add, op1=ALU.mult)
                else:
                    ins = ve.scalar_tensor_tensor(out=ln_s[:, :], in0=mv[:, :, 0], scalar=-1.0, in1=ln_r[:, :],
                                                  op0=ALU.mult, op1=ALU.mult)
                ins.then_inc(ln_step, 1)

            def wide(t):
                return t.unsqueeze(2).broadcast_to([P, QT, E])

            def route_a(i, q):
                d1, c1, d2, c2 = (ra[:, k] for k in range(4))
                m1, f1, m2, f2 = (r_m[:, k] for k in range(4))
                if i == 0:
                    need(ve, lgT_done, q, total=NQ)
                    ve.tensor_copy(lg[:, :, :], fb_ps[:, 0:P].rearrange("p (t e) -> p t e", t=QT)[:, :, 0:E])\
                        .then_inc(lg_copied, 1)
                    return
                if i == 1:
                    need(ve, lg_copied, q, total=NQ)
                    ins = ve.tensor_reduce(m1, lg[:, :, :], X, ALU.max)
                else:
                    need(ve, ra_step, q, per=RA_STEPS, k=i - 1, total=NQ)
                if i == 2:
                    ins = ve.tensor_tensor(d1, lg[:, :, :], wide(m1), ALU.subtract)
                elif i == 3:
                    ins = ve.scalar_tensor_tensor(out=c1, in0=d1, scalar=0.0, in1=rev, op0=ALU.is_equal, op1=ALU.mult)
                elif i == 4:
                    ins = ve.tensor_reduce(f1, c1, X, ALU.max)
                elif i == 5:
                    ins = ve.tensor_tensor(oh[:, 0], rev, wide(f1), ALU.is_equal)
                elif i == 6:
                    ins = ve.scalar_tensor_tensor(out=d2, in0=oh[:, 0], scalar=-3.0e38, in1=d1, op0=ALU.mult,
                                                  op1=ALU.add)
                elif i == 7:
                    ins = ve.tensor_reduce(m2, d2, X, ALU.max)
                elif i == 8:
                    ins = ve.tensor_tensor(c2, d2, wide(m2), ALU.is_equal)
                elif i == 9:
                    ins = ve.tensor_tensor(c2, c2, rev, ALU.mult)
                elif i == 10:
                    ins = ve.tensor_reduce(f2, c2, X, ALU.max)
                elif i == 11:
                    ins = ve.tensor_tensor(oh[:, 1], rev, wide(f2), ALU.is_equal)
                elif i == 12:
                    ins = ve.tensor_tensor(oh_bf[:, :, :], oh[:, 0], oh[:, 1], ALU.add)
                ins.then_inc(ra_step, 1)

            def route_b(i, q, par):
                p2, s2 = r_m[:, 4], r_m[:, 5]
                tiles = bass.ds(q * QT, QT)
                if i == 0:
                    need(ve, p2_ready, q, total=NQ)
                    need(ve, pref_done, q, total=NQ)
                    pre = out_ps[:, P:P + QT * E].rearrange("p (t e) -> p t e", t=QT)
                    ve.tensor_tensor(posn[:, :, :], pre, count[:, :].unsqueeze(1).broadcast_to([P, QT, E]), ALU.add)\
                        .then_inc(pref_copied, 1)
                elif i == 1:
                    ve.tensor_scalar(s2, p2, 1.0, None, ALU.add).then_inc(rb_step, 1)
                elif i == 2:
                    need(ve, pref_copied, q, per=2, k=1, total=NQ)
                    ve.tensor_tensor(count[:, :], out_ps[:, P + QT * E:P + (QT + 1) * E], count[:, :],
                                     ALU.add).then_inc(pref_copied, 1)
                elif i == 3:
                    need(ve, rb_step, q, per=RB_STEPS, k=1, total=NQ)
                    ve.reciprocal(s2, s2).then_inc(rb_step, 1)
                elif i == 4:
                    ve.tensor_tensor(rt[:, 0], oh[:, 0], posn[:, :, :], ALU.mult)
                    ve.tensor_tensor(rt[:, 1], oh[:, 1], posn[:, :, :], ALU.mult).then_inc(rb_step, 1)
                elif i == 5:
                    need(ve, rb_step, q, per=RB_STEPS, k=2, total=NQ)
                    ve.tensor_copy(weight[:, tiles, 0], s2)
                    ve.tensor_tensor(weight[:, tiles, 1], p2, s2, ALU.mult)
                    need(ve, rb_step, q, per=RB_STEPS, k=3, total=NQ)
                    ve.tensor_reduce(slotf[:, :, 0], rt[:, 0], X, ALU.add)
                    ve.tensor_reduce(slotf[:, :, 1], rt[:, 1], X, ALU.add).then_inc(rb_step, 1)
                elif i == 6:
                    need(ve, xn2_ready, q, per=QT, total=NQ)
                    ve.tensor_scalar(xn2[:, par, :, D], r_m[:, 1], -1.0, float(E), ALU.mult, ALU.add)
                    ve.tensor_copy(xn2[:, par, :, D + 1], tokf[:, tiles])
                else:
                    need(ve, rb_step, q, per=RB_STEPS, k=4, total=NQ)
                    ve.tensor_copy(slots[:, par], slotf[:, :, :]).then_inc(rb_step, 1)

            def keys(q):
                need(ve, k_done, q, total=NQ)
                need(ve, keep_ready, q, total=NQ)
                need(ve, k_ready, q - 1, per=HG, total=NQ)
                ve.scalar_tensor_tensor(out=kT[:, :], in0=fb_ps[:, :], scalar=cols[:, 1:2], in1=keep[:, :],
                                        op0=ALU.add, op1=ALU.mult).then_inc(kT_ready, 1)

            NORMS_AT = ((0, 1), (2, 3), (4, 5), (6, 7), (8, 9), (10, 11), (12, 13), (14,))
            ROUTE_A_AT = ((0,), (1, 2), (3, 4), (5,), (6, 7), (8, 9), (10, 11), (12,))

            def between(place, j, u, par, q):
                if u == 0 and (not isinstance(q, int) or -2 <= q <= NQ + 1):
                    for i in NORMS_AT[place]:
                        norms(i, j, par, q)
                if u == 1 and exists(q - 3, NQ):
                    route_b(place, q - 3, 1 - par)
                if u == 2 and place == 0 and exists(q + 1, NQ):
                    keys(q + 1)
                if u == 3 and exists(q - 2, NQ):
                    for i in ROUTE_A_AT[place]:
                        route_a(i, q - 2)

            def step(j):
                for v in range(2 * QT):
                    par, u = v // QT, v % QT
                    q = j * 2 + par
                    n = j * 2 * QT + v
                    place = (j, u, par, q)
                    if exists(n - 2, NT):
                        sums(n - 2, (u - 2) % QT)
                    between(0, *place)
                    if exists(n - 2, NT):
                        sums_inverse(n - 2, (u - 2) % QT)
                    between(1, *place)
                    if exists(n - 2, NT):
                        sums_spread(n - 2, (u - 2) % QT)
                    between(2, *place)
                    if exists(n - 4, NT):
                        normalise(n - 4, u)
                    between(3, *place)
                    if exists(n, NT):
                        add_mask(n, u, par, q, 0)
                    between(4, *place)
                    if exists(n, NT):
                        add_mask(n, u, par, q, 1)
                    between(5, *place)
                    if exists(n, NT):
                        maxima(n, u)
                    between(6, *place)
                    if exists(n - 4, NT):
                        add_out(n - 4, u, q - 1)
                    between(7, *place)
                    if exists(n - 4, NT):
                        out_stats(n - 4, u)

            loop(ve, step, J0, J1)

        @block.scalar
        def _(ac):
            ac.wait_ge(const_in, CONSTS)
            ac.activation(gates[:, 0:2], gates[:, 0:2], ACT.Tanh).then_inc(setup_act, 1)
            ac.activation(gates[:, 2:3], gates[:, 2:3], ACT.Exp, scale=-1.0).then_inc(setup_act, 1)
            ac.wait_ge(setup_dve, 9)
            ac.wait_ge(setup_pool, 5)

            def step(j):
                for v in range(2 * QT):
                    par, u = v // QT, v % QT
                    q = j * 2 + par
                    n = j * 2 * QT + v
                    if exists(n - 4, NT):
                        need(ac, att_done, n - 4)
                        ac.activation(rsT[:, u % 2, :], att_ps[:, P:2 * P], ACT.Copy).then_inc(rsT_ready, 1)
                    if u == 0 and exists(q - 3, NQ):
                        need(ac, ra_step, q - 3, per=RA_STEPS, total=NQ)
                        ac.activation(r_m[:, 4], r_m[:, 2], ACT.Exp).then_inc(p2_ready, 1)
                    if u == 0 and exists(q + 1, NQ):
                        need(ac, xT_done, q + 1, total=NQ)
                        ac.activation(xT[:, :], fa_ps[:, :], ACT.Copy).then_inc(xT_ready, 1)
                    if u == 2 and exists(q - 2, NQ):
                        need(ac, x2T_done, q - 2, total=NQ)
                        need(ac, x2T_kept[par], j - 2, per=16, total=NQ // 2)
                        ac.activation(x2T[:, par, :], fa_ps[:, :], ACT.Copy).then_inc(x2T_ready, 1)
                    if exists(n - 2, NT):
                        for h in range(2):
                            need(ac, turned, n - 2, per=2, k=h + 1)
                            ac.activation(PT[:, u % 2, h * 512:(h + 1) * 512], pt_ps[h][:, :], ACT.Copy)\
                                .then_inc(PT_ready, 1)
                    if exists(n - 1, NT):
                        need(ac, subbed, n - 1)
                        ps = prob[:, (u - 1) % QT, :]
                        ac.activation(ps, ps, ACT.Exp).then_inc(exped, 1)
                    if u == 0 and exists(q + 1, NQ):
                        need(ac, cT_done, q + 1, total=NQ)
                        ac.activation(cT[:, :], fb_ps[:, :], ACT.Copy).then_inc(cT_ready, 1)
                    if u == 1 and exists(q - 2, NQ):
                        need(ac, ln_step, q + 2, per=LN_STEPS, total=NQ + 4)
                        need(ac, scattered[par], j - 2, per=16 * 2 * QT, total=NQ // 2)
                        for t in range(QT):
                            ac.activation(xn2[:, par, t, 0:D], x_all[:, cols_of((q - 2) * QT + t)], ACT.Identity,
                                          bias=ln_s[:, QT + t:QT + t + 1], scale=ln_r[:, QT + t:QT + t + 1])\
                              .then_inc(xn2_ready, 1)
                    if u == 1 and exists(q + 1, NQ):
                        need(ac, q_done, q + 1, total=NQ)
                        for g in range(NG):
                            r = slice(32 * g, 32 * g + 32)
                            ac.activation(qg[r, 1 - par, g, :], fa_ps[r, :], ACT.Identity, bias=cols[r, 3:4],
                                          scale=float(DK) ** -0.5).then_inc(q_ready, 1)
                    if u == 2 and exists(q - 2, NQ):
                        need(ac, lg_done, q - 2, total=NQ)
                        ac.activation(LT[:, :], fb_ps[:, 0:P], ACT.Identity, bias=rb[:, 0:1]).then_inc(LT_ready, 1)
                        ac.dma_start(xn2T[:, cols_of((q - 2) * QT, QT)], x2T[:, par, :]).then_inc(x2T_kept[par], 16)
                    if u == 2 and exists(q + 1, NQ):
                        need(ac, kT_ready, q + 1, total=NQ)
                        for i in range(HG):
                            dst = kbd[:, 1 - par, :, i, :]
                            ac.activation(dst, kT[:, :].rearrange("p (b k) -> p b k", k=S), ACT.Copy,
                                          scale=cst[:, C_JM + i:C_JM + i + 1]).then_inc(k_ready, 1)
                    if u == 3 and exists(q + 1, NQ):
                        need(ac, v_done, q + 1, total=NQ)
                        for b in range(2):
                            for c in range(2):
                                src = fa_ps[b * S:(b + 1) * S, :].rearrange("k (t p c d) -> k t p c d", t=QT, c=2, d=DK)
                                dst = vb[c * S:(c + 1) * S, 1 - par, :, b, :].rearrange("k t (p m) -> k t p m", m=VS)
                                src, dst = src[:, :, :, c, :], dst[:, :, :, 16 + DK * c:16 + DK * c + DK]
                                ac.activation(dst, src, ACT.Copy).then_inc(v_ready, 1)
                    if u == 3 and exists(q + 2, NQ):
                        need(ac, ln_step, q + 2, per=LN_STEPS, total=NQ + 4)
                        need(ac, xT_done, q + 1, total=NQ)
                        for t in range(QT):
                            ac.activation(xn[:, t * P:(t + 1) * P], x_all[:, cols_of((q + 2) * QT + t)], ACT.Identity,
                                          bias=ln_s[:, t:t + 1], scale=ln_r[:, t:t + 1]).then_inc(xn_ready, 1)

            loop(ac, step, J0, J1)
            for i in range(2):
                ac.wait_ge(x2T_kept[i], 16 * (NQ // 2))

        @block.gpsimd
        def _(po):
            po.memset(rw[:, :], 0.0).then_inc(setup_pool, 1)
            po.memset(rb[:, :], 0.0).then_inc(setup_pool, 1)
            po.memset(qg[:, :, :, :], 0.0).then_inc(setup_pool, 1)
            po.memset(vb[:, :, :, :, :], 0.0).then_inc(setup_pool, 1)
            po.memset(ones_bf[:, :], 1.0).then_inc(setup_pool, 1)
            po.wait_ge(const_in, CONSTS)
            po.wait_ge(setup_dve, 9 + NT)

            def scatter(q, par, which):
                need(po, rb_step, q, per=RB_STEPS, total=NQ, apart=True)
                scatter_rows(po, lists, m, par, which)

            def step(j):
                for v in range(2 * QT):
                    par, u = v // QT, v % QT
                    q = j * 2 + par
                    n = j * 2 * QT + v
                    if exists(n, NT):
                        need(po, maxed, n)
                        ps = prob[:, u, :].rearrange("p (h k) -> p h k", k=S)
                        po.tensor_tensor(ps, ps, mx[:, u, :].unsqueeze(2).broadcast_to([P, H, S]),
                                         ALU.subtract).then_inc(subbed, 1)
                    if u == 0 and exists(q + 1, NQ):
                        p2 = quad_loaded(po, j, par, 1)
                        need(po, kT_ready, q, total=NQ, apart=True)
                        po.tensor_scalar(keep[:, :], pad_k[:, p2, :], 0, 0.0, ALU.is_equal, ALU.is_equal).then_inc(keep_ready, 1)
                        po.tensor_scalar(mask[:, p2], pad_q[:, p2], 0, NEG, ALU.is_equal, ALU.mult).then_inc(mask_tmp, 1)
                        need(po, mask_tmp, q + 1, total=NQ)
                        po.tensor_tensor(mask[:, p2], mask[:, p2], srcm[:, :].unsqueeze(1).broadcast_to([P, QT, S]),
                                         ALU.add).then_inc(mask_ready, 1)
                        need(po, xn_ready, q + 1, per=QT, total=NQ, apart=True)
                        xs = x_all[:, cols_of((q + 1) * QT, QT)].rearrange("p (t d) -> p t d", t=QT)
                        po.tensor_tensor(xs, xs, bo_row[:, :].unsqueeze(1).broadcast_to([P, QT, D]),
                                         ALU.add).then_inc(xb_ready, 1)
                    if u == 1 and exists(q - 3, NQ - 2):
                        scatter(q - 3, 1 - par, range(0, 2))
                    if u == 2 and exists(q - 3, NQ - 2):
                        scatter(q - 3, 1 - par, range(2, 5))
                    if u == 3 and exists(q - 3, NQ - 2):
                        scatter(q - 3, 1 - par, range(5, 8))

            loop(po, step, J0, J1)


def experts(nc, a, NT, REGION, lists, results, m):
    TOK = NT * P
    NQ = NT // QT
    FC = F // P
    SC = FS // P
    HB = FC * SL // 512
    T = steps_listed(NT)
    xn2T, cst, gates, count, banks = m.xn2T, m.cst, m.gates, m.count, m.banks
    sw1, sw2, scols, sb2_row, shared_in = m.sw1, m.sw2, m.scols, m.sb2_row, m.shared_in
    with ExitStack() as ctx:
        sb, sem = tools(nc, ctx)
        hs = sb("hs", [P, 2, SC, QW])
        w1 = sb("w1", [P, E, F])
        w2 = sb("w2", [P, E, FC, D])
        gate_c = sb("gate_c", [P, FC, E])
        b1g_c = sb("b1g_c", [P, FC, E])
        b2_row = sb("b2_row", [P, E, D])
        pad_rows = sb("pad_rows", [P, E + 1, 2, ROW])
        tf = sb("tf", [P, 4, E])
        trips = sb("trips", [P, E], I32)
        ends = sb("ends", [P, E], I32)
        begun = sb("begun", [P, T, E])
        step_f = sb("step_f", [P, 2, T])
        expert_of = sb("expert_of", [P, T], I32)
        row_of = sb("row_of", [P, T], I32)
        pairs = sb("pairs", [P, 1], I32)
        rows = sb("rows", [P, 2, 2, ROW])
        meta = sb("meta", [P, 2, 2, 2])
        destf = sb("destf", [P, 2])
        dest = sb("dest", [P, 2, 2, 1], I32)
        rT = sb("rT", [P, 2, SL])
        w1_now = sb("w1_now", [P, 2, F])
        hT = sb("hT", [P, 2, FC, SL])
        y = sb("y", [P, 2, 2, D])

        sh_ps, sy_ps = [banks[0:2], banks[2:4]], banks[4:6]
        h_ps, y_ps, t_ps = [banks[0:2], banks[2:4]], banks[4:6], banks[6:8]

        biases_in, weights_in = sem("biases_in"), sem("weights_in")
        shared_scaled, biases_ready = sem("shared_scaled"), sem("biases_ready")
        sh_done, sh_gelued, sy_done, kept = (sem(n) for n in ("sh_done", "sh_gelued", "sy_done", "kept"))
        plan_step, pads_ready, pads_in, table_ready = (sem(n) for n in ("plan_step", "pads_ready", "pads_in", "table_ready"))
        rows_in = [sem(f"rows_in{i}") for i in range(2)]
        meta_read, turned, rT_ready = (sem(n) for n in ("meta_read", "rows_turned", "rT_ready"))
        h_done, gelued, y_done, y_ready = (sem(n) for n in ("h_done", "gelued", "y_done", "y_ready"))
        dest_step, w1_ready = sem("dest_step"), sem("w1_ready")
        sent = [sem(f"sent{i}") for i in range(2)]
        passed = sem("e_passed")

        def wait_apart(eng, s, value):
            wait_alone(eng, s, value, passed)

        def iterations(eng, body):
            n = eng.value_load(pairs[0:1, 0:1], min_val=TOK // SL, max_val=(T - 2) // 2)
            body(0, 0, 0)
            body(1, 1, 0)
            with eng.Fori(1, n) as i:
                body(i * 2, 0, i)
                body(i * 2 + 1, 1, i)

        def expert(eng, t):
            return eng.value_load(expert_of[0:1, bass.ds(t, 1)], min_val=0, max_val=E - 1)

        block = ctx.enter_context(nc.Block())

        @block.sync
        def _(sp):
            sp.dma_start(gate_c[:, :, :], a["gate"]).then_inc(biases_in, 16)
            sp.dma_start(b1g_c[:, :, :], a["b1"]).then_inc(biases_in, 16)
            sp.dma_start(b2_row[:, :, :], a["b2"].unsqueeze(0).broadcast_to([P, E, D])).then_inc(biases_in, 16)
            sp.wait_ge(table_ready, 1)
            sp.wait_ge(pads_ready, 2)
            for e in range(E):
                at = sp.value_load(ends[0:1, e:e + 1], min_val=e * REGION, max_val=e * REGION + TOK)
                sp.dma_start(lists[bass.ds(at, SL), :].rearrange("(t p) d -> p t d", p=P), pad_rows[:, e])\
                  .then_inc(pads_in, 16)
            for i in range(3):
                sp.dma_start(lists[E * REGION + i * SL:E * REGION + (i + 1) * SL, :]
                             .rearrange("(t p) d -> p t d", p=P), pad_rows[:, E]).then_inc(pads_in, 16)
            sp.wait_ge(pads_in, 16 * (E + 3))
            for i in range(2):
                sp.wait_ge(m.scattered[i], 16 * 2 * QT * (NQ // 2))

            def load(t, par, wait=True):
                at = sp.value_load(row_of[0:1, bass.ds(t, 1)], min_val=0, max_val=E * REGION + 2 * SL)
                if wait:
                    sp.wait_ge(turned, t - 1)
                    sp.wait_ge(meta_read, t - 1)
                sp.dma_start(rows[:, par], lists[bass.ds(at, SL), :].rearrange("(t p) d -> p t d", p=P))\
                  .then_inc(rows_in[par], 16)
            load(0, 0, False)
            load(1, 1, False)
            iterations(sp, lambda t, par, i: load(t + 2, par))
            n = sp.value_load(pairs[0:1, 0:1], min_val=TOK // SL, max_val=(T - 2) // 2)
            for i in range(2):
                wait_apart(sp, rows_in[i], n * 16 + 16)
                wait_apart(sp, sent[i], n * 32)

        @block.tensor
        def _(pe):
            ident = cst[:, C_ID:C_ID + P]

            def hidden(q, par):
                for c in range(SC):
                    if not isinstance(q, int) or q >= 2:
                        pe.wait_ge(sh_gelued, (q - 2) * SC + c + 1)
                    pe.matmul(sh_ps[par][c][:, :], sw1[:, c * P:(c + 1) * P], xn2T[:, bass.ds(q * QW, QW)],
                              start=True, stop=True).then_inc(sh_done, 1)

            def second(q, par):
                pe.wait_ge(sh_gelued, q * SC + SC)
                if not isinstance(q, int) or q >= 2:
                    pe.wait_ge(kept, q - 1)
                for t in range(QT):
                    for c in range(SC):
                        last = pe.matmul(sy_ps[par][:, t * D:(t + 1) * D], hs[:, par, c, t * P:(t + 1) * P],
                                      sw2[:, c, :], start=(c == 0), stop=(c == SC - 1))
                last.then_inc(sy_done, 1)

            pe.wait_ge(shared_in, 80)
            pe.wait_ge(shared_scaled, 3)
            hidden(0, 0)
            hidden(1, 1)
            second(0, 0)
            with pe.Fori(1, NQ // 2) as j:
                hidden(j * 2, 0)
                second(j * 2 - 1, 1)
                hidden(j * 2 + 1, 1)
                second(j * 2, 0)
            second(NQ - 1, 1)

            def turn(t, par, i):
                pe.wait_ge(rows_in[par], i * 16 + 16)
                if not isinstance(t, int) or t >= 2:
                    pe.wait_ge(rT_ready, t - 1)
                for h in range(2):
                    last = pe.transpose(t_ps[par][:, h * P:(h + 1) * P], rows[:, par, h, 0:D], ident)
                last.then_inc(turned, 1)

            def first_layer(t, par):
                pe.wait_ge(rT_ready, t + 1)
                pe.wait_ge(w1_ready, t + 1)
                if not isinstance(t, int) or t >= 2:
                    pe.wait_ge(gelued, (t - 1) * FC)
                for c in range(FC):
                    last = pe.matmul(h_ps[par][c // 2][:, (c % 2) * SL:(c % 2 + 1) * SL],
                                  w1_now[:, par, c * P:(c + 1) * P], rT[:, par, :], start=True, stop=True)
                    if c % 2:
                        last.then_inc(h_done, 1)

            def second_layer(t, par, e):
                if not isinstance(t, int) or t >= 2:
                    pe.wait_ge(y_ready, t - 1)
                for h in range(2):
                    for c in range(FC):
                        if h == 0:
                            pe.wait_ge(gelued, t * FC + c + 1)
                        last = pe.matmul(y_ps[par][:, h * D:(h + 1) * D], hT[:, par, c, h * P:(h + 1) * P],
                                      w2[:, bass.ds(e, 1), c, :].rearrange("p a d -> p (a d)"),
                                      start=(c == 0), stop=(c == FC - 1))
                last.then_inc(y_done, 1)

            pe.wait_ge(table_ready, 1)
            turn(0, 0, 0)
            pe.wait_ge(weights_in, 64)
            pe.wait_ge(sh_gelued, NQ * SC)
            pe.wait_ge(kept, NQ)
            first_layer(0, 0)
            turn(1, 1, 0)

            def body(t, par, i):
                first_layer(t + 1, 1 - par)
                turn(t + 2, par, i + 1)
                second_layer(t, par, expert(pe, t))
            iterations(pe, body)

        @block.scalar
        def _(ac):
            for k in range(2):
                es = slice(k * E // 2, (k + 1) * E // 2)
                ac.dma_start(w1[:, es, :], a["w1"][es].rearrange("e d f -> d e f")).then_inc(weights_in, 16)
                ac.dma_start(w2[:, es], a["w2"][es].rearrange("e (c f) d -> f e c d", f=P)).then_inc(weights_in, 16)
            ac.wait_ge(shared_scaled, 1)

            def shared_gelu(q, par):
                for c in range(SC):
                    if c == 0 and (not isinstance(q, int) or q >= 2):
                        ac.wait_ge(sy_done, q - 1)
                    ac.wait_ge(sh_done, q * SC + c + 1)
                    ac.activation(hs[:, par, c, :], sh_ps[par][c][:, :], ACT.Gelu, bias=scols[:, 2, c:c + 1],
                                  scale=scols[:, 0, c:c + 1]).then_inc(sh_gelued, 1)
            shared_gelu(0, 0)
            shared_gelu(1, 1)
            with ac.Fori(1, NQ // 2) as j:
                shared_gelu(j * 2, 0)
                shared_gelu(j * 2 + 1, 1)

            ac.wait_ge(biases_ready, 1)
            ac.wait_ge(table_ready, 1)

            def body(t, par, i):
                e = expert(ac, t)
                if not isinstance(t, int) or t >= 2:
                    ac.wait_ge(y_done, t - 1)
                for c in range(FC):
                    if c % 2 == 0:
                        ac.wait_ge(h_done, t * HB + c // 2 + 1)
                    ac.activation(hT[:, par, c, :], h_ps[par][c // 2][:, (c % 2) * SL:(c % 2 + 1) * SL], ACT.Gelu,
                                  bias=b1g_c[:, c, bass.ds(e, 1)], scale=gate_c[:, c, bass.ds(e, 1)])\
                      .then_inc(gelued, 1)
            iterations(ac, body)

        @block.vector
        def _(ve):
            ve.wait_ge(shared_in, 80)
            ve.tensor_tensor(scols[:, 2, :], scols[:, 0, :], scols[:, 1, :], ALU.mult).then_inc(shared_scaled, 1)
            ve.tensor_scalar(sw2[:, :, :], sw2[:, :, :], gates[:, 2:3], None, ALU.mult).then_inc(shared_scaled, 1)
            ve.tensor_scalar(sb2_row[:, :], sb2_row[:, :], gates[:, 2:3], None, ALU.mult).then_inc(shared_scaled, 1)

            steps = [0]

            def then(ins):
                steps[0] += 1
                ins.then_inc(plan_step, 1)
                ve.wait_ge(plan_step, steps[0])
            n, cum, gap = tf[:, 0], tf[:, 1], tf[:, 2]
            then(ve.tensor_tensor(n, count[:, :], cst[:, C_BASE:C_BASE + E], ALU.subtract))
            then(ve.tensor_scalar(n, n, float(SL - 1), None, ALU.add))
            then(ve.tensor_copy(trips[:, :], n))
            then(ve.tensor_scalar(trips[:, :], trips[:, :], SL.bit_length() - 1, None, ALU.logical_shift_right))
            then(ve.tensor_copy(cum, trips[:, :]))
            then(ve.tensor_scalar(gap, cum, -float(SL), float(REGION), ALU.mult, ALU.add))
            for e in range(1, E):
                then(ve.tensor_tensor(cum[:, e:e + 1], cum[:, e - 1:e], cum[:, e:e + 1], ALU.add))
            then(ve.tensor_tensor(begun[:, :, :], cst[:, C_STEP:C_STEP + T].unsqueeze(2).broadcast_to([P, T, E]),
                                  cum.unsqueeze(1).broadcast_to([P, T, E]), ALU.is_ge))
            then(ve.tensor_reduce(step_f[:, 0], begun[:, :, :], X, ALU.add))
            then(ve.tensor_scalar(expert_of[:, :], step_f[:, 0], float(E - 1), None, ALU.min))
            then(ve.tensor_tensor(begun[:, :, :], begun[:, :, :], gap.unsqueeze(1).broadcast_to([P, T, E]), ALU.mult))
            then(ve.tensor_reduce(step_f[:, 1], begun[:, :, :], X, ALU.add))
            then(ve.scalar_tensor_tensor(out=row_of[:, :], in0=cst[:, C_STEP:C_STEP + T], scalar=float(SL),
                                         in1=step_f[:, 1], op0=ALU.mult, op1=ALU.add))
            then(ve.tensor_scalar(tf[:, 3, 0:1], cum[:, E - 1:E], 1.0, None, ALU.add))
            then(ve.tensor_copy(pairs[:, :], tf[:, 3, 0:1]))
            then(ve.tensor_scalar(pairs[:, :], pairs[:, :], 1, None, ALU.logical_shift_right))
            ve.tensor_copy(ends[:, :], count[:, :]).then_inc(table_ready, 1)
            ve.wait_ge(biases_in, 48)
            ve.tensor_tensor(b1g_c[:, :, :], b1g_c[:, :, :], gate_c[:, :, :], ALU.mult).then_inc(biases_ready, 1)

            def keep(q, par):
                ve.wait_ge(sy_done, q + 1)
                out = xn2T[:, bass.ds(q * QW, QW)].rearrange("p (t d) -> p t d", d=D)
                ve.tensor_tensor(out, sy_ps[par][:, :].rearrange("p (t d) -> p t d", d=D),
                                 sb2_row[:, :].unsqueeze(1).broadcast_to([P, QT, D]), ALU.add).then_inc(kept, 1)
            with ve.Fori(0, NQ // 2) as j:
                keep(j * 2, 0)
                keep(j * 2 + 1, 1)

            def take_meta(t, par, i):
                ve.wait_ge(rows_in[par], i * 16 + 16)
                if not isinstance(t, int) or t >= 2:
                    ve.wait_ge(dest_step, (t - 1) * 3)
                ve.tensor_copy(meta[:, par], rows[:, par, :, D:ROW]).then_inc(meta_read, 1)

            def take_rows(t, par):
                ve.wait_ge(turned, t + 1)
                if not isinstance(t, int) or t >= 2:
                    ve.wait_ge(h_done, (t - 1) * HB)
                ve.tensor_copy(rT[:, par, :], t_ps[par][:, 0:SL]).then_inc(rT_ready, 1)

            def take_weights(t, par):
                e = expert(ve, t)
                if not isinstance(t, int) or t >= 2:
                    wait_apart(ve, h_done, (t - 1) * HB)
                ve.tensor_copy(w1_now[:, par, :], w1[:, bass.ds(e, 1), :].rearrange("p a f -> p (a f)"))\
                  .then_inc(w1_ready, 1)

            def destinations(t, par, i, e):
                ve.wait_ge(meta_read, t + 1)
                if not isinstance(t, int) or t >= 2:
                    ve.wait_ge(dest_step, t * 3)
                ve.tensor_scalar(destf[:, :], meta[:, par, :, 0], cst[:, bass.ds(C_EXP + e, 1)], float(TOK),
                                 ALU.not_equal, ALU.mult).then_inc(dest_step, 1)
                ve.wait_ge(dest_step, t * 3 + 1)
                ve.tensor_tensor(destf[:, :], destf[:, :], meta[:, par, :, 1], ALU.add).then_inc(dest_step, 1)
                ve.wait_ge(dest_step, t * 3 + 2)
                if not isinstance(i, int) or i >= 1:
                    ve.wait_ge(sent[par], i * 32)
                ve.tensor_copy(dest[:, par, :, 0], destf[:, :]).then_inc(dest_step, 1)

            ve.wait_ge(table_ready, 1)
            ve.wait_ge(weights_in, 64)
            for t in range(2):
                take_weights(t, t)
            for t in range(2):
                take_meta(t, t, 0)
                take_rows(t, t)

            def body(t, par, i):
                take_weights(t + 2, par)
                e = expert(ve, t)
                take_rows(t + 2, par)
                destinations(t, par, i, e)
                take_meta(t + 2, par, i + 1)
                ve.wait_ge(y_done, t + 1)
                ve.tensor_tensor(y[:, par], y_ps[par][:, 0:2 * D].rearrange("p (h d) -> p h d", d=D),
                                 b2_row[:, bass.ds(e, 1), :].broadcast_to([P, 2, D]), ALU.add).then_inc(y_ready, 1)
            iterations(ve, body)

        @block.gpsimd
        def _(po):
            for par in range(2):
                scatter_rows(po, lists, m, par, range(2 * QT))
            po.memset(pad_rows[:, :, :, :], 0.0).then_inc(pads_ready, 1)
            po.wait_ge(pads_ready, 1)
            po.memset(pad_rows[:, :, :, D:D + 1], -1.0)
            for e in range(E + 1):
                for h in range(2):
                    last = po.tensor_scalar(pad_rows[:, e, h, D + 1:ROW], cst[:, C_PART:C_PART + 1],
                                            float(TOK + e * SL + h * P), None, ALU.add)
            last.then_inc(pads_ready, 1)
            po.wait_ge(table_ready, 1)

            def body(t, par, i):
                po.wait_ge(dest_step, t * 3 + 3)
                wait_apart(po, y_ready, t + 1)
                for h in range(2):
                    po.indirect_dma_start(results[:, :], bass.IndirectOffsetOnAxis(ap=dest[:, par, h, :], axis=0),
                                          y[:, par, h, :], None).then_inc(sent[par], 16)
            iterations(po, body)


def combine(nc, a, NT, results, out, m):
    NQ = NT // QT
    TOK = NT * P
    x_all, xn2T, weight, gates = m.x_all, m.xn2T, m.weight, m.gates
    out_rows = out.rearrange("b s d -> (b s) d")
    with ExitStack() as ctx:
        sb, sem = tools(nc, ctx)
        ln_row = sb("ln_row", [P, 2, D])
        yin = sb("yin", [P, 2, 2, QT, D])
        acc = sb("acc", [P, 2, QT, D])
        st = sb("st", [P, QT, 6])
        mv = sb("mv3", [P, 2, QT, 2])
        tmp = sb("tmp", [P, 5, QT])
        tmi = sb("tmi", [P, QT], I32)
        rr = sb("rr", [P, 2, 2, QT])
        res = sb("res", [P, 2, QT, D])

        w_in, setup, wready = sem("sw_in"), sem("s_setup"), sem("s_wready")
        y_in = [sem(f"y_in{i}") for i in range(2)]
        h_done, h_ready, y_done, acc_step, stat_step, n_step, normed, scaled, xb, fin = (
            sem("c_" + n) for n in ("h_done", "h_ready", "y_done", "acc_step", "stat_step", "n_step", "normed",
                                    "scaled", "xb", "fin"))
        stored = [sem(f"stored{i}") for i in range(2)]
        passed = sem("c_passed")
        N_STEPS = 14

        def wait_apart(eng, s, value):
            wait_alone(eng, s, value, passed)

        block = ctx.enter_context(nc.Block())

        @block.sync
        def _(sp):
            for i, n in enumerate(("ln_g", "ln_b")):
                sp.dma_start(ln_row[:, i, :], a[n].unsqueeze(0).broadcast_to([P, D])).then_inc(w_in, 16)

            def load(q, par, wait):
                if wait:
                    sp.wait_ge(acc_step, (q - 1) * 2 * QT)
                for k in range(2):
                    sp.dma_start(yin[:, par, k], results[bass.ds(q * QW + k * TOK, QW), :]
                                 .rearrange("(t p) d -> p t d", p=P)).then_inc(y_in[par], 16)
            load(0, 0, False)
            load(1, 1, False)
            if NQ > 2:
                with sp.Fori(1, NQ // 2) as j:
                    for par in range(2):
                        load(j * 2 + par, par, True)

        @block.scalar
        def _(ac):
            def scale(q, par):
                ac.wait_ge(n_step, q * N_STEPS + N_STEPS)
                for t in range(QT):
                    ac.activation(acc[:, par, t, :], acc[:, par, t, :], ACT.Identity, bias=rr[:, par, 1, t:t + 1],
                                  scale=rr[:, par, 0, t:t + 1]).then_inc(scaled, 1)
            with ac.Fori(0, NQ // 2) as j:
                for par in range(2):
                    scale(j * 2 + par, par)

        @block.vector
        def _(ve):
            ve.wait_ge(w_in, 32)
            ve.tensor_scalar(ln_row[:, :, :], ln_row[:, :, :], gates[:, 1:2], None, ALU.mult).then_inc(setup, 1)

            def quad(q, par, j):
                ve.wait_ge(y_in[par], j * 32 + 32)
                if not isinstance(j, int) or j > 0:
                    ve.wait_ge(fin, q - 1)
                for t in range(QT):
                    w = weight[:, bass.ds(q * QT + t, 1), :].rearrange("p a k -> p (a k)")
                    ve.scalar_tensor_tensor(out=acc[:, par, t, :], in0=yin[:, par, 0, t, :], scalar=w[:, 0:1],
                                            in1=xn2T[:, bass.ds(q * QW + t * D, D)], op0=ALU.mult, op1=ALU.add)\
                      .then_inc(acc_step, 1)
                for t in range(QT):
                    w = weight[:, bass.ds(q * QT + t, 1), :].rearrange("p a k -> p (a k)")
                    ve.wait_ge(acc_step, q * 2 * QT + t + 1)
                    ve.scalar_tensor_tensor(out=acc[:, par, t, :], in0=yin[:, par, 1, t, :], scalar=w[:, 1:2],
                                            in1=acc[:, par, t, :], op0=ALU.mult, op1=ALU.add).then_inc(acc_step, 1)
                for t in range(QT):
                    wait_apart(ve, acc_step, q * 2 * QT + QT + t + 1)
                    ve.bn_stats(st[:, t, :], acc[:, par, t, :]).then_inc(stat_step, 1)
                for t in range(QT):
                    wait_apart(ve, stat_step, q * QT + t + 1)
                    i = ve.bn_aggr(mv[:, par, t, :], st[:, t, :])
                k = [0]

                def then(ins):
                    k[0] += 1
                    ins.then_inc(n_step, 1)
                    ve.wait_ge(n_step, q * N_STEPS + k[0])
                v, aa, bb = tmp[:, 0], tmp[:, 1], tmp[:, 2]
                rs, sh = rr[:, par, 0], rr[:, par, 1]
                then(i)
                then(ve.tensor_scalar(v, mv[:, par, :, 1], EPS, None, ALU.add))
                then(ve.tensor_scalar(tmi[:, :], v.bitcast(I32), 1, None, ALU.logical_shift_right))
                then(ve.tensor_scalar(rs.bitcast(I32), tmi[:, :], -1.0, RSQRT_MAGIC, ALU.mult, ALU.add))
                for _ in range(3):
                    then(ve.tensor_tensor(aa, rs, rs, ALU.mult))
                    then(ve.scalar_tensor_tensor(out=bb, in0=aa, scalar=-0.5, in1=v, op0=ALU.mult, op1=ALU.mult))
                    then(ve.scalar_tensor_tensor(out=rs, in0=bb, scalar=1.5, in1=rs, op0=ALU.add, op1=ALU.mult))
                then(ve.scalar_tensor_tensor(out=sh, in0=mv[:, par, :, 0], scalar=-1.0, in1=rs, op0=ALU.mult,
                                             op1=ALU.mult))

            quad(0, 0, 0)
            quad(1, 1, 0)
            with ve.Fori(1, NQ // 2) as j:
                for par in range(2):
                    quad(j * 2 + par, par, j)

        @block.gpsimd
        def _(po):
            po.wait_ge(setup, 1)

            def finish(q, par, wait):
                xs = x_all[:, bass.ds(q * QW, QW)].rearrange("p (t d) -> p t d", t=QT)
                po.tensor_tensor(xs, xs, ln_row[:, 1, :].unsqueeze(1).broadcast_to([P, QT, D]), ALU.add).then_inc(xb, 1)
                po.wait_ge(scaled, q * QT + QT)
                if wait:
                    po.wait_ge(stored[par], (q - par) * 8)
                po.tensor_tensor(res[:, par], acc[:, par], ln_row[:, 0, :].unsqueeze(1).broadcast_to([P, QT, D]),
                                 ALU.mult).then_inc(fin, 1)
                po.wait_ge(fin, q + 1)
                wait_apart(po, xb, q * 2 + 1)
                po.tensor_tensor(res[:, par], res[:, par], xs, ALU.add).then_inc(xb, 1)
                po.wait_ge(xb, q * 2 + 2)
                po.dma_start(out_rows[bass.ds(q * QW, QW), :].rearrange("(t p) d -> p t d", p=P), res[:, par])\
                  .then_inc(stored[par], 16)
            finish(0, 0, False)
            finish(1, 1, False)
            with po.Fori(1, NQ // 2) as j:
                for par in range(2):
                    finish(j * 2 + par, par, True)
            for i in range(2):
                po.wait_ge(stored[i], 8 * NQ)


def build_inputs(inputs):
    g = {k: np.asarray(v) for k, v in inputs.items()}
    f32 = {}
    f32["x"], f32["ctx_1024"] = g["x"], g["ctx_1024"]
    f32["mask_BxS2_ik0"] = g["mask_BxS2_ik0"]
    f32["src_mask"] = g["mask_1x1xSxS2_ff0"][0, 0]
    for n in ("Wq", "Wk", "Wv", "Wo"):
        f32[n + "T"] = g["L0_xattn_" + n].T
    for n in ("bq", "bk", "bv", "bo"):
        f32[n] = g["L0_xattn_" + n]
    f32["g_xattn"], f32["g_ffn"] = g["g_xattn"], g["g_ffn"]
    f32["shared_weight"] = g["L0_ffn_shared_weight"].reshape(1)
    for n in ("router_w", "router_b"):
        f32[n] = g["L0_ffn_" + n]
    for n in ("w1", "b1", "gate", "w2", "b2", "sw1", "sb1", "sgate", "sw2", "sb2", "ln_g", "ln_b"):
        f32[n] = g["L0_ffn_" + n]
    for n in ("b1", "gate"):
        f32[n] = f32[n].reshape(E, F // P, P).transpose(2, 1, 0)
    for n in ("sb1", "sgate"):
        f32[n] = f32[n].reshape(FS // P, P).T
    f32["consts"] = constants(g["x"].shape[0] // 2)
    return {k: np.ascontiguousarray(v) for k, v in f32.items()}


def kernel(**inputs):
    import concourse.bacc as bacc
    from concourse.bass_utils import run_bass_kernel_spmd

    arrays = build_inputs(inputs)
    nc = bacc.Bacc("TRN2", target_bir_lowering=False, num_devices=1)
    a = {n: nc.dram_tensor(f"in_{n}", v.shape, mybir.dt.from_np(v.dtype), kind="ExternalInput").ap()
         for n, v in arrays.items()}
    out = nc.dram_tensor("out", inputs["x"].shape, F32, kind="ExternalOutput").ap()
    bass_kernel(nc, a, out)
    r = run_bass_kernel_spmd(nc, [{f"in_{n}": v for n, v in arrays.items()}], core_ids=[0])
    return r.results[0]["out"]
```

```python
from contextlib import ExitStack

import numpy as np
import concourse.bass as bass
from concourse import mybir
from concourse.alu_op_type import AluOpType as ALU

ACT = mybir.ActivationFunctionType
F32 = mybir.dt.float32
BF16 = mybir.dt.bfloat16
I32 = mybir.dt.int32
F32R = mybir.dt.float32r
X = mybir.AxisListType.X

P = 128
D = 128
H = 16
DK = D // H
HG = 32 // DK
NG = H // HG
S = 64
E = 8
F = 512
FS = 256
QT = 4
QW = QT * D
VS = 48
ROW = D + 2
SL = 256
NEG = -1.0e9
EPS = 1e-5
RSQRT_MAGIC = float(0x5F3759DF)
LN_STEPS = 14
RA_STEPS = 12
RB_STEPS = 5

C_ID = 0
C_TRI = C_ID + P
C_JM = C_TRI + P
C_REV = C_JM + HG
C_BASE = C_REV + QT * E
C_PART = C_BASE + E
C_EXP = C_PART + 1
C_TOKEN = C_EXP + E


def split(ve, done, high, low, x):
    sem, then = done
    ve.tensor_copy(high, x).then_inc(sem, 1)
    then()
    ve.tensor_tensor(low, x, high.bitcast(F32), ALU.subtract).then_inc(sem, 1)


def product(pe, out, a, b):
    (ah, al), (bh, bl) = a, b
    pe.matmul(out, ah, bh, start=True, stop=False)
    pe.matmul(out, ah, bl, start=False, stop=False)
    return pe.matmul(out, al, bh, start=False, stop=True)


def steps_listed(NT):
    return 2 * NT * P // SL + E + 3


def constants(NT):
    c = np.zeros((P, C_TOKEN + NT + steps_listed(NT)), np.float32)
    p = np.arange(P)
    c[:, C_ID:C_ID + P] = np.eye(P)
    c[:, C_TRI:C_TRI + P] = p[:, None] < p[None, :]
    c[:, C_JM:C_JM + HG] = (p[:, None] % 32) // DK == np.arange(HG)[None, :]
    c[:, C_REV:C_REV + QT * E] = np.tile(E - np.arange(E), QT)
    c[:, C_BASE:C_BASE + E] = np.arange(E) * (NT * P + SL)
    c[:, C_PART] = p
    c[:, C_EXP:C_EXP + E] = np.arange(E)
    c[:, C_TOKEN:C_TOKEN + NT] = NT * P + p[:, None] + P * np.arange(NT)[None, :]
    c[:, C_TOKEN + NT:] = np.arange(steps_listed(NT))
    return c


def bass_kernel(nc, a, out):
    NT = a["x"].shape[0] // 2
    TOK = NT * P
    REGION = TOK + SL
    assert NT % (2 * QT) == 0


    lists = nc.dram_tensor("expert_lists", [E * REGION + 3 * SL, ROW], F32).ap()
    results = nc.dram_tensor("expert_results", [2 * TOK + (E + 1) * SL, D], F32).ap()

    with ExitStack() as whole:
        m = shared_memory(nc, whole, NT)
        attention(nc, a, NT, lists, m)
        experts(nc, a, NT, REGION, lists, results, m)
        combine(nc, a, NT, results, out, m)


def wait_alone(eng, s, value, passed):
    eng.wait_ge(s, value)
    eng.sem_inc(passed, 1)


def tools(nc, ctx):
    def sb(name, shape, dt=F32):
        return ctx.enter_context(nc.sbuf_tensor(name, shape, dt))

    def sem(name):
        return ctx.enter_context(nc.semaphore(name))
    return sb, sem


class Shared:
    pass


def shared_memory(nc, ctx, NT):
    sb, sem = tools(nc, ctx)
    m = Shared()
    m.x_all = sb("x_all", [P, NT * D])
    m.xn2T = sb("xn2T", [P, NT * D])
    m.weight = sb("weight", [P, NT, 2])
    m.cst = sb("cst", [P, C_TOKEN + NT + steps_listed(NT)])
    m.gates = sb("gates", [P, 4])
    m.count = sb("count", [P, E])
    m.xn2 = sb("xn2", [P, 2, QT, ROW])
    m.slots = sb("slots", [P, 2, QT, 2], I32)
    m.scattered = [sem(f"scattered{i}") for i in range(2)]
    m.sw1 = sb("sw1", [P, FS])
    m.sw2 = sb("sw2", [P, FS // P, D])
    m.scols = sb("scols", [P, 3, FS // P])
    m.sb2_row = sb("sb2_row", [P, D])
    m.ln_row = sb("ln_row", [P, 2, D])
    m.shared_in = sem("shared_in")
    m.banks = [ctx.enter_context(nc.psum_tensor(f"bank{i}", [P, 512], F32)) for i in range(8)]
    return m


def scatter_rows(po, lists, m, par, which):
    for i in which:
        t, k = i // 2, i % 2
        po.indirect_dma_start(lists[:, :], bass.IndirectOffsetOnAxis(ap=m.slots[:, par, t, k:k + 1], axis=0),
                              m.xn2[:, par, t, :], None).then_inc(m.scattered[par], 16)


def attention(nc, a, NT, lists, m):
    NQ = NT // QT
    x_all, xn2T, weight, cst, gates, count = m.x_all, m.xn2T, m.weight, m.cst, m.gates, m.count
    xn2, slots, scattered, banks = m.xn2, m.slots, m.scattered, m.banks
    x_rows = a["x"].rearrange("b s d -> (b s) d")
    c_rows = a["ctx_1024"].rearrange("b s d -> (b s) d")
    pad_mask = a["mask_BxS2_ik0"]
    with ExitStack() as ctx:
        sb, sem = tools(nc, ctx)

        ident = cst[:, C_ID:C_ID + P]
        rev = cst[:, C_REV:C_REV + QT * E].rearrange("p (t e) -> p t e", t=QT)
        tri_bf = sb("tri_bf", [P, P], BF16)
        ones_bf = sb("ones_bf", [P, P], BF16)
        w_att = sb("w_att", [P, 4, D])
        wq, wk, wv, wo = (w_att[:, i, :] for i in range(4))
        cols = sb("cols", [P, 8])
        bo_row = sb("bo_row", [P, D])
        bo_tmp = sb("bo_tmp", [P, D])
        bv_mat = sb("bv_mat", [P, P])
        router = sb("router", [P, 33])
        rw = router[:, 0:32]
        rb = router[:, 32:33]
        srcm = sb("srcm", [P, S])
        ctx_in = sb("ctx_in", [P, 2, QW])
        pad_q = sb("pad_q", [P, 2, QT, S], I32)
        pad_k = sb("pad_k", [P, 2, QW], I32)
        keep = sb("keep", [P, QW])
        mask = sb("mask", [P, 2, QT, S])
        xn = sb("xn", [P, QW])
        xT = sb("xT", [P, QW])
        cT = sb("cT", [P, QW])
        kT = sb("kT", [P, QW])
        qg = sb("qg", [P, 2, NG, QW])
        kbd = sb("kbd", [P, 2, QT * 2, HG, S])
        vb = sb("vb", [P, 2, QT, 2, 8 * VS])
        prob = sb("prob", [P, QT, H * S])
        PT = sb("PT", [P, 2, 8 * P])
        mx = sb("mx", [P, QT, H])
        sm = sb("sm", [P, QT, H])
        rsx = sb("rsx", [P, QT, D])
        rsT = sb("rsT", [P, 2, P])
        aT = sb("aT", [P, 2, P])
        st1 = sb("st1", [P, QT, 6])
        st2 = sb("st2", [P, QT, 6])
        mv = sb("mv", [P, 2 * QT, 2])
        ln_v = sb("ln_v", [P, 2 * QT])
        ln_i = sb("ln_i", [P, 2 * QT], I32)
        ln_a = sb("ln_a", [P, 2 * QT])
        ln_b = sb("ln_b", [P, 2 * QT])
        ln_r = sb("ln_r", [P, 2 * QT])
        ln_s = sb("ln_s", [P, 2 * QT])
        x2T = sb("x2T", [P, 2, QW])
        LT = sb("LT", [P, P])
        lg = sb("lg", [P, QT, E])
        ra = sb("ra", [P, 4, QT, E])
        r_m = sb("r_m", [P, 6, QT])
        oh = sb("oh", [P, 2, QT, E])
        oh_bf = sb("oh_bf", [P, QT, E], BF16)
        posn = sb("posn", [P, QT, E])
        rt = sb("rt", [P, 2, QT, E])
        slotf = sb("slotf", [P, QT, 2])

        sc_ps, pt_ps = banks[0:2], banks[2:4]
        fa_ps, fb_ps, att_ps, out_ps = banks[4:8]

        const_in = sem("const_in")
        setup_pool = sem("setup_pool")
        setup_act = sem("setup_act")
        setup_pe = sem("setup_pe")
        setup_dve = sem("setup_dve")
        quad_in = [sem(f"quad_in{i}") for i in range(2)]
        stats1 = sem("stats1")
        stats2 = sem("stats2")
        ln_step = sem("ln_step")
        xn_ready = sem("xn_ready")
        xT_done, xT_ready = sem("xT_done"), sem("xT_ready")
        cT_done, cT_ready = sem("cT_done"), sem("cT_ready")
        q_done, q_ready = sem("q_done"), sem("q_ready")
        k_done, kT_ready, k_ready = sem("k_done"), sem("kT_ready"), sem("k_ready")
        v_done, v_ready = sem("v_done"), sem("v_ready")
        keep_ready, mask_tmp, mask_ready, xb_ready = sem("keep_ready"), sem("mask_tmp"), sem("mask_ready"), sem("xb_ready")
        scores_done, masked, maxed, subbed, exped = (sem(n) for n in ("scores_done", "masked", "maxed", "subbed", "exped"))
        summed, recips, rs_ready = sem("summed"), sem("recips"), sem("rs_ready")
        turned, PT_ready, att_done, rsT_ready, aT_ready = (sem(n) for n in ("turned", "PT_ready", "att_done", "rsT_ready", "aT_ready"))
        wo_done, x2_ready = sem("wo_done"), sem("x2_ready")
        xn2_ready, x2T_done, x2T_ready = sem("xn2_ready"), sem("x2T_done"), sem("x2T_ready")
        lg_done, LT_ready, lgT_done, lg_copied = (sem(n) for n in ("lg_done", "LT_ready", "lgT_done", "lg_copied"))
        ra_step, p2_ready, pref_done, pref_copied, rb_step = (sem(n) for n in ("ra_step", "p2_ready", "pref_done", "pref_copied", "rb_step"))
        x2T_kept = [sem(f"x2T_kept{i}") for i in range(2)]
        passed = sem("a_passed")

        def need(eng, s, item, per=1, k=None, total=NT, apart=False):
            k = per if k is None else k
            if isinstance(item, int):
                if item < 0:
                    return
                if item >= total:
                    item, k = total - 1, per
            if apart and not isinstance(item, int):
                wait_alone(eng, s, item * per + k, passed)
            else:
                eng.wait_ge(s, item * per + k)

        def exists(item, total):
            return not isinstance(item, int) or 0 <= item < total

        def loop(eng, step, first, last):
            lo, hi = 2, NQ // 2 - 2
            for j in range(first, min(lo, last)):
                step(j)
            if hi > lo:
                with eng.Fori(lo, hi) as j:
                    step(j)
            for j in range(max(hi, lo), last):
                step(j)

        J0, J1 = -1, NQ // 2 + 2

        def cols_of(t, n=1):
            return bass.ds(t * D, n * D)

        block = ctx.enter_context(nc.Block())

        @block.sync
        def _(sp):
            sp.dma_start(cst[:, :], a["consts"]).then_inc(const_in, 16)
            for t, n in ((w_att, "w_att"), (srcm, "src_mask"), (router, "router"), (cols[:, 0:3], "b_att")):
                sp.dma_start(t if n == "b_att" else t[:], a[n]).then_inc(const_in, 16)
            sp.dma_start(bo_tmp[:, :], a["bo"].unsqueeze(0).broadcast_to([P, D])).then_inc(const_in, 16)
            sp.dma_start(gates[:, 0:3], a["gates"].unsqueeze(0).broadcast_to([P, 3])).then_inc(const_in, 16)

            def load(q, par):
                need(sp, cT_done, q - 2, total=NQ)
                need(sp, mask_ready, q - 2, total=NQ)
                need(sp, keep_ready, q - 2, total=NQ)
                rows = bass.ds(q * QW, QW)
                done = quad_in[par]
                sp.dma_start(x_all[:, cols_of(q * QT, QT)].rearrange("p (t d) -> p t d", t=QT),
                             x_rows[rows, :].rearrange("(t p) d -> p t d", p=P)).then_inc(done, 16)
                sp.dma_start(ctx_in[:, par, :].rearrange("p (t d) -> p t d", t=QT),
                             c_rows[rows, :].rearrange("(t p) d -> p t d", p=P)).then_inc(done, 16)
                pads = pad_mask[bass.ds(q * 2 * QT, 2 * QT), :]
                for b in range(2):
                    src = pads.rearrange("(t b) k -> b t k", b=2)[b:b + 1].broadcast_to([S, QT, S])
                    sp.dma_start(pad_q[b * S:(b + 1) * S, par], src).then_inc(done, 16)
                sp.dma_start(pad_k[:, par].rearrange("p (b k) -> p b k", k=S),
                             pads.unsqueeze(0).broadcast_to([P, 2 * QT, S])).then_inc(done, 16)

            load(0, 0)
            load(1, 1)
            if NQ // 2 > 1:
                with sp.Fori(1, NQ // 2) as j:
                    load(j * 2, 0)
                    load(j * 2 + 1, 1)
            sp.dma_start(m.sw1[:, :], a["sw1"]).then_inc(m.shared_in, 16)
            for i, n in enumerate(("sgate", "sb1")):
                sp.dma_start(m.scols[:, i, :], a[n]).then_inc(m.shared_in, 16)
            sp.dma_start(m.sw2[:, :, :], a["sw2"].rearrange("(c f) d -> f c d", f=P)).then_inc(m.shared_in, 16)
            sp.dma_start(m.sb2_row[:, :], a["sb2"].unsqueeze(0).broadcast_to([P, D])).then_inc(m.shared_in, 16)
            for i, n in enumerate(("ln_g", "ln_b")):
                sp.dma_start(m.ln_row[:, i, :], a[n].unsqueeze(0).broadcast_to([P, D])).then_inc(m.shared_in, 16)

        LOADS = 5
        CONSTS = 16 * 7

        def quad_loaded(eng, j, par, dq, apart=False):
            p2, j2 = (par + dq) % 2, j + (par + dq) // 2
            need(eng, quad_in[p2], j2, per=16 * LOADS, total=NQ // 2, apart=apart)
            return p2

        @block.tensor
        def _(pe):
            pe.wait_ge(const_in, CONSTS)
            pe.wait_ge(setup_dve, 4)
            pe.matmul(att_ps[:, 0:D], bv_mat[:, :], wo, start=True, stop=True).then_inc(setup_pe, 1)
            pe.wait_ge(setup_dve, 5)
            pe.wait_ge(setup_pool, 3)

            def scores(n, u, par, q, h):
                if u == 0 and h == 0:
                    need(pe, q_ready, q, per=NG, total=NQ)
                    need(pe, k_ready, q, per=HG, total=NQ)
                need(pe, masked, n - 1, per=2, k=h + 1)
                for g in (2 * h, 2 * h + 1):
                    for b in range(2):
                        i = pe.matmul(sc_ps[h][b * S:(b + 1) * S, (g % 2) * 256:(g % 2) * 256 + 256],
                                      qg[:, par, g, u * P + b * S:u * P + (b + 1) * S],
                                      kbd[:, par, 2 * u + b].rearrange("p j k -> p (j k)"), start=True, stop=True)
                i.then_inc(scores_done, 1)

            def turn(n, u):
                need(pe, exped, n)
                for h in range(2):
                    need(pe, PT_ready, n - 1, per=2, k=h + 1)
                    for i in range(4):
                        p = 4 * h + i
                        t = pe.transpose(pt_ps[h][:, i * P:(i + 1) * P], prob[:, u, p * P:(p + 1) * P], ident)
                    t.then_inc(turned, 1)

            def project_out(n, u):
                need(pe, aT_ready, n)
                need(pe, x2_ready, n - 1)
                pe.matmul(out_ps[:, 0:D], aT[:, u % 2, :], wo, start=True, stop=True).then_inc(wo_done, 1)

            def step(j):
                for v in range(2 * QT):
                    par, u = v // QT, v % QT
                    q = j * 2 + par
                    n = j * 2 * QT + v
                    for h in range(2):
                        if exists(n, NT):
                            scores(n, u, par, q, h)
                        if h == 0 and u == 3 and exists(q - 2, NQ):
                            need(pe, LT_ready, q - 2, total=NQ)
                            pe.transpose(fb_ps[:, 0:P], LT[:, :], ident).then_inc(lgT_done, 1)
                    if u == 0 and exists(q + 1, NQ):
                        need(pe, xn_ready, q + 1, per=QT, total=NQ)
                        need(pe, v_ready, q, per=4, total=NQ)
                        for t in range(QT):
                            i = pe.transpose(fa_ps[:, t * P:(t + 1) * P], xn[:, t * P:(t + 1) * P], ident)
                        i.then_inc(xT_done, 1)
                    if u == 1 and exists(q + 1, NQ):
                        need(pe, xT_ready, q + 1, total=NQ)
                        pe.matmul(fa_ps[:, :], wq, xT[:, :], start=True, stop=True).then_inc(q_done, 1)
                    if u == 2 and exists(q - 2, NQ):
                        need(pe, xn2_ready, q - 2, per=QT, total=NQ)
                        need(pe, q_ready, q + 1, per=NG, total=NQ)
                        for t in range(QT):
                            i = pe.transpose(fa_ps[:, t * P:(t + 1) * P], xn2[:, par, t, 0:D], ident)
                        i.then_inc(x2T_done, 1)
                    if u == 3 and exists(q + 1, NQ):
                        need(pe, cT_ready, q + 1, total=NQ)
                        need(pe, q_ready, q + 1, per=NG, total=NQ)
                        need(pe, x2T_ready, q - 2, total=NQ)
                        for t in range(QT):
                            i = pe.matmul(fa_ps[:, t * P:(t + 1) * P], cT[:, t * P:(t + 1) * P], wv,
                                          start=True, stop=True)
                        i.then_inc(v_done, 1)
                    if exists(n - 2, NT):
                        turn(n - 2, (u - 2) % QT)
                    if u == 0 and exists(q - 3, NQ):
                        need(pe, ra_step, q - 3, per=RA_STEPS, total=NQ)
                        need(pe, x2_ready, n - 5)
                        pre = out_ps[:, P:P + QT * E]
                        pe.matmul(pre, tri_bf[:, :], oh_bf[:, :, :].rearrange("p t e -> p (t e)"),
                                  start=True, stop=False, skip_group_check=True)
                        for t in range(QT):
                            for t2 in range(t + 1, QT + 1):
                                i = pe.matmul(out_ps[:, P + t2 * E:P + (t2 + 1) * E], ones_bf[:, :],
                                              oh_bf[:, t, :], start=False, stop=(t == QT - 1),
                                              skip_group_check=True)
                        i.then_inc(pref_done, 1)
                    if exists(n - 4, NT):
                        if u == 1:
                            need(pe, pref_copied, q - 3, per=2, total=NQ)
                        project_out(n - 4, u)
                    if u == 0 and exists(q + 1, NQ):
                        p2 = quad_loaded(pe, j, par, 1)
                        need(pe, lg_copied, q - 3, total=NQ)
                        for t in range(QT):
                            i = pe.transpose(fb_ps[:, t * P:(t + 1) * P], ctx_in[:, p2, t * P:(t + 1) * P], ident)
                        i.then_inc(cT_done, 1)
                    if u == 1 and exists(q + 1, NQ):
                        need(pe, cT_ready, q + 1, total=NQ)
                        pe.matmul(fb_ps[:, :], wk, cT[:, :], start=True, stop=True).then_inc(k_done, 1)
                    if exists(n - 3, NT):
                        if u == 3:
                            need(pe, v_ready, q, per=4, total=NQ)
                        values(n - 3, (u - 3) % QT, par if u == 3 else 1 - par)
                    if u == 2 and exists(q - 2, NQ):
                        need(pe, x2T_ready, q - 2, total=NQ)
                        need(pe, kT_ready, q + 1, total=NQ)
                        for t in range(QT):
                            i = pe.matmul(fb_ps[32 * t:32 * t + 32, 0:P], rw,
                                          x2T[:, par, t * P:(t + 1) * P], start=True, stop=True)
                        i.then_inc(lg_done, 1)

            def values(n, u, par):
                need(pe, PT_ready, n, per=2)
                need(pe, aT_ready, n - 1)
                for b in range(2):
                    for c in range(2):
                        for g in range(NG):
                            p = 2 * g + c
                            pe.matmul(att_ps[32 * g:32 * g + 32, b * S:(b + 1) * S],
                                      vb[:, par, u, b, 16 + VS * p - 16 * c:16 + VS * p - 16 * c + 32],
                                      PT[:, u % 2, p * P + b * S:p * P + (b + 1) * S],
                                      start=(c == 0), stop=(c == 1))
                need(pe, rs_ready, n)
                pe.transpose(att_ps[:, P:2 * P], rsx[:, u, :], ident).then_inc(att_done, 1)

            loop(pe, step, J0, J1)

        @block.vector
        def _(ve):
            ve.wait_ge(const_in, CONSTS)
            ve.tensor_copy(tri_bf[:, :], cst[:, C_TRI:C_TRI + P]).then_inc(setup_dve, 1)
            ve.tensor_copy(count[:, :], cst[:, C_BASE:C_BASE + E]).then_inc(setup_dve, 1)
            ve.tensor_scalar(cols[:, 3:4], cols[:, 0:1], float(DK) ** -0.5, None, ALU.mult).then_inc(setup_dve, 1)
            ve.tensor_copy(bv_mat[:, :], cols[:, 2:3].broadcast_to([P, P])).then_inc(setup_dve, 1)
            ve.wait_ge(setup_pe, 1)
            ve.wait_ge(setup_act, 1)
            ve.tensor_tensor(bo_tmp[:, :], att_ps[:, 0:D], bo_tmp[:, :], ALU.add).then_inc(setup_dve, 1)
            ve.wait_ge(setup_dve, 5)
            ve.tensor_scalar(bo_row[:, :], bo_tmp[:, :], gates[:, 0:1], None, ALU.mult).then_inc(setup_dve, 1)
            ve.memset(mv[:, :, :], 1.0).then_inc(setup_dve, 1)
            ve.memset(st1[:, :, :], 1.0).then_inc(setup_dve, 1)
            ve.memset(st2[:, :, :], 1.0).then_inc(setup_dve, 1)
            ve.wait_ge(setup_act, 2)
            ve.wait_ge(setup_dve, 9)
            ve.tensor_scalar(gates[:, 2:3], gates[:, 2:3], 1.0, None, ALU.add).then_inc(setup_dve, 1)
            ve.wait_ge(setup_dve, 10)
            ve.reciprocal(gates[:, 2:3], gates[:, 2:3]).then_inc(setup_dve, 1)

            def chain(s, base, per):
                k = [0]

                def then(ins):
                    k[0] += 1
                    ins.then_inc(s, 1)
                    ve.wait_ge(s, base * per + k[0])
                    assert k[0] <= per
                return then

            def sums(n, u):
                need(ve, exped, n)
                ve.tensor_reduce(sm[:, u, :], prob[:, u, :].rearrange("p (h k) -> p h k", k=S),
                                 X, ALU.add).then_inc(summed, 1)

            def sums_inverse(n, u):
                need(ve, summed, n)
                ve.reciprocal(sm[:, u, :], sm[:, u, :]).then_inc(recips, 1)

            def sums_spread(n, u):
                need(ve, recips, n)
                need(ve, att_done, n - QT)
                ve.tensor_copy(rsx[:, u, :].rearrange("p (h d) -> p h d", d=DK),
                               sm[:, u, :].unsqueeze(2).broadcast_to([P, H, DK])).then_inc(rs_ready, 1)

            def normalise(n, u):
                need(ve, rsT_ready, n)
                need(ve, wo_done, n - 2)
                ve.tensor_tensor(aT[:, u % 2, :], att_ps[:, 0:P], rsT[:, u % 2, :], ALU.mult).then_inc(aT_ready, 1)

            def add_mask(n, u, par, q, h):
                if h == 0:
                    need(ve, turned, n - QT, per=2)
                    need(ve, mask_ready, q, total=NQ)
                need(ve, scores_done, n, per=2, k=h + 1)
                ve.tensor_tensor(prob[:, u, h * 512:(h + 1) * 512].rearrange("p (h k) -> p h k", k=S),
                                 sc_ps[h][:, :].rearrange("p (h k) -> p h k", k=S),
                                 mask[:, par, u, :].unsqueeze(1).broadcast_to([P, H // 2, S]),
                                 ALU.add).then_inc(masked, 1)

            def maxima(n, u):
                need(ve, masked, n, per=2)
                ve.tensor_reduce(mx[:, u, :], prob[:, u, :].rearrange("p (h k) -> p h k", k=S),
                                 X, ALU.max).then_inc(maxed, 1)

            def add_out(n, u, q):
                need(ve, wo_done, n)
                need(ve, xb_ready, q, total=NQ)
                xs = x_all[:, cols_of(n)]
                ve.scalar_tensor_tensor(out=xs, in0=out_ps[:, 0:D], scalar=gates[:, 0:1], in1=xs,
                                        op0=ALU.mult, op1=ALU.add).then_inc(x2_ready, 1)

            def out_stats(n, u):
                need(ve, x2_ready, n, apart=True)
                ve.bn_stats(st2[:, u, :], x_all[:, cols_of(n)]).then_inc(stats2, 1)

            def in_stats(j, par, q, dq):
                quad_loaded(ve, j, par, dq, apart=True)
                for t in range(QT):
                    ve.bn_stats(st1[:, t, :], x_all[:, cols_of((q + dq) * QT + t)]).then_inc(stats1, 1)

            def norms(i, q):
                if i > 1:
                    need(ve, ln_step, q + 2, per=LN_STEPS, k=i - 1, total=NQ + 4)
                if i == 1:
                    need(ve, stats1, q + 2, per=QT, total=NQ)
                    need(ve, stats2, q - 2, per=QT, total=NQ)
                    need(ve, xn2_ready, q - 3, per=QT, total=NQ)
                    need(ve, xn_ready, q + 1, per=QT, total=NQ, apart=True)
                    for t in range(QT):
                        ve.bn_aggr(mv[:, t, :], st1[:, t, :])
                        ins = ve.bn_aggr(mv[:, QT + t, :], st2[:, t, :])
                elif i == 2:
                    ins = ve.tensor_scalar(ln_v[:, :], mv[:, :, 1], EPS, None, ALU.add)
                elif i == 3:
                    ins = ve.tensor_scalar(ln_i[:, :], ln_v[:, :].bitcast(I32), 1, None, ALU.logical_shift_right)
                elif i == 4:
                    ins = ve.tensor_scalar(ln_r[:, :].bitcast(I32), ln_i[:, :], -1.0, RSQRT_MAGIC, ALU.mult, ALU.add)
                elif i in (5, 8, 11):
                    ins = ve.tensor_tensor(ln_a[:, :], ln_r[:, :], ln_r[:, :], ALU.mult)
                elif i in (6, 9, 12):
                    ins = ve.scalar_tensor_tensor(out=ln_b[:, :], in0=ln_a[:, :], scalar=-0.5, in1=ln_v[:, :],
                                                  op0=ALU.mult, op1=ALU.mult)
                elif i in (7, 10, 13):
                    ins = ve.scalar_tensor_tensor(out=ln_r[:, :], in0=ln_b[:, :], scalar=1.5, in1=ln_r[:, :],
                                                  op0=ALU.add, op1=ALU.mult)
                else:
                    ins = ve.scalar_tensor_tensor(out=ln_s[:, :], in0=mv[:, :, 0], scalar=-1.0, in1=ln_r[:, :],
                                                  op0=ALU.mult, op1=ALU.mult)
                ins.then_inc(ln_step, 1)

            def wide(t):
                return t.unsqueeze(2).broadcast_to([P, QT, E])

            def route_a(i, q):
                d1, c1, d2, c2 = (ra[:, k] for k in range(4))
                m1, f1, m2, f2 = (r_m[:, k] for k in range(4))
                if i == 0:
                    need(ve, lgT_done, q, total=NQ)
                    ve.tensor_copy(lg[:, :, :], fb_ps[:, 0:P].rearrange("p (t e) -> p t e", t=QT)[:, :, 0:E])\
                        .then_inc(lg_copied, 1)
                    return
                if i == 1:
                    need(ve, lg_copied, q, total=NQ)
                    ins = ve.tensor_reduce(m1, lg[:, :, :], X, ALU.max)
                else:
                    need(ve, ra_step, q, per=RA_STEPS, k=i - 1, total=NQ)
                if i == 2:
                    ins = ve.tensor_tensor(d1, lg[:, :, :], wide(m1), ALU.subtract)
                elif i == 3:
                    ins = ve.scalar_tensor_tensor(out=c1, in0=d1, scalar=0.0, in1=rev, op0=ALU.is_equal, op1=ALU.mult)
                elif i == 4:
                    ins = ve.tensor_reduce(f1, c1, X, ALU.max)
                elif i == 5:
                    ins = ve.tensor_tensor(oh[:, 0], rev, wide(f1), ALU.is_equal)
                elif i == 6:
                    ins = ve.scalar_tensor_tensor(out=d2, in0=oh[:, 0], scalar=-3.0e38, in1=d1, op0=ALU.mult,
                                                  op1=ALU.add)
                elif i == 7:
                    ins = ve.tensor_reduce(m2, d2, X, ALU.max)
                elif i == 8:
                    ins = ve.tensor_tensor(c2, d2, wide(m2), ALU.is_equal)
                elif i == 9:
                    ins = ve.tensor_tensor(c2, c2, rev, ALU.mult)
                elif i == 10:
                    ins = ve.tensor_reduce(f2, c2, X, ALU.max)
                elif i == 11:
                    ins = ve.tensor_tensor(oh[:, 1], rev, wide(f2), ALU.is_equal)
                elif i == 12:
                    ins = ve.tensor_tensor(oh_bf[:, :, :], oh[:, 0], oh[:, 1], ALU.add)
                ins.then_inc(ra_step, 1)

            def route_b(i, q, par):
                p2, s2 = r_m[:, 4], r_m[:, 5]
                tiles = bass.ds(q * QT, QT)
                if i == 0:
                    need(ve, p2_ready, q, total=NQ)
                    need(ve, pref_done, q, total=NQ)
                    pre = out_ps[:, P:P + QT * E].rearrange("p (t e) -> p t e", t=QT)
                    ve.tensor_tensor(posn[:, :, :], pre, count[:, :].unsqueeze(1).broadcast_to([P, QT, E]), ALU.add)\
                        .then_inc(pref_copied, 1)
                elif i == 1:
                    ve.tensor_scalar(s2, p2, 1.0, None, ALU.add).then_inc(rb_step, 1)
                elif i == 2:
                    need(ve, pref_copied, q, per=2, k=1, total=NQ)
                    ve.tensor_tensor(count[:, :], out_ps[:, P + QT * E:P + (QT + 1) * E], count[:, :],
                                     ALU.add).then_inc(pref_copied, 1)
                elif i == 3:
                    need(ve, rb_step, q, per=RB_STEPS, k=1, total=NQ)
                    ve.reciprocal(s2, s2).then_inc(rb_step, 1)
                elif i == 4:
                    ve.tensor_tensor(rt[:, 0], oh[:, 0], posn[:, :, :], ALU.mult)
                    ve.tensor_tensor(rt[:, 1], oh[:, 1], posn[:, :, :], ALU.mult).then_inc(rb_step, 1)
                elif i == 5:
                    need(ve, rb_step, q, per=RB_STEPS, k=2, total=NQ)
                    ve.tensor_copy(weight[:, tiles, 0], s2)
                    ve.tensor_tensor(weight[:, tiles, 1], p2, s2, ALU.mult)
                    need(ve, rb_step, q, per=RB_STEPS, k=3, total=NQ)
                    ve.tensor_reduce(slotf[:, :, 0], rt[:, 0], X, ALU.add)
                    ve.tensor_reduce(slotf[:, :, 1], rt[:, 1], X, ALU.add).then_inc(rb_step, 1)
                elif i == 6:
                    need(ve, xn2_ready, q, per=QT, total=NQ)
                    ve.tensor_scalar(xn2[:, par, :, D], r_m[:, 1], -1.0, float(E), ALU.mult, ALU.add)
                    ve.tensor_copy(xn2[:, par, :, D + 1], cst[:, bass.ds(q * QT + C_TOKEN, QT)])
                else:
                    need(ve, rb_step, q, per=RB_STEPS, k=4, total=NQ)
                    ve.tensor_copy(slots[:, par], slotf[:, :, :]).then_inc(rb_step, 1)

            def keys(q):
                need(ve, k_done, q, total=NQ)
                need(ve, keep_ready, q, total=NQ)
                need(ve, k_ready, q - 1, per=HG, total=NQ)
                ve.scalar_tensor_tensor(out=kT[:, :], in0=fb_ps[:, :], scalar=cols[:, 1:2], in1=keep[:, :],
                                        op0=ALU.add, op1=ALU.mult).then_inc(kT_ready, 1)

            NORMS_AT = (((1,), (2,), (3,), (4,), (5,), (6,), (7,), (8,)),
                        ((9,), (10,), (11,), (12,), (13,), (14,), (), ()))
            ROUTE_A_AT = ((0,), (1, 2), (3, 4), (5,), (6, 7), (8, 9), (10, 11), (12,))

            def between(place, j, u, par, q):
                if isinstance(q, int) and q == -2 and u == 0 and place == 0:
                    in_stats(j, par, q, 2)
                if u < 2 and (not isinstance(q, int) or q <= NQ + 1):
                    for i in NORMS_AT[u][place]:
                        norms(i, q)
                if u == 2 and place == 6 and exists(q + 3, NQ):
                    in_stats(j, par, q, 3)
                if u == 1 and exists(q - 3, NQ):
                    route_b(place, q - 3, 1 - par)
                if u == 2 and place == 3 and exists(q + 1, NQ):
                    keys(q + 1)
                if u == 3 and exists(q - 2, NQ):
                    for i in ROUTE_A_AT[place]:
                        route_a(i, q - 2)

            def step(j):
                for v in range(2 * QT):
                    par, u = v // QT, v % QT
                    q = j * 2 + par
                    n = j * 2 * QT + v
                    place = (j, u, par, q)
                    if exists(n - 2, NT):
                        sums(n - 2, (u - 2) % QT)
                    between(0, *place)
                    if exists(n, NT):
                        add_mask(n, u, par, q, 0)
                    between(1, *place)
                    if exists(n - 2, NT):
                        sums_inverse(n - 2, (u - 2) % QT)
                    between(2, *place)
                    if exists(n, NT):
                        add_mask(n, u, par, q, 1)
                    between(3, *place)
                    if exists(n - 2, NT):
                        sums_spread(n - 2, (u - 2) % QT)
                    between(4, *place)
                    if exists(n - 4, NT):
                        normalise(n - 4, u)
                    between(5, *place)
                    if exists(n, NT):
                        maxima(n, u)
                    between(6, *place)
                    if exists(n - 4, NT):
                        add_out(n - 4, u, q - 1)
                    between(7, *place)
                    if exists(n - 4, NT):
                        out_stats(n - 4, u)

            loop(ve, step, J0, J1)

        @block.scalar
        def _(ac):
            ac.wait_ge(const_in, CONSTS)
            ac.activation(gates[:, 0:2], gates[:, 0:2], ACT.Tanh).then_inc(setup_act, 1)
            ac.activation(gates[:, 2:3], gates[:, 2:3], ACT.Exp, scale=-1.0).then_inc(setup_act, 1)
            ac.wait_ge(setup_dve, 9)
            ac.wait_ge(setup_pool, 3)

            def step(j):
                for v in range(2 * QT):
                    par, u = v // QT, v % QT
                    q = j * 2 + par
                    n = j * 2 * QT + v
                    if exists(n - 4, NT):
                        need(ac, att_done, n - 4)
                        ac.activation(rsT[:, u % 2, :], att_ps[:, P:2 * P], ACT.Copy).then_inc(rsT_ready, 1)
                    if u == 3 and exists(q + 2, NQ):
                        need(ac, ln_step, q + 2, per=LN_STEPS, total=NQ + 4)
                        need(ac, xT_done, q + 1, total=NQ)
                        for t in range(QT):
                            ac.activation(xn[:, t * P:(t + 1) * P], x_all[:, cols_of((q + 2) * QT + t)], ACT.Identity,
                                          bias=ln_s[:, t:t + 1], scale=ln_r[:, t:t + 1]).then_inc(xn_ready, 1)
                    if u == 0 and exists(q - 3, NQ):
                        need(ac, ra_step, q - 3, per=RA_STEPS, total=NQ)
                        ac.activation(r_m[:, 4], r_m[:, 2], ACT.Exp).then_inc(p2_ready, 1)
                    if u == 0 and exists(q + 1, NQ):
                        need(ac, xT_done, q + 1, total=NQ)
                        ac.activation(xT[:, :], fa_ps[:, :], ACT.Copy).then_inc(xT_ready, 1)
                    if u == 2 and exists(q - 2, NQ):
                        need(ac, x2T_done, q - 2, total=NQ)
                        need(ac, x2T_kept[par], j - 2, per=16, total=NQ // 2)
                        ac.activation(x2T[:, par, :], fa_ps[:, :], ACT.Copy).then_inc(x2T_ready, 1)
                    if exists(n - 2, NT):
                        for h in range(2):
                            need(ac, turned, n - 2, per=2, k=h + 1)
                            ac.activation(PT[:, u % 2, h * 512:(h + 1) * 512], pt_ps[h][:, :], ACT.Copy)\
                                .then_inc(PT_ready, 1)
                    if exists(n - 1, NT):
                        need(ac, subbed, n - 1)
                        ps = prob[:, (u - 1) % QT, :]
                        ac.activation(ps, ps, ACT.Exp).then_inc(exped, 1)
                    if u == 0 and exists(q + 1, NQ):
                        need(ac, cT_done, q + 1, total=NQ)
                        ac.activation(cT[:, :], fb_ps[:, :], ACT.Copy).then_inc(cT_ready, 1)
                    if u == 1 and exists(q - 2, NQ):
                        need(ac, ln_step, q + 2, per=LN_STEPS, total=NQ + 4)
                        need(ac, scattered[par], j - 2, per=16 * 2 * QT, total=NQ // 2)
                        for t in range(QT):
                            ac.activation(xn2[:, par, t, 0:D], x_all[:, cols_of((q - 2) * QT + t)], ACT.Identity,
                                          bias=ln_s[:, QT + t:QT + t + 1], scale=ln_r[:, QT + t:QT + t + 1])\
                              .then_inc(xn2_ready, 1)
                    if u == 1 and exists(q + 1, NQ):
                        need(ac, q_done, q + 1, total=NQ)
                        for g in range(NG):
                            r = slice(32 * g, 32 * g + 32)
                            ac.activation(qg[r, 1 - par, g, :], fa_ps[r, :], ACT.Identity, bias=cols[r, 3:4],
                                          scale=float(DK) ** -0.5).then_inc(q_ready, 1)
                    if u == 2 and exists(q - 2, NQ):
                        need(ac, lg_done, q - 2, total=NQ)
                        ac.activation(LT[:, :], fb_ps[:, 0:P], ACT.Identity, bias=rb).then_inc(LT_ready, 1)
                        ac.dma_start(xn2T[:, cols_of((q - 2) * QT, QT)], x2T[:, par, :]).then_inc(x2T_kept[par], 16)
                    if u == 2 and exists(q + 1, NQ):
                        need(ac, kT_ready, q + 1, total=NQ)
                        for i in range(HG):
                            dst = kbd[:, 1 - par, :, i, :]
                            ac.activation(dst, kT[:, :].rearrange("p (b k) -> p b k", k=S), ACT.Copy,
                                          scale=cst[:, C_JM + i:C_JM + i + 1]).then_inc(k_ready, 1)
                    if u == 3 and exists(q + 1, NQ):
                        need(ac, v_done, q + 1, total=NQ)
                        for b in range(2):
                            for c in range(2):
                                src = fa_ps[b * S:(b + 1) * S, :].rearrange("k (t p c d) -> k t p c d", t=QT, c=2, d=DK)
                                dst = vb[c * S:(c + 1) * S, 1 - par, :, b, :].rearrange("k t (p m) -> k t p m", m=VS)
                                src, dst = src[:, :, :, c, :], dst[:, :, :, 16 + DK * c:16 + DK * c + DK]
                                ac.activation(dst, src, ACT.Copy).then_inc(v_ready, 1)

            loop(ac, step, J0, J1)
            for i in range(2):
                ac.wait_ge(x2T_kept[i], 16 * (NQ // 2))

        @block.gpsimd
        def _(po):
            po.memset(qg[:, :, :, :], 0.0).then_inc(setup_pool, 1)
            po.memset(vb[:, :, :, :, :], 0.0).then_inc(setup_pool, 1)
            po.memset(ones_bf[:, :], 1.0).then_inc(setup_pool, 1)
            po.wait_ge(const_in, CONSTS)
            po.wait_ge(setup_dve, 9)

            def scatter(q, par, which):
                need(po, rb_step, q, per=RB_STEPS, total=NQ, apart=True)
                scatter_rows(po, lists, m, par, which)

            def step(j):
                for v in range(2 * QT):
                    par, u = v // QT, v % QT
                    q = j * 2 + par
                    n = j * 2 * QT + v
                    if exists(n, NT):
                        need(po, maxed, n)
                        ps = prob[:, u, :].rearrange("p (h k) -> p h k", k=S)
                        po.tensor_tensor(ps, ps, mx[:, u, :].unsqueeze(2).broadcast_to([P, H, S]),
                                         ALU.subtract).then_inc(subbed, 1)
                    if u == 0 and exists(q + 1, NQ):
                        p2 = quad_loaded(po, j, par, 1)
                        need(po, kT_ready, q, total=NQ, apart=True)
                        po.tensor_scalar(keep[:, :], pad_k[:, p2, :], 0, 0.0, ALU.is_equal, ALU.is_equal).then_inc(keep_ready, 1)
                        po.tensor_scalar(mask[:, p2], pad_q[:, p2], 0, NEG, ALU.is_equal, ALU.mult).then_inc(mask_tmp, 1)
                        need(po, mask_tmp, q + 1, total=NQ)
                        po.tensor_tensor(mask[:, p2], mask[:, p2], srcm[:, :].unsqueeze(1).broadcast_to([P, QT, S]),
                                         ALU.add).then_inc(mask_ready, 1)
                        need(po, xn_ready, q + 1, per=QT, total=NQ, apart=True)
                        xs = x_all[:, cols_of((q + 1) * QT, QT)].rearrange("p (t d) -> p t d", t=QT)
                        po.tensor_tensor(xs, xs, bo_row[:, :].unsqueeze(1).broadcast_to([P, QT, D]),
                                         ALU.add).then_inc(xb_ready, 1)
                    if u == 1 and exists(q - 3, NQ - 2):
                        scatter(q - 3, 1 - par, range(0, 2))
                    if u == 2 and exists(q - 3, NQ - 2):
                        scatter(q - 3, 1 - par, range(2, 5))
                    if u == 3 and exists(q - 3, NQ - 2):
                        scatter(q - 3, 1 - par, range(5, 8))

            loop(po, step, J0, J1)


def experts(nc, a, NT, REGION, lists, results, m):
    TOK = NT * P
    NQ = NT // QT
    FC = F // P
    SC = FS // P
    HB = FC * SL // 512
    T = steps_listed(NT)
    xn2T, cst, gates, count, banks = m.xn2T, m.cst, m.gates, m.count, m.banks
    sw1, sw2, scols, sb2_row, shared_in = m.sw1, m.sw2, m.scols, m.sb2_row, m.shared_in
    with ExitStack() as ctx:
        sb, sem = tools(nc, ctx)
        hs = sb("hs", [P, 2, SC, QW])
        sw1_hl = sb("sw1_hl", [P, 2, FS])
        xs_hl = sb("xs_hl", [P, 2, 2, QW])
        w1 = sb("w1", [P, E, 2, F])
        w2 = sb("w2", [P, E, FC, D])
        gate_c = sb("gate_c", [P, FC, E])
        b1g_c = sb("b1g_c", [P, FC, E])
        b2_row = sb("b2_row", [P, E, D + 1])
        pad_rows = sb("pad_rows", [P, E + 1, 2, ROW])
        tf = sb("tf", [P, 4, E])
        trips = sb("trips", [P, E], I32)
        ends = sb("ends", [P, E], I32)
        begun = sb("begun", [P, T, E])
        step_f = sb("step_f", [P, 2, T])
        expert_of = sb("expert_of", [P, T], I32)
        row_of = sb("row_of", [P, T], I32)
        pairs = sb("pairs", [P, 1], I32)
        rows = sb("rows", [P, 2, 2, ROW])
        meta = sb("meta", [P, 2, 2, 2])
        b2_now = sb("b2_now", [P, 2, D + 1])
        destf = sb("destf", [P, 2, 2])
        dest = sb("dest", [P, 2, 2, 1], I32)
        rT = sb("rT", [P, 2, 2, SL])
        w1_now = sb("w1_now", [P, 2, 2, F])
        hT = sb("hT", [P, 2, FC, SL])
        y = sb("y", [P, 2, 2, D])

        sh_ps, sy_ps = [banks[0:2], banks[2:4]], banks[4:6]
        h_ps, y_ps, t_ps = [banks[0:2], banks[2:4]], banks[4:6], banks[6:8]

        biases_in, w1_in, w2_in = sem("biases_in"), sem("w1_in"), sem("w2_in")
        shared_scaled, biases_ready = sem("shared_scaled"), sem("biases_ready")
        sh_done, sh_gelued, sy_done, kept = (sem(n) for n in ("sh_done", "sh_gelued", "sy_done", "kept"))
        plan_step, pads_ready, pads_in, table_ready = (sem(n) for n in ("plan_step", "pads_ready", "pads_in", "table_ready"))
        rows_in = [sem(f"rows_in{i}") for i in range(2)]
        meta_read, turned, rT_ready = (sem(n) for n in ("meta_read", "rows_turned", "rT_ready"))
        h_done, gelued, y_done, y_ready = (sem(n) for n in ("h_done", "gelued", "y_done", "y_ready"))
        destf_step, dest_ready, w1_ready, b2_ready = (sem(n) for n in ("destf_step", "dest_ready", "w1_ready", "b2_ready"))
        w_split, sw1_split, xs_split = sem("w_split"), sem("sw1_split"), sem("xs_split")
        sent = [sem(f"sent{i}") for i in range(2)]
        biased = sem("biased")
        passed = sem("e_passed")

        SHARED_IN = 16 * 7

        def wait_apart(eng, s, value):
            wait_alone(eng, s, value, passed)

        def iterations(eng, body):
            n = eng.value_load(pairs[0:1, 0:1], min_val=TOK // SL, max_val=(T - 3) // 2)
            body(0, 0, 0)
            body(1, 1, 0)
            with eng.Fori(1, n) as i:
                body(i * 2, 0, i)
                body(i * 2 + 1, 1, i)

        def expert(eng, t):
            return eng.value_load(expert_of[0:1, bass.ds(t, 1)], min_val=0, max_val=E - 1)

        block = ctx.enter_context(nc.Block())

        @block.sync
        def _(sp):
            sp.dma_start(gate_c[:, :, :], a["gate"]).then_inc(biases_in, 16)
            sp.dma_start(b1g_c[:, :, :], a["b1"]).then_inc(biases_in, 16)
            sp.dma_start(b2_row[:, :, 0:D], a["b2"].unsqueeze(0).broadcast_to([P, E, D])).then_inc(biases_in, 16)
            sp.wait_ge(table_ready, 1)
            sp.wait_ge(pads_ready, 2)
            for e in range(E):
                at = sp.value_load(ends[0:1, e:e + 1], min_val=e * REGION, max_val=e * REGION + TOK)
                sp.dma_start(lists[bass.ds(at, SL), :].rearrange("(t p) d -> p t d", p=P), pad_rows[:, e])\
                  .then_inc(pads_in, 16)
            for i in range(3):
                sp.dma_start(lists[E * REGION + i * SL:E * REGION + (i + 1) * SL, :]
                             .rearrange("(t p) d -> p t d", p=P), pad_rows[:, E]).then_inc(pads_in, 16)
            sp.wait_ge(pads_in, 16 * (E + 3))
            for i in range(2):
                sp.wait_ge(m.scattered[i], 16 * 2 * QT * (NQ // 2))

            def load(t, par, wait=True):
                at = sp.value_load(row_of[0:1, bass.ds(t, 1)], min_val=0, max_val=E * REGION + 2 * SL)
                if wait:
                    sp.wait_ge(turned, t - 1)
                    sp.wait_ge(meta_read, t - 1)
                sp.dma_start(rows[:, par], lists[bass.ds(at, SL), :].rearrange("(t p) d -> p t d", p=P))\
                  .then_inc(rows_in[par], 16)
            load(0, 0, False)
            load(1, 1, False)
            iterations(sp, lambda t, par, i: load(t + 2, par))
            n = sp.value_load(pairs[0:1, 0:1], min_val=TOK // SL, max_val=(T - 3) // 2)
            for i in range(2):
                wait_apart(sp, rows_in[i], n * 16 + 16)
                wait_apart(sp, sent[i], n * 32)

        @block.tensor
        def _(pe):
            ident = cst[:, C_ID:C_ID + P]

            def hidden(q, par):
                for c in range(SC):
                    if not isinstance(q, int) or q >= 2:
                        pe.wait_ge(sh_gelued, (q - 2) * SC + c + 1)
                    if c == 0:
                        pe.wait_ge(xs_split, q * 2 + 2)
                    product(pe, sh_ps[par][c][:, :],
                            [sw1_hl[:, i, c * P:(c + 1) * P].bitcast(F32R) for i in range(2)],
                            [xs_hl[:, par, i, :].bitcast(F32R) for i in range(2)]).then_inc(sh_done, 1)

            def second(q, par):
                pe.wait_ge(sh_gelued, q * SC + SC)
                if not isinstance(q, int) or q >= 2:
                    pe.wait_ge(kept, q - 1)
                for t in range(QT):
                    for c in range(SC):
                        last = pe.matmul(sy_ps[par][:, t * D:(t + 1) * D], hs[:, par, c, t * P:(t + 1) * P],
                                      sw2[:, c, :], start=(c == 0), stop=(c == SC - 1))
                last.then_inc(sy_done, 1)

            pe.wait_ge(shared_in, SHARED_IN)
            pe.wait_ge(sw1_split, 2)
            hidden(0, 0)
            hidden(1, 1)
            pe.wait_ge(shared_scaled, 3)
            second(0, 0)
            with pe.Fori(1, NQ // 2) as j:
                hidden(j * 2, 0)
                second(j * 2 - 1, 1)
                hidden(j * 2 + 1, 1)
                second(j * 2, 0)

            def turn(t, par, i):
                pe.wait_ge(rows_in[par], i * 16 + 16)
                if not isinstance(t, int) or t >= 2:
                    pe.wait_ge(rT_ready, t * 2 - 2)
                for h in range(2):
                    last = pe.transpose(t_ps[par][:, h * P:(h + 1) * P], rows[:, par, h, 0:D], ident)
                last.then_inc(turned, 1)

            def first_layer(t, par):
                pe.wait_ge(rT_ready, t * 2 + 2)
                pe.wait_ge(w1_ready, t + 1)
                if not isinstance(t, int) or t >= 2:
                    pe.wait_ge(gelued, (t - 1) * FC)
                for c in range(FC):
                    last = product(pe, h_ps[par][c // 2][:, (c % 2) * SL:(c % 2 + 1) * SL],
                                   [w1_now[:, par, i, c * P:(c + 1) * P].bitcast(F32R) for i in range(2)],
                                   [rT[:, par, i, :].bitcast(F32R) for i in range(2)])
                    if c % 2:
                        last.then_inc(h_done, 1)

            def second_layer(t, par, e):
                if not isinstance(t, int) or t >= 2:
                    pe.wait_ge(y_ready, t - 1)
                for h in range(2):
                    for c in range(FC):
                        if h == 0:
                            pe.wait_ge(gelued, t * FC + c + 1)
                        last = pe.matmul(y_ps[par][:, h * D:(h + 1) * D], hT[:, par, c, h * P:(h + 1) * P],
                                      w2[:, bass.ds(e, 1), c, :].rearrange("p a d -> p (a d)"),
                                      start=(c == 0), stop=(c == FC - 1))
                last.then_inc(y_done, 1)

            for t in range(2):
                turn(t, t, 0)
            second(NQ - 1, 1)
            pe.wait_ge(sh_gelued, NQ * SC)
            first_layer(0, 0)
            pe.wait_ge(w2_in, 32)
            pe.wait_ge(kept, NQ)

            def body(t, par, i):
                first_layer(t + 1, 1 - par)
                turn(t + 2, par, i + 1)
                second_layer(t, par, expert(pe, t))
            iterations(pe, body)

        @block.scalar
        def _(ac):
            halves = [slice(k * E // 2, (k + 1) * E // 2) for k in range(2)]
            for es in halves:
                ac.dma_start(w1[:, es, 1, :], a["w1"][es].rearrange("e d f -> d e f")).then_inc(w1_in, 16)
            for es in halves:
                ac.dma_start(w2[:, es], a["w2"][es].rearrange("e (c f) d -> f e c d", f=P)).then_inc(w2_in, 16)
            ac.wait_ge(shared_scaled, 1)

            def shared_gelu(q, par):
                for c in range(SC):
                    if c == 0 and (not isinstance(q, int) or q >= 2):
                        ac.wait_ge(sy_done, q - 1)
                    ac.wait_ge(sh_done, q * SC + c + 1)
                    ac.activation(hs[:, par, c, :], sh_ps[par][c][:, :], ACT.Gelu, bias=scols[:, 2, c:c + 1],
                                  scale=scols[:, 0, c:c + 1]).then_inc(sh_gelued, 1)
            shared_gelu(0, 0)
            shared_gelu(1, 1)
            with ac.Fori(1, NQ // 2) as j:
                shared_gelu(j * 2, 0)
                shared_gelu(j * 2 + 1, 1)

            ac.wait_ge(biases_ready, 1)
            ac.wait_ge(table_ready, 1)

            def body(t, par, i):
                e = expert(ac, t)
                if not isinstance(t, int) or t >= 2:
                    ac.wait_ge(y_done, t - 1)
                for c in range(FC):
                    if c == 2:
                        if not isinstance(t, int) or t >= 2:
                            ac.wait_ge(y_ready, t - 1)
                            wait_apart(ac, destf_step, t * 2 - 2)
                        ac.activation(b2_now[:, par, :], b2_row[:, bass.ds(e, 1), :].rearrange("p a d -> p (a d)"),
                                      ACT.Copy).then_inc(b2_ready, 1)
                    if c % 2 == 0:
                        ac.wait_ge(h_done, t * HB + c // 2 + 1)
                    ac.activation(hT[:, par, c, :], h_ps[par][c // 2][:, (c % 2) * SL:(c % 2 + 1) * SL], ACT.Gelu,
                                  bias=b1g_c[:, c, bass.ds(e, 1)], scale=gate_c[:, c, bass.ds(e, 1)])\
                      .then_inc(gelued, 1)
            iterations(ac, body)

        @block.vector
        def _(ve):
            ve.wait_ge(shared_in, SHARED_IN)

            def split_tokens(q, par):
                if not isinstance(q, int) or q >= 2:
                    wait_apart(ve, sh_done, (q - 1) * SC)
                split(ve, (xs_split, lambda: wait_apart(ve, xs_split, q * 2 + 1)), xs_hl[:, par, 0, :].bitcast(F32R),
                      xs_hl[:, par, 1, :].bitcast(F32R), xn2T[:, bass.ds(q * QW, QW)])

            def keep(q, par):
                ve.wait_ge(sy_done, q + 1)
                out = xn2T[:, bass.ds(q * QW, QW)].rearrange("p (t d) -> p t d", d=D)
                ve.tensor_tensor(out, sy_ps[par][:, :].rearrange("p (t d) -> p t d", d=D),
                                 sb2_row[:, :].unsqueeze(1).broadcast_to([P, QT, D]), ALU.add).then_inc(kept, 1)

            split(ve, (sw1_split, lambda: ve.wait_ge(sw1_split, 1)), sw1_hl[:, 0, :].bitcast(F32R),
                  sw1_hl[:, 1, :].bitcast(F32R), sw1[:, :])
            split_tokens(0, 0)
            ve.tensor_tensor(scols[:, 2, :], scols[:, 0, :], scols[:, 1, :], ALU.mult).then_inc(shared_scaled, 1)
            split_tokens(1, 1)
            ve.tensor_scalar(sw2[:, :, :], sw2[:, :, :], gates[:, 2:3], None, ALU.mult).then_inc(shared_scaled, 1)
            ve.tensor_scalar(sb2_row[:, :], sb2_row[:, :], gates[:, 2:3], None, ALU.mult).then_inc(shared_scaled, 1)
            ve.tensor_scalar(m.ln_row[:, :, :], m.ln_row[:, :, :], gates[:, 1:2], None, ALU.mult)\
              .then_inc(shared_scaled, 1)

            steps = [0]

            def then(ins):
                steps[0] += 1
                ins.then_inc(plan_step, 1)
                ve.wait_ge(plan_step, steps[0])
            n, cum, gap = tf[:, 0], tf[:, 1], tf[:, 2]

            def table(part):
                if part == 0:
                    then(ve.tensor_tensor(n, count[:, :], cst[:, C_BASE:C_BASE + E], ALU.subtract))
                    then(ve.tensor_scalar(n, n, float(SL - 1), None, ALU.add))
                    then(ve.tensor_copy(trips[:, :], n))
                    then(ve.tensor_scalar(trips[:, :], trips[:, :], SL.bit_length() - 1, None,
                                          ALU.logical_shift_right))
                    then(ve.tensor_copy(cum, trips[:, :]))
                    then(ve.tensor_scalar(gap, cum, -float(SL), float(REGION), ALU.mult, ALU.add))
                elif part == 1:
                    for e in range(1, E):
                        then(ve.tensor_tensor(cum[:, e:e + 1], cum[:, e - 1:e], cum[:, e:e + 1], ALU.add))
                elif part == 2:
                    then(ve.tensor_tensor(begun[:, :, :],
                                          cst[:, C_TOKEN + NT:C_TOKEN + NT + T].unsqueeze(2).broadcast_to([P, T, E]),
                                          cum.unsqueeze(1).broadcast_to([P, T, E]), ALU.is_ge))
                    then(ve.tensor_reduce(step_f[:, 0], begun[:, :, :], X, ALU.add))
                    then(ve.tensor_scalar(expert_of[:, :], step_f[:, 0], float(E - 1), None, ALU.min))
                else:
                    then(ve.tensor_tensor(begun[:, :, :], begun[:, :, :], gap.unsqueeze(1).broadcast_to([P, T, E]),
                                          ALU.mult))
                    then(ve.tensor_reduce(step_f[:, 1], begun[:, :, :], X, ALU.add))
                    then(ve.scalar_tensor_tensor(out=row_of[:, :], in0=cst[:, C_TOKEN + NT:C_TOKEN + NT + T],
                                                 scalar=float(SL), in1=step_f[:, 1], op0=ALU.mult, op1=ALU.add))
                    then(ve.tensor_scalar(tf[:, 3, 0:1], cum[:, E - 1:E], 1.0, None, ALU.add))
                    then(ve.tensor_copy(pairs[:, :], tf[:, 3, 0:1]))
                    then(ve.tensor_scalar(pairs[:, :], pairs[:, :], 1, None, ALU.logical_shift_right))
                    ve.tensor_copy(ends[:, :], count[:, :]).then_inc(table_ready, 1)

            for q in range(4):
                table(q)
                split_tokens(q + 2, q % 2)
                keep(q, q % 2)
            ve.wait_ge(biases_in, 48)
            ve.tensor_copy(b2_row[:, :, D], cst[:, C_EXP:C_EXP + E])
            ve.tensor_tensor(b1g_c[:, :, :], b1g_c[:, :, :], gate_c[:, :, :], ALU.mult).then_inc(biases_ready, 1)
            first = max(4, NQ - 2 - E)
            for q in range(4, first):
                split_tokens(q + 2, q % 2)
                keep(q, q % 2)
            ve.wait_ge(w1_in, 32)
            es = 0
            for q in range(first, NQ - 1):
                if q + 2 < NQ:
                    split_tokens(q + 2, q % 2)
                keep(q, q % 2)
                while es < E and (q == NQ - 2 or es * (NQ - 2 - first) < E * (q + 1 - first)):
                    split(ve, (w_split, lambda: ve.wait_ge(w_split, es * 2 + 1)), w1[:, es, 0, :].bitcast(F32R),
                          w1[:, es, 1, :].bitcast(F32R), w1[:, es, 1, :])
                    es += 1
            ve.wait_ge(w_split, 2 * E)

            def take_meta(t, par, i):
                ve.wait_ge(rows_in[par], i * 16 + 16)
                if not isinstance(t, int) or t >= 2:
                    ve.wait_ge(destf_step, (t - 1) * 2)
                ve.tensor_copy(meta[:, par], rows[:, par, :, D:ROW]).then_inc(meta_read, 1)

            def take_rows(t, par):
                ve.wait_ge(turned, t + 1)
                if not isinstance(t, int) or t >= 2:
                    ve.wait_ge(h_done, (t - 1) * HB)
                split(ve, (rT_ready, lambda: ve.wait_ge(rT_ready, t * 2 + 1)), rT[:, par, 0, :].bitcast(F32R),
                      rT[:, par, 1, :].bitcast(F32R), t_ps[par][:, 0:SL])

            def take_weights(t, par):
                e = expert(ve, t)
                if not isinstance(t, int) or t >= 2:
                    wait_apart(ve, h_done, (t - 1) * HB)
                ve.tensor_copy(w1_now[:, par, :, :].rearrange("p i f -> p (i f)").bitcast(F32R),
                               w1[:, bass.ds(e, 1), :, :].rearrange("p a i f -> p (a i f)").bitcast(F32R))\
                  .then_inc(w1_ready, 1)

            ve.wait_ge(table_ready, 1)
            take_weights(0, 0)
            take_rows(0, 0)
            take_weights(1, 1)
            keep(NQ - 1, 1)
            for t in range(2):
                take_meta(t, t, 0)
            take_rows(1, 1)
            take_weights(2, 0)

            def body(t, par, i):
                take_rows(t + 2, par)
                take_weights(t + 3, 1 - par)
                ve.wait_ge(b2_ready, t + 1)
                if not isinstance(i, int) or i >= 1:
                    ve.wait_ge(sent[par], i * 32)
                ve.wait_ge(y_done, t + 1)
                ve.tensor_tensor(y[:, par], y_ps[par][:, 0:2 * D].rearrange("p (h d) -> p h d", d=D),
                                 b2_now[:, par, 0:D].unsqueeze(1).broadcast_to([P, 2, D]), ALU.add).then_inc(y_ready, 1)
                take_meta(t + 2, par, i + 1)
            iterations(ve, body)

        @block.gpsimd
        def _(po):
            for par in range(2):
                scatter_rows(po, lists, m, par, range(2 * QT))
            po.memset(pad_rows[:, :, :, :], 0.0).then_inc(pads_ready, 1)
            po.wait_ge(pads_ready, 1)
            po.memset(pad_rows[:, :, :, D:D + 1], -1.0)
            for e in range(E + 1):
                for h in range(2):
                    last = po.tensor_scalar(pad_rows[:, e, h, D + 1:ROW], cst[:, C_PART:C_PART + 1],
                                            float(2 * TOK + e * SL + h * P), None, ALU.add)
            last.then_inc(pads_ready, 1)
            po.wait_ge(shared_scaled, 4)

            def add_bias(q):
                xs = m.x_all[:, bass.ds(q * QW, QW)].rearrange("p (t d) -> p t d", t=QT)
                po.tensor_tensor(xs, xs, m.ln_row[:, 1, :].unsqueeze(1).broadcast_to([P, QT, D]), ALU.add)\
                  .then_inc(biased, 1)
            with po.Fori(0, NQ) as q:
                add_bias(q)
            po.wait_ge(table_ready, 1)

            def place(t, par):
                po.wait_ge(meta_read, t + 1)
                if not isinstance(t, int) or t >= 2:
                    po.wait_ge(dest_ready, t - 1)
                wait_apart(po, b2_ready, t + 1)
                po.tensor_scalar(destf[:, par], meta[:, par, :, 0], b2_now[:, par, D:D + 1], -float(TOK),
                                 ALU.is_equal, ALU.mult).then_inc(destf_step, 1)
                po.wait_ge(destf_step, t * 2 + 1)
                po.tensor_tensor(destf[:, par], destf[:, par], meta[:, par, :, 1], ALU.add).then_inc(destf_step, 1)

            def body(t, par, i):
                place(t, par)
                if not isinstance(i, int) or i >= 1:
                    po.wait_ge(sent[par], i * 32)
                wait_apart(po, destf_step, t * 2 + 2)
                po.tensor_copy(dest[:, par, :, 0], destf[:, par]).then_inc(dest_ready, 1)
                po.wait_ge(dest_ready, t + 1)
                wait_apart(po, y_ready, t + 1)
                for h in range(2):
                    po.indirect_dma_start(results[:, :], bass.IndirectOffsetOnAxis(ap=dest[:, par, h, :], axis=0),
                                          y[:, par, h, :], None).then_inc(sent[par], 16)
            iterations(po, body)


def combine(nc, a, NT, results, out, m):
    GT = 2 * QT
    GW = GT * D
    H = GT // 2
    NGR = NT // GT
    TOK = NT * P
    x_all, shared, weight, ln_row = m.x_all, m.xn2T, m.weight, m.ln_row
    out_rows = out.rearrange("b s d -> (b s) d")
    with ExitStack() as ctx:
        sb, sem = tools(nc, ctx)
        yin = sb("yin", [P, 2, 2, GT, D])
        acc = sb("acc", [P, 2, GT, D])
        first = sb("first", [P, 2, GT, D])
        second = sb("second", [P, 2, GT, D])
        normed = sb("normed", [P, 2, GT, D])
        st = sb("st", [P, 2, GT, 6])
        mv = sb("mv3", [P, GT, 2])
        tmp = sb("tmp", [P, 3, GT])
        tmi = sb("tmi", [P, GT], I32)
        rr = sb("rr", [P, 2, 2, GT])
        res = sb("res", [P, 2, GT, D])

        y_in = [sem(f"y_in{i}") for i in range(2)]
        acc_step, stat_step, n_step, scaled, res_step = (
            sem("c_" + n) for n in ("acc_step", "stat_step", "n_step", "scaled", "res_step"))
        weighed = sem("c_weighed")
        half_step = sem("c_half_step")
        stored = [sem(f"stored{i}") for i in range(2)]
        passed = sem("c_passed")
        N_STEPS = 14
        A_STEPS = 3
        W_STEPS = GT + H

        def wait_apart(eng, s, value):
            wait_alone(eng, s, value, passed)

        def groups(eng, body, pairs=1, end=NGR // 2):
            for i in range(pairs):
                body(2 * i, 0, i)
                body(2 * i + 1, 1, i)
            with eng.Fori(pairs, end) as i:
                body(i * 2, 0, i)
                body(i * 2 + 1, 1, i)

        def later(g):
            return not isinstance(g, int) or g >= 2

        block = ctx.enter_context(nc.Block())

        @block.sync
        def _(sp):
            def load(g, par, i):
                if later(g):
                    sp.wait_ge(acc_step, (g - 1) * A_STEPS)
                for k in range(2):
                    sp.dma_start(yin[:, par, k], results[bass.ds(g * GW + k * TOK, GW), :]
                                 .rearrange("(t p) d -> p t d", p=P)).then_inc(y_in[par], 16)
            groups(sp, load)

        @block.vector
        def _(ve):
            def add(g, par, i):
                if i == 0:
                    ve.tensor_tensor(first[:, par, 0:H], yin[:, par, 0, 0:H],
                                     weight[:, bass.ds(g * GT, H), 0:1].broadcast_to([P, H, D]),
                                     ALU.mult).then_inc(acc_step, 1)
                elif i == 1:
                    ve.wait_ge(acc_step, g * A_STEPS + 1)
                    ve.wait_ge(weighed, g * W_STEPS + W_STEPS)
                    ve.tensor_tensor(first[:, par], first[:, par],
                                     shared[:, bass.ds(g * GW, GW)].rearrange("p (t d) -> p t d", d=D),
                                     ALU.add).then_inc(acc_step, 1)
                else:
                    ve.wait_ge(acc_step, g * A_STEPS + 2)
                    if later(g):
                        ve.wait_ge(scaled, (g - 1) * GT)
                    ve.tensor_tensor(acc[:, par], first[:, par], second[:, par], ALU.add).then_inc(acc_step, 1)

            def stats(g, par, t):
                if t == 0:
                    wait_apart(ve, acc_step, g * A_STEPS + A_STEPS)
                ve.bn_stats(st[:, par, t, :], acc[:, par, t, :]).then_inc(stat_step, 1)

            def norm(i, g, par):
                v, aa, bb = tmp[:, 0], tmp[:, 1], tmp[:, 2]
                rs, sh = rr[:, par, 0], rr[:, par, 1]
                if i == 0:
                    if later(g):
                        ve.wait_ge(scaled, (g - 1) * GT)
                    wait_apart(ve, stat_step, g * GT + GT)
                    for t in range(GT):
                        ins = ve.bn_aggr(mv[:, t, :], st[:, par, t, :])
                    ins.then_inc(n_step, 1)
                    return
                ve.wait_ge(n_step, g * N_STEPS + i)
                if i == 1:
                    ins = ve.tensor_scalar(v, mv[:, :, 1], EPS, None, ALU.add)
                elif i == 2:
                    ins = ve.tensor_scalar(tmi[:, :], v.bitcast(I32), 1, None, ALU.logical_shift_right)
                elif i == 3:
                    ins = ve.tensor_scalar(rs.bitcast(I32), tmi[:, :], -1.0, RSQRT_MAGIC, ALU.mult, ALU.add)
                elif i in (4, 7, 10):
                    ins = ve.tensor_tensor(aa, rs, rs, ALU.mult)
                elif i in (5, 8, 11):
                    ins = ve.scalar_tensor_tensor(out=bb, in0=aa, scalar=-0.5, in1=v, op0=ALU.mult, op1=ALU.mult)
                elif i in (6, 9, 12):
                    ins = ve.scalar_tensor_tensor(out=rs, in0=bb, scalar=1.5, in1=rs, op0=ALU.add, op1=ALU.mult)
                else:
                    ins = ve.scalar_tensor_tensor(out=sh, in0=mv[:, :, 0], scalar=-1.0, in1=rs, op0=ALU.mult,
                                                  op1=ALU.mult)
                ins.then_inc(n_step, 1)

            BEHIND_ADD = ((0, 1), (2, 3), (4,))
            BEHIND_STATS = ((5,), (6, 7), (8,), (9, 10), (11,), (12, 13), (), ())

            def body(g, par, i):
                ve.wait_ge(y_in[par], i * 32 + 32)
                chained = later(g) or g == 1
                for k in range(A_STEPS):
                    add(g, par, k)
                    if chained:
                        for step in BEHIND_ADD[k]:
                            norm(step, g - 1, 1 - par)
                for t in range(GT):
                    stats(g, par, t)
                    if chained:
                        for step in BEHIND_STATS[t]:
                            norm(step, g - 1, 1 - par)
            groups(ve, body)
            for i in range(N_STEPS):
                norm(i, NGR - 1, 1)

            rest = res[:, 1, H:GT]
            ve.wait_ge(scaled, NGR * GT)
            ve.wait_ge(stored[1], (NGR // 2 - 1) * 16)
            ve.tensor_tensor(rest, normed[:, 1, H:GT], ln_row[:, 0, :].unsqueeze(1).broadcast_to([P, H, D]),
                             ALU.mult).then_inc(half_step, 1)
            ve.wait_ge(half_step, 1)
            ve.tensor_tensor(rest, rest, x_all[:, (NT - H) * D:NT * D].rearrange("p (t d) -> p t d", t=H),
                             ALU.add).then_inc(half_step, 1)

        @block.scalar
        def _(ac):
            def store(g, par):
                ac.wait_ge(res_step, g * 2 + 2)
                ac.dma_start(out_rows[bass.ds(g * GW, GW), :].rearrange("(t p) d -> p t d", p=P), res[:, par])\
                  .then_inc(stored[par], 16)

            def weigh(g, par, i):
                wait_apart(ac, y_in[par], i * 32 + 32)
                if later(g):
                    wait_apart(ac, acc_step, (g - 1) * A_STEPS)
                for k, t in [(0, t) for t in range(H, GT)] + [(1, t) for t in range(GT)]:
                    w = weight[:, bass.ds(g * GT + t, 1), :].rearrange("p a k -> p (a k)")
                    ac.activation((first, second)[k][:, par, t, :], yin[:, par, k, t, :], ACT.Copy, scale=w[:, k:k + 1])\
                      .then_inc(weighed, 1)

            def scale(g, par):
                ac.wait_ge(n_step, g * N_STEPS + N_STEPS)
                if later(g):
                    ac.wait_ge(res_step, (g - 1) * 2)
                for t in range(GT):
                    ac.activation(normed[:, par, t, :], acc[:, par, t, :], ACT.Identity, bias=rr[:, par, 1, t:t + 1],
                                  scale=rr[:, par, 0, t:t + 1]).then_inc(scaled, 1)

            def body(g, par, i):
                weigh(g, par, i)
                if later(g):
                    scale(g - 2, par)
                if later(g) and not (isinstance(g, int) and g < 3):
                    store(g - 3, 1 - par)
            groups(ac, body, pairs=2)
            scale(NGR - 2, 0)
            store(NGR - 3, 1)
            scale(NGR - 1, 1)
            store(NGR - 2, 0)
            for half, (s, value) in enumerate(((half_step, 2), (res_step, NGR * 2))[::-1]):
                tiles = slice(half * H, half * H + H)
                ac.wait_ge(s, value)
                ac.dma_start(out_rows[((NGR - 1) * GT + half * H) * P:((NGR - 1) * GT + half * H + H) * P, :]
                             .rearrange("(t p) d -> p t d", p=P), res[:, 1, tiles]).then_inc(stored[1], 16)
            for i in range(2):
                ac.wait_ge(stored[i], 8 * NGR + 16 * i)

        @block.gpsimd
        def _(po):
            def body(g, par, i, n=GT):
                po.wait_ge(scaled, g * GT + n)
                if later(g):
                    po.wait_ge(stored[par], i * 16)
                po.tensor_tensor(res[:, par, 0:n], normed[:, par, 0:n],
                                 ln_row[:, 0, :].unsqueeze(1).broadcast_to([P, n, D]), ALU.mult).then_inc(res_step, 1)
                wait_apart(po, res_step, g * 2 + 1)
                po.tensor_tensor(res[:, par, 0:n], res[:, par, 0:n],
                                 x_all[:, bass.ds(g * GW, n * D)].rearrange("p (t d) -> p t d", t=n),
                                 ALU.add).then_inc(res_step, 1)
            groups(po, body, end=NGR // 2 - 1)
            body(NGR - 2, 0, NGR // 2 - 1)
            body(NGR - 1, 1, NGR // 2 - 1, H)


def build_inputs(inputs):
    g = {k: np.asarray(v) for k, v in inputs.items()}
    f32 = {}
    f32["x"], f32["ctx_1024"] = g["x"], g["ctx_1024"]
    f32["mask_BxS2_ik0"] = g["mask_BxS2_ik0"]
    f32["src_mask"] = np.concatenate([g["mask_1x1xSxS2_ff0"][0, 0]] * 2)
    f32["w_att"] = np.stack([g["L0_xattn_" + n].T for n in ("Wq", "Wk", "Wv", "Wo")], axis=1)
    f32["b_att"] = np.stack([g["L0_xattn_" + n] for n in ("bq", "bk", "bv")], axis=1)
    f32["bo"] = g["L0_xattn_bo"]
    f32["gates"] = np.concatenate([g["g_xattn"], g["g_ffn"], g["L0_ffn_shared_weight"].reshape(1)])
    router = np.zeros((P, 33), np.float32)
    router[:, 0:E] = g["L0_ffn_router_w"]
    for t in range(QT):
        router[32 * t:32 * t + E, 32] = g["L0_ffn_router_b"]
    f32["router"] = router
    for n in ("w1", "b1", "gate", "w2", "b2", "sw1", "sb1", "sgate", "sw2", "sb2", "ln_g", "ln_b"):
        f32[n] = g["L0_ffn_" + n]
    for n in ("b1", "gate"):
        f32[n] = f32[n].reshape(E, F // P, P).transpose(2, 1, 0)
    for n in ("sb1", "sgate"):
        f32[n] = f32[n].reshape(FS // P, P).T
    f32["consts"] = constants(g["x"].shape[0] // 2)
    return {k: np.ascontiguousarray(v) for k, v in f32.items()}


def kernel(**inputs):
    import concourse.bacc as bacc
    from concourse.bass_utils import run_bass_kernel_spmd

    arrays = build_inputs(inputs)
    nc = bacc.Bacc("TRN2", target_bir_lowering=False, num_devices=1)
    a = {n: nc.dram_tensor(f"in_{n}", v.shape, mybir.dt.from_np(v.dtype), kind="ExternalInput").ap()
         for n, v in arrays.items()}
    out = nc.dram_tensor("out", inputs["x"].shape, F32, kind="ExternalOutput").ap()
    bass_kernel(nc, a, out)
    r = run_bass_kernel_spmd(nc, [{f"in_{n}": v for n, v in arrays.items()}], core_ids=[0])
    return r.results[0]["out"]
```
